# Optimizing a Trainium2 kernel written in Bass

```python
import numpy as np
import jax
import jax.numpy as jnp

def _softmax(x, axis=-1):
    return jax.nn.softmax(x, axis=axis)

def _gelu(x):
    return jax.nn.gelu(x, approximate=True)

def _silu(x):
    return jax.nn.silu(x)

def _sigmoid(x):
    return jax.nn.sigmoid(x)

def _layernorm(x, axis=-1, eps=1e-05):
    m = jnp.mean(x, axis=axis, keepdims=True)
    v = jnp.var(x, axis=axis, keepdims=True)
    return (x - m) / jnp.sqrt(v + eps)

def _scatter_add(tgt, idx, src, axis=0):
    return tgt.at[idx].add(src)

def _segment_sum(src, seg, n):
    return jax.ops.segment_sum(src, seg, n)
kernel_name = 'mk_seq_postln_d1_jaxref_r8_716fc8'

def setup_inputs(seed: int=0):
    np.random.seed(seed)
    _w = jnp.asarray

    def _L0_attn_setup():
        import jax, jax.numpy as jnp
        import numpy as np
        from jax import lax

        def _phi(x):
            return jax.nn.elu(x) + 1.0
        key = jax.random.key(seed)
        ks = jax.random.split(key, 5)
        B, T, D, H = (8, 512, 128, 64)
        x = jax.random.normal(ks[0], (B, T, D), dtype=jnp.float32)
        W_q = jax.random.normal(ks[1], (D, H), dtype=jnp.float32) * (1.0 / np.sqrt(D))
        W_k = jax.random.normal(ks[2], (D, H), dtype=jnp.float32) * (1.0 / np.sqrt(D))
        W_v = jax.random.normal(ks[3], (D, H), dtype=jnp.float32) * (1.0 / np.sqrt(D))
        W_o = jax.random.normal(ks[4], (H, D), dtype=jnp.float32) * (1.0 / np.sqrt(H))
        return {'x': x, 'W_q': W_q, 'W_k': W_k, 'W_v': W_v, 'W_o': W_o}
    _L0_attn_in = _L0_attn_setup()

    def _L0_ffn_setup():
        import jax, jax.numpy as jnp
        import numpy as np
        NUM_HEADS = 16
        TOP_K = 2
        ROPE_BASE = 10000.0
        LN_EPS = 1e-05

        def _rope_sin_cos(S, D, dtype):
            inv_freq = 1.0 / ROPE_BASE ** (jnp.arange(0, D, 2, dtype=jnp.float32) / D)
            freqs = jnp.arange(S, dtype=jnp.float32)[:, None] * inv_freq[None, :]
            sin = jnp.sin(freqs).astype(dtype)[None, :, None, :]
            cos = jnp.cos(freqs).astype(dtype)[None, :, None, :]
            return (sin, cos)

        def _apply_rope(x, sin, cos):
            x1, x2 = (x[..., 0::2], x[..., 1::2])
            r1 = x1 * cos - x2 * sin
            r2 = x1 * sin + x2 * cos
            return jnp.stack([r1, r2], axis=-1).reshape(x.shape)

        def _layer_norm(x, w, b):
            mu = jnp.mean(x, axis=-1, keepdims=True)
            var = jnp.mean(jnp.square(x - mu), axis=-1, keepdims=True)
            return (x - mu) * jax.lax.rsqrt(var + LN_EPS) * w + b
        key = jax.random.key(seed)
        ks = jax.random.split(key, 8)
        B, S, E, NE = (2, 256, 128, 8)
        s = 0.02
        return {'x': jax.random.normal(ks[0], (B, S, E), dtype=jnp.float32), 'in_proj_w': jax.random.normal(ks[1], (3 * E, E), dtype=jnp.float32) * s, 'in_proj_b': jnp.zeros((3 * E,), dtype=jnp.float32), 'out_proj_w': jax.random.normal(ks[2], (E, E), dtype=jnp.float32) * s, 'out_proj_b': jnp.zeros((E,), dtype=jnp.float32), 'gate_w': jax.random.normal(ks[3], (NE, E), dtype=jnp.float32) * s, 'gate_b': jnp.zeros((NE,), dtype=jnp.float32), 'expert_w': jax.random.normal(ks[4], (NE, E, E), dtype=jnp.float32) * s, 'expert_b': jnp.zeros((NE, E), dtype=jnp.float32), 'ln1_w': jnp.ones((E,), dtype=jnp.float32), 'ln1_b': jnp.zeros((E,), dtype=jnp.float32), 'ln2_w': jnp.ones((E,), dtype=jnp.float32), 'ln2_b': jnp.zeros((E,), dtype=jnp.float32)}
    _L0_ffn_in = _L0_ffn_setup()
    _d = {'L0_attn_x': _L0_attn_in['x'], 'L0_attn_W_q': _L0_attn_in['W_q'], 'L0_attn_W_k': _L0_attn_in['W_k'], 'L0_attn_W_v': _L0_attn_in['W_v'], 'L0_attn_W_o': _L0_attn_in['W_o'], 'L0_ffn_in_proj_w': _L0_ffn_in['in_proj_w'], 'L0_ffn_in_proj_b': _L0_ffn_in['in_proj_b'], 'L0_ffn_out_proj_w': _L0_ffn_in['out_proj_w'], 'L0_ffn_out_proj_b': _L0_ffn_in['out_proj_b'], 'L0_ffn_gate_w': _L0_ffn_in['gate_w'], 'L0_ffn_gate_b': _L0_ffn_in['gate_b'], 'L0_ffn_expert_w': _L0_ffn_in['expert_w'], 'L0_ffn_expert_b': _L0_ffn_in['expert_b'], 'L0_ffn_ln1_w': _L0_ffn_in['ln1_w'], 'L0_ffn_ln1_b': _L0_ffn_in['ln1_b'], 'L0_ffn_ln2_w': _L0_ffn_in['ln2_w'], 'L0_ffn_ln2_b': _L0_ffn_in['ln2_b']}
    _x0 = _d['L0_attn_x']
    _d['L0_attn_x'] = jax.random.normal(jax.random.fold_in(jax.random.key(seed), 1), (32, 256, 128), dtype=_x0.dtype)
    del _x0
    return _d

def reference(L0_attn_x, L0_attn_W_q, L0_attn_W_k, L0_attn_W_v, L0_attn_W_o, L0_ffn_in_proj_w, L0_ffn_in_proj_b, L0_ffn_out_proj_w, L0_ffn_out_proj_b, L0_ffn_gate_w, L0_ffn_gate_b, L0_ffn_expert_w, L0_ffn_expert_b, L0_ffn_ln1_w, L0_ffn_ln1_b, L0_ffn_ln2_w, L0_ffn_ln2_b):

    def _L0_attn_ref(x, W_q, W_k, W_v, W_o):
        import jax, jax.numpy as jnp
        import numpy as np
        from jax import lax

        def _phi(x):
            return jax.nn.elu(x) + 1.0
        B, T, D = x.shape
        H = W_q.shape[1]
        q = _phi(jnp.einsum('btd,dh->bth', x, W_q))
        k = _phi(jnp.einsum('btd,dh->bth', x, W_k))
        v = jnp.einsum('btd,dh->bth', x, W_v)
        qT = jnp.swapaxes(q, 0, 1)
        kT = jnp.swapaxes(k, 0, 1)
        vT = jnp.swapaxes(v, 0, 1)
        S0 = jnp.zeros((B, H, H), dtype=x.dtype)
        z0 = jnp.zeros((B, H), dtype=x.dtype)

        def step(carry, inp):
            S, z = carry
            q_t, k_t, v_t = inp
            S = S + k_t[:, :, None] * v_t[:, None, :]
            z = z + k_t
            o_t = jnp.einsum('bij,bj->bi', S, q_t)
            denom = jnp.maximum(jnp.sum(z * q_t, axis=-1, keepdims=True), 1e-06)
            return ((S, z), o_t / denom)
        (_, _), oT = lax.scan(step, (S0, z0), (qT, kT, vT))
        o = jnp.swapaxes(oT, 0, 1)
        return jnp.einsum('bth,hd->btd', o, W_o)

    def _L0_ffn_ref(x, in_proj_w, in_proj_b, out_proj_w, out_proj_b, gate_w, gate_b, expert_w, expert_b, ln1_w, ln1_b, ln2_w, ln2_b):
        import jax, jax.numpy as jnp
        import numpy as np
        NUM_HEADS = 16
        TOP_K = 2
        ROPE_BASE = 10000.0
        LN_EPS = 1e-05

        def _rope_sin_cos(S, D, dtype):
            inv_freq = 1.0 / ROPE_BASE ** (jnp.arange(0, D, 2, dtype=jnp.float32) / D)
            freqs = jnp.arange(S, dtype=jnp.float32)[:, None] * inv_freq[None, :]
            sin = jnp.sin(freqs).astype(dtype)[None, :, None, :]
            cos = jnp.cos(freqs).astype(dtype)[None, :, None, :]
            return (sin, cos)

        def _apply_rope(x, sin, cos):
            x1, x2 = (x[..., 0::2], x[..., 1::2])
            r1 = x1 * cos - x2 * sin
            r2 = x1 * sin + x2 * cos
            return jnp.stack([r1, r2], axis=-1).reshape(x.shape)

        def _layer_norm(x, w, b):
            mu = jnp.mean(x, axis=-1, keepdims=True)
            var = jnp.mean(jnp.square(x - mu), axis=-1, keepdims=True)
            return (x - mu) * jax.lax.rsqrt(var + LN_EPS) * w + b
        B, S, E = x.shape
        H = NUM_HEADS
        D = E // H
        xh = x.reshape(B, S, H, D)
        sin, cos = _rope_sin_cos(S, D, x.dtype)
        q_in = _apply_rope(xh, sin, cos).reshape(B, S, E)
        k_in = q_in
        v_in = x
        Wq, Wk, Wv = jnp.split(in_proj_w, 3, axis=0)
        bq, bk, bv = jnp.split(in_proj_b, 3, axis=0)
        q = (q_in @ Wq.T + bq).reshape(B, S, H, D)
        k = (k_in @ Wk.T + bk).reshape(B, S, H, D)
        v = (v_in @ Wv.T + bv).reshape(B, S, H, D)
        scale = 1.0 / jnp.sqrt(jnp.asarray(D, dtype=x.dtype))
        scores = jnp.einsum('bqhd,bkhd->bhqk', q, k) * scale
        causal = jnp.tril(jnp.ones((S, S), dtype=bool))
        scores = jnp.where(causal[None, None], scores, jnp.asarray(-jnp.inf, dtype=scores.dtype))
        attn = jax.nn.softmax(scores, axis=-1)
        ctx = jnp.einsum('bhqk,bkhd->bqhd', attn, v).reshape(B, S, E)
        attn_out = ctx @ out_proj_w.T + out_proj_b
        x1 = _layer_norm(x + attn_out, ln1_w, ln1_b)
        gates = jax.nn.softmax(x1 @ gate_w.T + gate_b, axis=-1)
        _, top_idx = jax.lax.top_k(gates, TOP_K)
        top_gates = jnp.take_along_axis(gates, top_idx, axis=-1)
        expert_outputs = jnp.einsum('bsd,efd->bsef', x1, expert_w) + expert_b[None, None]
        sel = jnp.take_along_axis(expert_outputs, top_idx[..., None], axis=2)
        moe_out = jnp.sum(sel * top_gates[..., None], axis=2)
        return _layer_norm(x1 + moe_out, ln2_w, ln2_b)
    x = L0_attn_x
    x = _layernorm(x + _L0_attn_ref(x, L0_attn_W_q, L0_attn_W_k, L0_attn_W_v, L0_attn_W_o), axis=-1)
    x = _layernorm(x + _L0_ffn_ref(x, L0_ffn_in_proj_w, L0_ffn_in_proj_b, L0_ffn_out_proj_w, L0_ffn_out_proj_b, L0_ffn_gate_w, L0_ffn_gate_b, L0_ffn_expert_w, L0_ffn_expert_b, L0_ffn_ln1_w, L0_ffn_ln1_b, L0_ffn_ln2_w, L0_ffn_ln2_b), axis=-1)
    return x

_drawn_inputs = setup_inputs


def setup_inputs(seed=0):
    import zlib

    import numpy as np

    out = dict(_drawn_inputs(seed))
    spreads = {'L0_ffn_in_proj_b': (0.0, 0.559),
     'L0_ffn_out_proj_b': (0.0, 0.1),
     'L0_ffn_gate_b': (0.0, 0.404),
     'L0_ffn_expert_b': (0.0, 0.751),
     'L0_ffn_ln1_w': (1.0, 0.2),
     'L0_ffn_ln1_b': (0.0, 0.1),
     'L0_ffn_ln2_w': (1.0, 0.2),
     'L0_ffn_ln2_b': (0.0, 0.1)}
    factors = {'L0_attn_W_q': 3.289,
     'L0_attn_W_k': 3.424,
     'L0_ffn_in_proj_w': 8.0,
     'L0_ffn_out_proj_w': 4.447}
    for name, (base, spread) in spreads.items():
        noise = np.random.default_rng([zlib.crc32(name.encode()), seed]).standard_normal(out[name].shape)
        drawn = base * np.exp(spread * noise) if base else spread * noise
        out[name] = jnp.asarray(drawn.astype(out[name].dtype))
    for name, factor in factors.items():
        out[name] = (out[name] * factor).astype(out[name].dtype)
    return out
```

```python
from contextlib import ExitStack

import concourse.bass as bass
from concourse import mybir

ALU = mybir.AluOpType
ACT = mybir.ActivationFunctionType
F32 = mybir.dt.float32
F32R = mybir.dt.float32r
BF16 = mybir.dt.bfloat16
U32 = mybir.dt.uint32
AX = mybir.AxisListType

P = 128
NB, T, D = 32, 256, 128
HID = 64
NPAIR = NB // 2
NT = T // P
H, HD = 16, 8
G = 4
NG = H // G
VW = 32
E = 8
EPS = 1e-5
SCALE = HD ** -0.5
UNITS = 3 * NG
TRI = T + P
ROWS_HI, ROWS_MID, ROWS_LO = 0, 8, 64
ROW_MAX = 126
NSTACK = 6

FIRST, LOOP_FROM, LOOP_TO, LAST = -6, 3, 23, NB + 1
UNROLL = 4

PACK = {}
_at = 0
for _name, _width in (
    ("ident", P), ("w_lin", 3 * HID), ("w_lin_out", 2 * D), ("w_qk", 2 * D), ("w_v", D), ("w_out", D),
    ("w_gate", E), ("w_expert", E * D), ("b_v", D), ("b_out", D), ("b_gate", E), ("b_qk", 2),
    ("ln1_w", D), ("ln1_b", D), ("ln2_w", D), ("ln2_b", D), ("rope_cos", NT * D), ("rope_sin", NT * D),
    ("causal", TRI), ("above", G * P), ("halves", 2), ("iota", E),
):
    PACK[_name] = (_at, _width)
    _at += _width
PACK_W = _at


class Step:

    def __init__(self, first, loop=None):
        self.first, self.loop = first, loop

    def batch(self, k):
        return self.first + k if self.loop is None else self.loop * UNROLL + (self.first + k)

    def pair(self, k):
        n = (self.first + k) // 2
        return n if self.loop is None else self.loop * (UNROLL // 2) + n

    def has(self, k):
        return self.loop is not None or 0 <= self.first + k < NB

    def has_pair(self, k):
        even = (self.first + k) % 2 == 0
        return even and (self.loop is not None or 0 <= self.first + k < NB)

    def began(self, k):
        return self.loop is not None or self.first + k >= 0

    def slot(self, k, ring):
        return (self.first + k) % ring

    def pair_slot(self, k):
        return (self.first + k) // 2 % 2

    def pair_round(self, k):
        n = (self.first + k) // 2 // 2
        return n if self.loop is None else self.loop * (UNROLL // 4) + n


def steps(eng, step):
    for s in range(FIRST, LOOP_FROM):
        step(Step(s))
    with eng.Fori(0, (LOOP_TO - LOOP_FROM) // UNROLL) as loop:
        for s in range(LOOP_FROM, LOOP_FROM + UNROLL):
            step(Step(s, loop))
    for s in range(LOOP_TO, LAST + 1):
        step(Step(s))


class Signal:

    def __init__(self, sem, per, count, by):
        self.sem, self.per, self.count, self.by = sem, per, count, by

    def at(self, index, nth=None):
        nth = self.per if nth is None else nth
        if isinstance(index, int) and index >= self.count:
            index, nth = self.count - 1, self.per
        return (index * self.per + nth) * self.by


def build(nc, x_d, pack_d, eb_d, out_d):
    x_v = x_d.rearrange("(j b) (t p) d -> j p (b t) d", b=2, p=P)
    out_v = out_d.rearrange("b (t p) d -> b p t d", p=P)

    with ExitStack() as ctx:
        def sb(name, shape, dt=F32):
            return ctx.enter_context(nc.sbuf_tensor(name, shape, dt))

        def signal(name, per=1, count=NB, by=1):
            return Signal(ctx.enter_context(nc.semaphore(name)), per, count, by)

        pack = sb("pack", [P, PACK_W])
        cut = {n: pack[:, a:a + w] for n, (a, w) in PACK.items()}
        ident = cut["ident"]
        w_lin = cut["w_lin"]
        w_expert = cut["w_expert"]
        ident_b = sb("ident_b", [P, P], BF16)
        neg_ident = sb("neg_ident", [P, P])
        above_b = sb("above_b", [P, G * P], BF16)
        eb_row = sb("eb_row", [1, E * D])
        eb_st = sb("eb_st", [P, E * D], F32R)
        ones_r = sb("ones_r", [P, P], F32R)
        ones_f = sb("ones_f", [P, T])
        ones_row = sb("ones_row", [2, H * T])
        half_neg = sb("half_neg", [P, 2 * NT])
        eps_t = sb("eps_t", [P, 2 * NT])

        x_in = [sb(f"x_in{i}", [P, 2 * NT, D]) for i in range(2)]
        xT = sb("xT", [P, 2 * T])
        ex_qk = sb("ex_qk", [P, 2, T])
        re_qk = sb("re_qk", [P, 2, T])
        q_f = sb("q_f", [P, T])
        q_z = sb("q_z", [P, 2, T])
        kT = sb("kT", [P, T])
        vT = sb("vT", [P, T])
        zT = sb("zT", [P, T])
        qzT = sb("qzT", [P, T])
        lin_sc = [sb(f"lin_sc{i}", [P, TRI]) for i in range(2)]
        k_tok = sb("k_tok", [P, NT, P])
        oT = sb("oT", [P, T])
        den = sb("den", [P, 4])
        den_inv = sb("den_inv", [P, 4])
        u_lin = sb("u_lin", [P, 2 * NT, D])
        st_p = sb("st_p", [P, 2 * NT, 6])
        mv_p = sb("mv_p", [P, 2 * NT, 2])
        ve_p = sb("ve_p", [P, 2 * NT])
        rs_p = sb("rs_p", [P, 2 * NT])
        xh = sb("xh", [P, 4, NT, D])

        q_in = [sb(f"q_in{i}", [P, NT, D]) for i in range(2)]
        xqT = sb("xqT", [P, 2, T])
        rot_c = sb("rot_c", [P, NT, D])
        rot_t = sb("rot_t", [P, NT, D])
        hl = sb("hl", [P, 4, T], F32R)
        q_st = [sb(f"q_st{i}", [P, H * T], F32R) for i in range(2)]
        k_st = [sb(f"k_st{i}", [P, H * T], F32R) for i in range(2)]
        v_aug = [sb(f"v_aug{i}", [P, NT, H, VW]) for i in range(2)]
        xb_out = [sb(f"xb_out{i}", [P, NT, D]) for i in range(2)]
        xb_ln2 = [sb(f"xb_ln2{i}", [P, NT, D]) for i in range(2)]

        mx = sb("mx", [P, 3, H])
        m_tok = sb("m_tok", [P, H])
        m_hl = sb("m_hl", [H, 2, T], F32R)
        probs = [sb(f"probs{i}", [P, 3, G, P]) for i in range(2)]
        ctx_a = sb("ctx_a", [P, NG, T])

        rd = sb("rd", [P, NT, H])
        ctx_t = sb("ctx_t", [P, NT, D])
        ctxT = sb("ctxT", [P, T])
        u2 = sb("u2", [P, NT, D])
        st1 = sb("st1", [P, NT, 6])
        mv1 = sb("mv1", [P, NT, 2])
        ve1 = sb("ve1", [P, NT])
        rs1 = sb("rs1", [P, NT])
        n1 = sb("n1", [P, NT, D])
        n1w = sb("n1w", [P, NT, D])
        x1 = sb("x1", [P, NT, D])
        x1T = sb("x1T", [P, T])
        lg = sb("lg", [P, NT, E])
        top = sb("top", [P, NT, 8])
        topi = sb("topi", [P, NT, 8], U32)
        topf = sb("topf", [P, NT, 8])
        lgd = sb("lgd", [P, NT, E])
        ge = sb("ge", [P, NT, E])
        gsum = sb("gsum", [P, NT])
        ginv = sb("ginv", [P, NT])
        hit = sb("hit", [P, 2, NT, E])
        sel = sb("sel", [P, NT, E])
        gsel = sb("gsel", [P, NT, E])
        gate = sb("gate", [P, NT, E])
        acc = sb("acc", [P, NT, 2, D])
        st2 = sb("st2", [P, NT, 6])
        mv2 = sb("mv2", [P, NT, 2])
        ve2 = sb("ve2", [P, NT])
        rs2 = sb("rs2", [P, NT])
        n2 = sb("n2", [P, NT, D])
        n2w = sb("n2w", [P, NT, D])
        z3 = sb("z3", [P, NT, D])
        st3 = sb("st3", [P, NT, 6])
        mv3 = sb("mv3", [P, NT, 2])
        ve3 = sb("ve3", [P, NT])
        rs3 = sb("rs3", [P, NT])
        y = sb("y", [P, NT, D])

        bank = [ctx.enter_context(nc.psum_tensor(f"bank{i}", [P, 512], F32)) for i in range(8)]
        SA, SB, PV, MA, MB, MC = bank[0:2], bank[2:4], bank[4], bank[5], bank[6], bank[7]

        loaded = signal("loaded", 2, 1, 16)
        setup_v = signal("setup_v", 1, 1)
        setup_q = signal("setup_q", 2, 1)
        setup_p = signal("setup_p", 1, 1)
        setup_done = signal("setup_done", 1, 1)
        ones_landed = signal("ones_landed", 2, 1, 16)
        x_landed = [signal(f"x_landed{i}", 1, NPAIR // 2, 16) for i in range(2)]
        p1_ready = signal("p1_ready", 1, NPAIR)
        xT_ready = signal("xT_ready", 1, NPAIR)
        p2v_ready = signal("p2v_ready", 1, NPAIR)
        p2qk_ready = signal("p2qk_ready", 1, NPAIR)
        vT_ready = signal("vT_ready", 1, NPAIR)
        phi_parts = signal("phi_parts", 1, NPAIR)
        phi_ready = signal("phi_ready", 1, NPAIR)
        q_split = signal("q_split", 1, NPAIR)
        z_ready = signal("z_ready", 1, NPAIR)
        qz_ready = signal("qz_ready", 1, NPAIR)
        lin_ready = signal("lin_ready", 2, NPAIR)
        lin_masked = signal("lin_masked", 2, NPAIR)
        ktok_ready = signal("ktok_ready", 1, NPAIR)
        ktok_copied = signal("ktok_copied", 1, NPAIR)
        oT_ready = signal("oT_ready", 1, NPAIR)
        oT_copied = signal("oT_copied", 1, NPAIR)
        den_ready = signal("den_ready", 1, NPAIR)
        den_max = signal("den_max", 1, NPAIR)
        den_done = signal("den_done", 1, NPAIR)
        p5_ready = signal("p5_ready", 1, NPAIR)
        u_ready = signal("u_ready", 1, NPAIR)
        stp_ready = signal("stp_ready", 1, NPAIR)
        mvp_ready = signal("mvp_ready", 1, NPAIR)
        vep_ready = signal("vep_ready", 1, NPAIR)
        rsp_ready = signal("rsp_ready", 1, NPAIR)
        xh_ready = signal("xh_ready", 1, NPAIR)

        rot_ready = signal("rot_ready", 2)
        xb_ready = signal("xb_ready")
        q1_ready = signal("q1_ready")
        xqT_ready = signal("xqT_ready")
        v_ready = signal("v_ready")
        v_stored = signal("v_stored")
        qk_ready = signal("qk_ready")
        hi_ready = signal("hi_ready")
        lo_ready = signal("lo_ready")
        stack_landed = signal("stack_landed", NSTACK, NB, 16)
        a_ready = signal("a_ready", UNITS)
        a_used = signal("a_used", UNITS)
        m_ready = signal("m_ready")
        mT_ready = signal("mT_ready")
        mhi_ready = signal("mhi_ready")
        mlo_ready = signal("mlo_ready")
        m_landed = signal("m_landed", 2, NB, 16)
        b_ready = signal("b_ready", UNITS)
        b_used = signal("b_used", UNITS)
        masked = signal("masked", NG)
        pv_ready = signal("pv_ready", NG)
        pv_copied = signal("pv_copied", 2)

        c1_ready = signal("c1_ready", NT)
        c1_inv = signal("c1_inv", NT)
        ctx_ready = signal("ctx_ready", NT)
        c2_ready = signal("c2_ready")
        ctxT_ready = signal("ctxT_ready")
        c3_ready = signal("c3_ready")
        u2_ready = signal("u2_ready")
        st1_ready = signal("st1_ready")
        mv1_ready = signal("mv1_ready")
        ve1_ready = signal("ve1_ready")
        rs1_ready = signal("rs1_ready")
        n1_ready = signal("n1_ready")
        n1w_ready = signal("n1w_ready")
        x1_ready = signal("x1_ready")
        c4_ready = signal("c4_ready")
        x1T_ready = signal("x1T_ready")
        gl_ready = signal("gl_ready")
        lg_ready = signal("lg_ready")
        top_ready = signal("top_ready")
        topi_ready = signal("topi_ready", 2)
        ge_ready = signal("ge_ready")
        hit_ready = signal("hit_ready", 2)
        sel_ready = signal("sel_ready")
        gsel_ready = signal("gsel_ready")
        gsum_ready = signal("gsum_ready")
        ginv_ready = signal("ginv_ready")
        gate_ready = signal("gate_ready")
        ex_ready = signal("ex_ready", 2 * NT)
        acc_ready = signal("acc_ready", NT * E)
        st2_ready = signal("st2_ready")
        mv2_ready = signal("mv2_ready")
        ve2_ready = signal("ve2_ready")
        rs2_ready = signal("rs2_ready")
        n2_ready = signal("n2_ready")
        n2w_ready = signal("n2w_ready")
        z3_ready = signal("z3_ready")
        st3_ready = signal("st3_ready")
        mv3_ready = signal("mv3_ready")
        ve3_ready = signal("ve3_ready")
        rs3_ready = signal("rs3_ready")
        y_ready = signal("y_ready")
        stored = signal("stored", 1, NB, 16)

        block = ctx.enter_context(nc.Block())

        @block.sync
        def _(sp):
            sp.dma_start(pack[:, :], pack_d).then_inc(loaded.sem, 16)
            sp.dma_start(eb_row[:, :], eb_d).then_inc(loaded.sem, 16)
            sp.wait_ge(setup_done.sem, setup_done.at(0))
            for i in range(2):
                sp.dma_start(k_st[i][ROW_MAX:ROW_MAX + 2, :].bitcast(F32), ones_row[:, :]).then_inc(ones_landed.sem, 16)

            def step(s):
                if s.has_pair(6):
                    slot = s.pair_slot(6)
                    if s.began(2):
                        sp.wait_ge(u_ready.sem, u_ready.at(s.pair(2)))
                    sp.dma_start(x_in[slot][:, :, :], x_v[s.pair(6), :, :, :]).then_inc(x_landed[slot].sem, 16)
                if s.has(0):
                    sp.wait_ge(mlo_ready.sem, mlo_ready.at(s.batch(0)))
                    for r in range(2):
                        sp.dma_start(q_st[s.slot(0, 2)][ROW_MAX + r:ROW_MAX + r + 1, :].bitcast(F32),
                                     m_hl[:, r, :].bitcast(F32)).then_inc(m_landed.sem, 16)
                if s.has(1):
                    i = s.slot(1, 2)
                    if s.began(-1):
                        count = sp.to_reg(b_ready.at(s.batch(-1)))
                        sp.wait_ge(b_ready.sem, 1)
                        sp.wait_ge(b_ready.sem, count)
                    sp.wait_ge(lo_ready.sem, lo_ready.at(s.batch(1)))
                    for stack, part, row in ((q_st, 0, ROWS_HI), (k_st, 2, ROWS_HI), (q_st, 0, ROWS_MID),
                                             (k_st, 3, ROWS_MID), (q_st, 1, ROWS_LO), (k_st, 2, ROWS_LO)):
                        sp.dma_start(stack[i][row:row + HD, :].bitcast(F32),
                                     hl[:, part, :].bitcast(F32)).then_inc(stack_landed.sem, 16)
                if s.has(-2):
                    sp.wait_ge(y_ready.sem, y_ready.at(s.batch(-2)))
                    sp.dma_start(out_v[s.batch(-2), :, :, :], y[:, :, :]).then_inc(stored.sem, 16)

            steps(sp, step)
            sp.wait_ge(stored.sem, stored.at(NB - 1))

        @block.tensor
        def _(pe):
            pe.wait_ge(setup_done.sem, setup_done.at(0))
            pe.wait_ge(ones_landed.sem, ones_landed.at(0))
            mm = nc.tensor.matmul

            def a_unit(s, c, n):
                i, bank_ = s.slot(1, 2), SA[(3 * c + n) % 2]
                if n == 0 and c == 0:
                    pe.wait_ge(stack_landed.sem, stack_landed.at(s.batch(1)))
                if 3 * c + n < 2:
                    if s.began(-2):
                        pe.wait_ge(acc_ready.sem, acc_ready.at(s.batch(-2), 4 * (3 + n)))
                    if s.began(0):
                        pe.wait_ge(a_used.sem, a_used.at(s.batch(0), UNITS - 1 + n))
                else:
                    if s.began(1):
                        pe.wait_ge(a_used.sem, a_used.at(s.batch(1), 3 * c + n - 1))
                qt, kt, diagonal = min(n, 1), n // 2, n != 1
                if diagonal:
                    mm(bank_[:, :], ident_b[:, :], above_b[:, :], start=True, stop=False)
                for g in range(G):
                    h = G * c + g
                    last = mm(bank_[:, g * P:(g + 1) * P],
                              q_st[i][0:ROW_MAX, h * T + qt * P:h * T + (qt + 1) * P],
                              k_st[i][0:ROW_MAX, h * T + kt * P:h * T + (kt + 1) * P],
                              start=not diagonal, stop=g == G - 1 or not diagonal)
                last.then_inc(a_ready.sem, 1)

            def b_unit(s, c, n):
                i, bank_ = s.slot(0, 2), SB[(3 * c + n) % 2]
                if n == 0 and c == 0:
                    if s.began(0):
                        pe.wait_ge(m_landed.sem, m_landed.at(s.batch(0)))
                if 3 * c + n < 2:
                    if n == 0:
                        if s.began(1):
                            pe.wait_ge(lo_ready.sem, lo_ready.at(s.batch(1)))
                    else:
                        if s.began(-1):
                            pe.wait_ge(ctxT_ready.sem, ctxT_ready.at(s.batch(-1)))
                    if s.began(-1):
                        pe.wait_ge(b_used.sem, b_used.at(s.batch(-1), UNITS - 1 + n))
                else:
                    if s.began(0):
                        pe.wait_ge(b_used.sem, b_used.at(s.batch(0), 3 * c + n - 1))
                if n < 2:
                    for g in (2 * n, 2 * n + 1):
                        h = G * c + g
                        last = mm(bank_[:, (g % 2) * T:(g % 2 + 1) * T], k_st[i][:, h * T:h * T + P],
                                  q_st[i][:, h * T:(h + 1) * T], start=True, stop=True)
                else:
                    for g in range(G):
                        h = G * c + g
                        last = mm(bank_[:, g * P:(g + 1) * P], k_st[i][:, h * T + P:(h + 1) * T],
                                  q_st[i][:, h * T + P:(h + 1) * T], start=True, stop=True)
                last.then_inc(b_ready.sem, 1)

            def pv(s, k, c):
                b, i, col = s.batch(k), s.slot(k, 2), (c % 2) * T
                pe.wait_ge(masked.sem, masked.at(b, c + 1))
                if c >= 2:
                    pe.wait_ge(pv_copied.sem, pv_copied.at(b, 1))
                else:
                    if s.began(k - 1):
                        pe.wait_ge(pv_copied.sem, pv_copied.at(s.batch(k - 1), 2))
                for g in range(G):
                    h, rows = G * c + g, slice(VW * g, VW * (g + 1))
                    mm(PV[rows, col:col + T], v_aug[i][:, 0, h, :], probs[c % 2][:, 0:3:2, g, :],
                       start=True, stop=False)
                    last = mm(PV[rows, col + P:col + T], v_aug[i][:, 1, h, :], probs[c % 2][:, 1, g, :],
                              start=False, stop=True)
                last.then_inc(pv_ready.sem, 1)

            def experts(s, t, n, bank_):
                cols = slice(4 * n * D, 4 * (n + 1) * D)
                mm(bank_[:, :], ones_r[:, :], eb_st[:, cols], start=True, stop=False)
                mm(bank_[:, :], x1T[:, t * P:(t + 1) * P], w_expert[:, cols],
                   start=False, stop=True).then_inc(ex_ready.sem, 1)

            def section1(s):
                if s.has(0):
                    b = s.batch(0)
                    pe.wait_ge(m_ready.sem, m_ready.at(b))
                    p5_used(s)
                    if s.began(-2):
                        pe.wait_ge(lg_ready.sem, lg_ready.at(s.batch(-2)))
                    mm(MC[0:H, 0:P], mx[:, 0, :], neg_ident[:, :], start=True, stop=True)
                    mm(MC[0:H, P:T], m_tok[:, :], neg_ident[:, :], start=True, stop=True).then_inc(mT_ready.sem, 1)
                if s.has(1):
                    b = s.batch(1)
                    pe.wait_ge(rot_ready.sem, rot_ready.at(b))
                    if s.began(-1):
                        pe.wait_ge(b_used.sem, b_used.at(s.batch(-1), UNITS - 1))
                    for t in range(NT):
                        nc.tensor.transpose(SB[0][:, t * P:(t + 1) * P], xh[:, s.slot(1, 4), t, :], ident)
                    for t in range(NT):
                        last = nc.tensor.transpose(SB[0][:, T + t * P:T + (t + 1) * P],
                                                   q_in[s.slot(1, 2)][:, t, :], ident)
                    last.then_inc(q1_ready.sem, 1)
                if s.has(-1):
                    pv(s, -1, NG - 1)
                if s.has(1):
                    b = s.batch(1)
                    pe.wait_ge(xqT_ready.sem, xqT_ready.at(b))
                    if s.began(-1):
                        pe.wait_ge(b_used.sem, b_used.at(s.batch(-1)))
                    for t in range(NT):
                        last = mm(SB[1][:, t * D:(t + 1) * D], xqT[:, 0, t * P:(t + 1) * P], cut["w_v"],
                                  start=True, stop=True)
                    last.then_inc(v_ready.sem, 1)
                    for n in range(2):
                        last = mm(SB[0][:, n * T:(n + 1) * T], cut["w_qk"][:, n * D:(n + 1) * D],
                                  xqT[:, 1, :], start=True, stop=True)
                    last.then_inc(qk_ready.sem, 1)
                if s.has(-1):
                    b = s.batch(-1)
                    for t in range(NT):
                        bank_ = (MA, MB)[t]
                        if t == 0:
                            pe.wait_ge(pv_copied.sem, pv_copied.at(b, 2))
                        if s.began(-2):
                            pe.wait_ge(acc_ready.sem, acc_ready.at(s.batch(-2), 4 * (t + 1)))
                        for c in range(NG):
                            last = nc.tensor.transpose(bank_[:, c * P:(c + 1) * P],
                                                       ctx_a[:, c, t * P:(t + 1) * P], ident)
                        last.then_inc(c1_ready.sem, 1)
                if s.has_pair(3):
                    j = s.pair(3)
                    pe.wait_ge(q_split.sem, q_split.at(j))
                    pe.wait_ge(vT_ready.sem, vT_ready.at(j))
                    for n in range(2):
                        bank_ = (MA, MB)[n]
                        if s.began(-1):
                            pe.wait_ge(ctx_ready.sem, ctx_ready.at(s.batch(-1), n + 1))
                        mm(bank_[:, 0:T], vT[:, 0:P], q_z[:, n, :], start=True, stop=True)
                        mm(bank_[:, T:TRI], vT[:, P:T], q_z[:, n, P:T],
                           start=True, stop=True).then_inc(lin_ready.sem, 1)
                if s.has(-1):
                    b = s.batch(-1)
                    pe.wait_ge(ctx_ready.sem, ctx_ready.at(b))
                    if s.began(1):
                        pe.wait_ge(v_stored.sem, v_stored.at(s.batch(1)))
                    if not s.has(1):
                        pe.wait_ge(b_used.sem, b_used.at(s.batch(-1)))
                    for t in range(NT):
                        last = nc.tensor.transpose(SB[1][:, t * P:(t + 1) * P], ctx_t[:, t, :], ident)
                    last.then_inc(c2_ready.sem, 1)
                    pe.wait_ge(ctxT_ready.sem, ctxT_ready.at(b))
                    if s.began(0):
                        pe.wait_ge(mlo_ready.sem, mlo_ready.at(s.batch(0)))
                    for t in range(NT):
                        last = mm(MC[:, t * D:(t + 1) * D], ctxT[:, t * P:(t + 1) * P], cut["w_out"],
                                  start=True, stop=True)
                    last.then_inc(c3_ready.sem, 1)

            def p5_used(s):
                if s.began(2):
                    pe.wait_ge(u_ready.sem, u_ready.at(s.pair(2) if s.has_pair(2) else s.pair(1)))

            def section2(s):
                def ab(c):
                    for n in range(3):
                        if s.has(1):
                            a_unit(s, c, n)
                        if s.has(0):
                            b_unit(s, c, n)

                ab(0)
                if s.has_pair(4):
                    j, slot = s.pair(4), s.pair_slot(4)
                    pe.wait_ge(x_landed[slot].sem, x_landed[slot].at(s.pair_round(4)))
                    p5_used(s)
                    if s.began(0):
                        pe.wait_ge(mlo_ready.sem, mlo_ready.at(s.batch(0)))
                    if s.began(-1):
                        pe.wait_ge(u2_ready.sem, u2_ready.at(s.batch(-1)))
                    for n in range(2 * NT):
                        last = nc.tensor.transpose(MC[:, n * P:(n + 1) * P], x_in[slot][:, n, :], ident)
                    last.then_inc(p1_ready.sem, 1)
                if s.has_pair(3):
                    j = s.pair(3)
                    pe.wait_ge(vT_ready.sem, vT_ready.at(j))
                    if s.began(-1):
                        pe.wait_ge(u2_ready.sem, u2_ready.at(s.batch(-1)))
                    if s.began(0):
                        pe.wait_ge(mlo_ready.sem, mlo_ready.at(s.batch(0)))
                    pe.wait_ge(phi_ready.sem, phi_ready.at(j))
                    for t in range(NT):
                        last = nc.tensor.transpose(MC[:, t * P:(t + 1) * P], kT[:, t * P:(t + 1) * P], ident)
                    last.then_inc(ktok_ready.sem, 1)

                ab(1)
                if s.has(0):
                    pv(s, 0, 0)
                if s.has(-1):
                    b = s.batch(-1)
                    pe.wait_ge(x1_ready.sem, x1_ready.at(b))
                    if s.has_pair(3):
                        pe.wait_ge(lin_masked.sem, lin_masked.at(s.pair(3)))
                    for t in range(NT):
                        last = nc.tensor.transpose(MB[:, t * P:(t + 1) * P], x1[:, t, :], ident)
                    last.then_inc(c4_ready.sem, 1)
                if s.has_pair(4):
                    j = s.pair(4)
                    pe.wait_ge(xT_ready.sem, xT_ready.at(j))
                    for n in range(2):
                        last = mm(MC[HID * n:HID * (n + 1), 0:T], w_lin[:, 2 * HID:3 * HID],
                                  xT[:, n * T:(n + 1) * T], start=True, stop=True)
                    last.then_inc(p2v_ready.sem, 1)
                    if s.began(-1):
                        pe.wait_ge(ctx_ready.sem, ctx_ready.at(s.batch(-1)))
                    if s.began(-2):
                        pe.wait_ge(acc_ready.sem, acc_ready.at(s.batch(-2), 4))
                    for part in range(2):
                        for n in range(2):
                            last = mm(MA[HID * n:HID * (n + 1), part * T:(part + 1) * T],
                                      w_lin[:, part * HID:(part + 1) * HID], xT[:, n * T:(n + 1) * T],
                                      start=True, stop=True)
                    last.then_inc(p2qk_ready.sem, 1)
                if s.has_pair(3):
                    j = s.pair(3)
                    pe.wait_ge(ktok_copied.sem, ktok_copied.at(j))
                    pe.wait_ge(lin_masked.sem, lin_masked.at(j))
                    for n in range(2):
                        rows = slice(HID * n, HID * (n + 1))
                        mm(MC[rows, 0:T], k_tok[:, 0, rows], lin_sc[n][:, 0:T], start=True, stop=False)
                        last = mm(MC[rows, P:T], k_tok[:, 1, rows], lin_sc[n][:, T:TRI],
                                  start=False, stop=True)
                    last.then_inc(oT_ready.sem, 1)
                    pe.wait_ge(qz_ready.sem, qz_ready.at(j))
                    for t in range(NT):
                        last = mm(MA[:, 2 * t:2 * t + 2], qzT[:, t * P:(t + 1) * P], cut["halves"],
                                  start=True, stop=True)
                    last.then_inc(den_ready.sem, 1)

                ab(2)
                if s.has(0):
                    pv(s, 0, 1)
                if s.has(-1):
                    b = s.batch(-1)
                    pe.wait_ge(x1T_ready.sem, x1T_ready.at(b))
                    if s.has_pair(4):
                        pe.wait_ge(vT_ready.sem, vT_ready.at(s.pair(4)))
                        pe.wait_ge(phi_parts.sem, phi_parts.at(s.pair(4)))
                    if s.has_pair(3):
                        pe.wait_ge(oT_copied.sem, oT_copied.at(s.pair(3)))
                        pe.wait_ge(den_max.sem, den_max.at(s.pair(3)))
                    for t in range(NT):
                        last = mm(MC[:, t * E:(t + 1) * E], x1T[:, t * P:(t + 1) * P], cut["w_gate"],
                                  start=True, stop=True)
                    last.then_inc(gl_ready.sem, 1)
                    experts(s, 0, 0, MA)
                    experts(s, 0, 1, MB)

                ab(3)
                if s.has(0):
                    pv(s, 0, 2)
                if s.has(-1):
                    for n in range(2):
                        if s.began(1):
                            pe.wait_ge(a_used.sem, a_used.at(s.batch(1), UNITS - 1 + n))
                        experts(s, 1, n, SA[n])
                if s.has_pair(3):
                    j = s.pair(3)
                    pe.wait_ge(oT_copied.sem, oT_copied.at(j))
                    if s.began(-1):
                        pe.wait_ge(lg_ready.sem, lg_ready.at(s.batch(-1)))
                    for t in range(NT):
                        last = mm(MC[:, t * 2 * D:(t + 1) * 2 * D], oT[:, t * P:(t + 1) * P],
                                  cut["w_lin_out"], start=True, stop=True)
                    last.then_inc(p5_ready.sem, 1)

            def step(s):
                section1(s)
                section2(s)

            steps(pe, step)

        @block.scalar
        def _(act):
            act.wait_ge(setup_done.sem, setup_done.at(0))
            run = nc.scalar.activation

            def exps(s, c):
                if not s.has(0):
                    return
                b = s.batch(0)
                if c >= 2:
                    act.wait_ge(pv_ready.sem, pv_ready.at(b, c - 1))
                else:
                    if s.began(-1):
                        act.wait_ge(pv_ready.sem, pv_ready.at(s.batch(-1), c + 3))
                for n in range(3):
                    act.wait_ge(b_ready.sem, b_ready.at(b, 3 * c + n + 1))
                    src = SB[(3 * c + n) % 2][:, :]
                    if n < 2:
                        src = src.rearrange("p (g t x) -> p t g x", t=NT, x=P)
                        dst = probs[c % 2][:, 0:3:2, 2 * n:2 * n + 2, :]
                    else:
                        src = src.rearrange("p (g x) -> p g x", x=P)
                        dst = probs[c % 2][:, 1, :, :]
                    run(dst, src, ACT.Exp, scale=SCALE).then_inc(b_used.sem, 1)

            def pv_copy(s, k, half_):
                if s.began(k):
                    act.wait_ge(pv_ready.sem, pv_ready.at(s.batch(k), 2 * half_ + 2))
                if half_ == 0:
                    if s.began(k - 1):
                        act.wait_ge(c1_ready.sem, c1_ready.at(s.batch(k - 1)))
                run(ctx_a[:, 2 * half_:2 * half_ + 2, :],
                    PV[:, :].rearrange("p (c x) -> p c x", c=2), ACT.Copy).then_inc(pv_copied.sem, 1)

            def step(s):
                if s.has(0):
                    act.wait_ge(mT_ready.sem, mT_ready.at(s.batch(0)))
                    if s.began(-1):
                        act.wait_ge(m_landed.sem, m_landed.at(s.batch(-1)))
                    run(m_hl[:, 0, :], MC[0:H, 0:T], ACT.Copy).then_inc(mhi_ready.sem, 1)
                if s.has(1):
                    b = s.batch(1)
                    act.wait_ge(q1_ready.sem, q1_ready.at(b))
                    if s.began(0):
                        act.wait_ge(qk_ready.sem, qk_ready.at(s.batch(0)))
                    run(xqT[:, :, :], SB[0][:, :].rearrange("p (n x) -> p n x", n=2), ACT.Copy).then_inc(xqT_ready.sem, 1)
                if s.has(-1):
                    pv_copy(s, -1, 1)
                if s.has(1):
                    act.wait_ge(qk_ready.sem, qk_ready.at(b))
                    if s.began(0):
                        act.wait_ge(stack_landed.sem, stack_landed.at(s.batch(0)))
                    for n in range(2):
                        last = run(hl[:, 2 * n, :], SB[0][:, n * T:(n + 1) * T], ACT.Identity,
                                   bias=cut["b_qk"][:, n:n + 1])
                    last.then_inc(hi_ready.sem, 1)
                if s.has(-1):
                    act.wait_ge(c2_ready.sem, c2_ready.at(s.batch(-1)))
                    if s.began(-2):
                        act.wait_ge(c3_ready.sem, c3_ready.at(s.batch(-2)))
                    run(ctxT[:, :], SB[1][:, 0:T], ACT.Copy).then_inc(ctxT_ready.sem, 1)
                exps(s, 0)
                if s.has_pair(4):
                    act.wait_ge(p1_ready.sem, p1_ready.at(s.pair(4)))
                    if s.began(2):
                        act.wait_ge(p2qk_ready.sem, p2qk_ready.at(s.pair(2)))
                    run(xT[:, :], MC[:, :], ACT.Copy).then_inc(xT_ready.sem, 1)
                if s.has_pair(3):
                    act.wait_ge(ktok_ready.sem, ktok_ready.at(s.pair(3)))
                    if s.began(1):
                        act.wait_ge(oT_ready.sem, oT_ready.at(s.pair(1)))
                    run(k_tok[:, :, :], MC[:, 0:T].rearrange("p (t x) -> p t x", t=NT),
                        ACT.Copy).then_inc(ktok_copied.sem, 1)
                exps(s, 1)
                if s.has(-1):
                    act.wait_ge(c4_ready.sem, c4_ready.at(s.batch(-1)))
                    if s.began(-2):
                        act.wait_ge(ex_ready.sem, ex_ready.at(s.batch(-2)))
                    run(x1T[:, :], MB[:, 0:T], ACT.Copy).then_inc(x1T_ready.sem, 1)
                if s.has_pair(4):
                    j = s.pair(4)
                    act.wait_ge(p2v_ready.sem, p2v_ready.at(j))
                    if s.began(2):
                        act.wait_ge(lin_ready.sem, lin_ready.at(s.pair(2)))
                    run(vT[:, :], MC[:, 0:T], ACT.Copy).then_inc(vT_ready.sem, 1)
                    act.wait_ge(p2qk_ready.sem, p2qk_ready.at(j))
                    if s.began(2):
                        act.wait_ge(phi_ready.sem, phi_ready.at(s.pair(2)))
                    both = MA[:, :].rearrange("p (n x) -> p n x", n=2)
                    run(ex_qk[:, :, :], both, ACT.Exp)
                    run(re_qk[:, :, :], both, ACT.Relu).then_inc(phi_parts.sem, 1)
                if s.has_pair(3):
                    act.wait_ge(oT_ready.sem, oT_ready.at(s.pair(3)))
                    if s.began(1):
                        act.wait_ge(p5_ready.sem, p5_ready.at(s.pair(1)))
                    run(oT[:, :], MC[:, 0:T], ACT.Copy).then_inc(oT_copied.sem, 1)
                exps(s, 2)
                if s.has(0):
                    pv_copy(s, 0, 0)
                exps(s, 3)
                if s.has_pair(4):
                    act.wait_ge(phi_ready.sem, phi_ready.at(s.pair(4)))
                    if s.began(2):
                        act.wait_ge(lin_ready.sem, lin_ready.at(s.pair(2)))
                    for n in range(2):
                        rows = slice(HID * n, HID * (n + 1))
                        last = run(q_z[rows, n, :], q_f[rows, :], ACT.Copy)
                    last.then_inc(q_split.sem, 1)
                if s.has(-1):
                    act.wait_ge(topi_ready.sem, topi_ready.at(s.batch(-1)))
                    if s.began(-2):
                        act.wait_ge(gsel_ready.sem, gsel_ready.at(s.batch(-2)))
                        act.wait_ge(gsum_ready.sem, gsum_ready.at(s.batch(-2)))
                    run(ge[:, :, :], lgd[:, :, :], ACT.Exp).then_inc(ge_ready.sem, 1)

            steps(act, step)

        @block.vector
        def _(dve):
            vec = nc.vector
            dve.wait_ge(loaded.sem, loaded.at(0))
            vec.tensor_copy(ident_b[:, :], ident)
            vec.tensor_scalar(neg_ident[:, :], ident, -1.0, None, ALU.mult)
            vec.tensor_copy(above_b[:, :], cut["above"])
            vec.memset(ones_r[:, :].bitcast(F32), 1.0)
            vec.memset(ones_f[:, :], 1.0)
            vec.memset(ones_row[:, :], 1.0)
            vec.memset(q_z[:, :, :], 0.0)
            vec.memset(eb_st[:, :].bitcast(F32), 0.0)
            for i in range(2):
                vec.memset(q_st[i][:, :].bitcast(F32), 0.0)
            vec.memset(k_st[0][:, :].bitcast(F32), 0.0).then_inc(setup_v.sem, 1)
            dve.wait_ge(setup_v.sem, setup_v.at(0, 1))
            vec.tensor_copy(eb_st[0:1, :], eb_row[:, :]).then_inc(setup_v.sem, 1)
            dve.wait_ge(setup_v.sem, setup_v.at(0, 2))
            vec.tensor_tensor(eb_st[32:33, :], eb_row[:, :], eb_st[0:1, :].bitcast(F32),
                              ALU.subtract).then_inc(setup_v.sem, 1)
            dve.wait_ge(setup_v.sem, setup_v.at(0, 3))
            dve.wait_ge(setup_p.sem, setup_p.at(0))
            vec.memset(ones_f[:, :], 1.0).then_inc(setup_done.sem, 1)

            def maxima(s, c):
                if not s.has(1):
                    return
                b = s.batch(1)
                if c == 0:
                    if s.began(0):
                        dve.wait_ge(mT_ready.sem, mT_ready.at(s.batch(0)))
                for n in range(3):
                    dve.wait_ge(a_ready.sem, a_ready.at(b, 3 * c + n + 1))
                    vec.tensor_reduce(
            mx[:, n, G * c:G * (c + 1)],
            SA[(3 * c + n) % 2][:, :].rearrange("p (g x) -> p g x", g=G), AX.X, ALU.max).then_inc(a_used.sem, 1)

            def stats(src, st, mv, st_ready, mv_ready, index, n):
                for t in range(n):
                    last = vec.bn_stats(st[:, t, :], src(t))
                last.then_inc(st_ready.sem, 1)
                count = dve.to_reg(st_ready.at(index))
                dve.wait_ge(st_ready.sem, 1)
                dve.wait_ge(st_ready.sem, count)
                for t in range(n):
                    last = vec.bn_aggr(mv[:, t, :], st[:, t, :])
                last.then_inc(mv_ready.sem, 1)

            def normed(dst, src, mv, rs, n):
                for t in range(n):
                    last = vec.tensor_scalar(dst(t), src(t), mv[:, t, 0:1], rs[:, t:t + 1],
                                             ALU.subtract, ALU.mult)
                return last

            def combine(s, t, n, bank_):
                b = s.batch(-1)
                dve.wait_ge(ex_ready.sem, ex_ready.at(b, 2 * t + n + 1))
                for e in range(4 * n, 4 * n + 4):
                    before = x1[:, t, :] if e == 0 else acc[:, t, (e - 1) % 2, :]
                    if e > 0:
                        dve.wait_ge(acc_ready.sem, acc_ready.at(b, E * t + e))
                    vec.scalar_tensor_tensor(
         acc[:, t, e % 2, :], bank_[:, (e % 4) * D:(e % 4 + 1) * D], gate[:, t, e:e + 1],
         before, ALU.mult, ALU.add).then_inc(acc_ready.sem, 1)

            def step(s):
                if s.has(0):
                    b = s.batch(0)
                    dve.wait_ge(mhi_ready.sem, mhi_ready.at(b))
                    vec.tensor_tensor(m_hl[:, 1, :], MC[0:H, 0:T],
                                      m_hl[:, 0, :].bitcast(F32), ALU.subtract).then_inc(mlo_ready.sem, 1)
                if s.has(-2):
                    b = s.batch(-2)
                    dve.wait_ge(z3_ready.sem, z3_ready.at(b))
                    stats(lambda t: z3[:, t, :], st3, mv3, st3_ready, mv3_ready, b, NT)
                if s.has(1):
                    b = s.batch(1)
                    dve.wait_ge(v_ready.sem, v_ready.at(b))
                    if s.began(-1):
                        dve.wait_ge(pv_ready.sem, pv_ready.at(s.batch(-1)))
                    vec.tensor_tensor(
          v_aug[s.slot(1, 2)][:, :, :, 0:HD],
          SB[1][:, 0:T].rearrange("p (t h d) -> p t h d", t=NT, d=HD),
          cut["b_v"].rearrange("p (h d) -> p h d", d=HD).unsqueeze(1)
          .to_broadcast([P, NT, H, HD]), ALU.add).then_inc(v_stored.sem, 1)
                    dve.wait_ge(hi_ready.sem, hi_ready.at(b))
                    for n in range(2):
                        last = vec.scalar_tensor_tensor(
                            hl[:, 2 * n + 1, :], SB[0][:, n * T:(n + 1) * T], cut["b_qk"][:, n:n + 1],
                            hl[:, 2 * n, :].bitcast(F32), ALU.add, ALU.subtract)
                    last.then_inc(lo_ready.sem, 1)
                if s.has(-1):
                    b = s.batch(-1)
                    for t in range(NT):
                        by_head = (MA, MB)[t][:, :].rearrange("p (h w) -> p h w", w=VW)
                        dve.wait_ge(c1_ready.sem, c1_ready.at(b, t + 1))
                        vec.reciprocal(rd[:, t, :].unsqueeze(2), by_head[:, :, HD:HD + 1]).then_inc(c1_inv.sem, 1)
                        dve.wait_ge(c1_inv.sem, c1_inv.at(b, t + 1))
                        if t == 0:
                            if s.began(-2):
                                dve.wait_ge(c2_ready.sem, c2_ready.at(s.batch(-2)))
                        vec.tensor_tensor(
             ctx_t[:, t, :].rearrange("p (h d) -> p h d", d=HD), by_head[:, :, 0:HD],
             rd[:, t, :].unsqueeze(2).to_broadcast([P, H, HD]), ALU.mult).then_inc(ctx_ready.sem, 1)
                if s.has(-2):
                    b = s.batch(-2)
                    dve.wait_ge(rs3_ready.sem, rs3_ready.at(b))
                    if s.began(-3):
                        dve.wait_ge(stored.sem, stored.at(s.batch(-3)))
                    normed(lambda t: y[:, t, :], lambda t: z3[:, t, :], mv3, rs3, NT).then_inc(y_ready.sem, 1)
                if s.has_pair(3):
                    j = s.pair(3)
                    if s.began(1):
                        dve.wait_ge(oT_ready.sem, oT_ready.at(s.pair(1)))
                    for n in range(2):
                        dve.wait_ge(lin_ready.sem, lin_ready.at(j, n + 1))
                        vec.tensor_tensor(lin_sc[n][:, :], (MA, MB)[n][:, 0:TRI],
                                          cut["causal"], ALU.mult).then_inc(lin_masked.sem, 1)
                if s.has(-1):
                    b = s.batch(-1)
                    dve.wait_ge(c3_ready.sem, c3_ready.at(b))
                    dve.wait_ge(xb_ready.sem, xb_ready.at(b))
                    vec.tensor_tensor(u2[:, :, :], MC[:, 0:T].rearrange("p (t d) -> p t d", t=NT),
                                      xb_out[s.slot(-1, 2)][:, :, :], ALU.add).then_inc(u2_ready.sem, 1)
                    dve.wait_ge(u2_ready.sem, u2_ready.at(b))
                    if s.began(-2):
                        dve.wait_ge(ve1_ready.sem, ve1_ready.at(s.batch(-2)))
                    stats(lambda t: u2[:, t, :], st1, mv1, st1_ready, mv1_ready, b, NT)
                maxima(s, 0)
                if s.has(-1):
                    dve.wait_ge(rs1_ready.sem, rs1_ready.at(b))
                    if s.began(-2):
                        dve.wait_ge(n1w_ready.sem, n1w_ready.at(s.batch(-2)))
                    normed(lambda t: n1[:, t, :], lambda t: u2[:, t, :], mv1, rs1, NT).then_inc(n1_ready.sem, 1)
                maxima(s, 1)
                if s.has_pair(3):
                    j = s.pair(3)
                    dve.wait_ge(den_ready.sem, den_ready.at(j))
                    vec.tensor_scalar(den[:, :], MA[:, 0:4], 1e-6, None, ALU.max).then_inc(den_max.sem, 1)
                    dve.wait_ge(den_max.sem, den_max.at(j))
                    vec.reciprocal(den_inv[:, :], den[:, :]).then_inc(den_done.sem, 1)
                maxima(s, 2)
                if s.has_pair(4):
                    j = s.pair(4)
                    dve.wait_ge(phi_parts.sem, phi_parts.at(j))
                    if s.began(2):
                        dve.wait_ge(ktok_ready.sem, ktok_ready.at(s.pair(2)))
                        dve.wait_ge(z_ready.sem, z_ready.at(s.pair(2)))
                        dve.wait_ge(q_split.sem, q_split.at(s.pair(2)))
                        dve.wait_ge(qz_ready.sem, qz_ready.at(s.pair(2)))
                    vec.scalar_tensor_tensor(q_f[:, :], ex_qk[:, 0, :], 1.0, re_qk[:, 0, :], ALU.min, ALU.add)
                    vec.scalar_tensor_tensor(kT[:, :], ex_qk[:, 1, :], 1.0, re_qk[:, 1, :],
                                             ALU.min, ALU.add).then_inc(phi_ready.sem, 1)
                    dve.wait_ge(phi_ready.sem, phi_ready.at(j))
                    vec.tensor_tensor_scan(zT[:, :], ones_f[:, :], kT[:, :], 0.0,
                                           ALU.mult, ALU.add).then_inc(z_ready.sem, 1)
                if s.has(-1):
                    dve.wait_ge(gl_ready.sem, gl_ready.at(b))
                    vec.tensor_tensor(
          lg[:, :, :], MC[:, 0:NT * E].rearrange("p (t e) -> p t e", t=NT),
          cut["b_gate"].unsqueeze(1).to_broadcast([P, NT, E]), ALU.add).then_inc(lg_ready.sem, 1)
                    count = dve.to_reg(lg_ready.at(b))
                    dve.wait_ge(lg_ready.sem, 1)
                    dve.wait_ge(lg_ready.sem, count)
                    for t in range(NT):
                        last = vec.max(top[:, t, :], lg[:, t, :])
                    last.then_inc(top_ready.sem, 1)
                    count = dve.to_reg(top_ready.at(b))
                    dve.wait_ge(top_ready.sem, 1)
                    dve.wait_ge(top_ready.sem, count)
                    if s.began(-2):
                        count = dve.to_reg(hit_ready.at(s.batch(-2), 1))
                        dve.wait_ge(hit_ready.sem, 1)
                        dve.wait_ge(hit_ready.sem, count)
                    for t in range(NT):
                        last = vec.max_index(topi[:, t, :], top[:, t, :], lg[:, t, :])
                    last.then_inc(topi_ready.sem, 1)
                    vec.tensor_tensor(lgd[:, :, :], lg[:, :, :],
                                      top[:, :, 0:1].to_broadcast([P, NT, E]), ALU.subtract).then_inc(topi_ready.sem, 1)
                    dve.wait_ge(topi_ready.sem, topi_ready.at(b, 1))
                    if s.began(-2):
                        dve.wait_ge(hit_ready.sem, hit_ready.at(s.batch(-2), 2))
                    vec.tensor_copy(topf[:, :, :], topi[:, :, :]).then_inc(hit_ready.sem, 1)
                    dve.wait_ge(hit_ready.sem, hit_ready.at(b, 1))
                    if s.began(-2):
                        dve.wait_ge(sel_ready.sem, sel_ready.at(s.batch(-2)))
                    for r in range(2):
                        last = vec.tensor_tensor(hit[:, r, :, :],
                                                 cut["iota"].unsqueeze(1).to_broadcast([P, NT, E]),
                                                 topf[:, :, r:r + 1].to_broadcast([P, NT, E]), ALU.is_equal)
                    last.then_inc(hit_ready.sem, 1)
                maxima(s, 3)
                if s.has(-1):
                    dve.wait_ge(ge_ready.sem, ge_ready.at(b))
                    vec.tensor_reduce(gsum[:, :], ge[:, :, :], AX.X, ALU.add).then_inc(gsum_ready.sem, 1)
                    dve.wait_ge(gsum_ready.sem, gsum_ready.at(b))
                    vec.reciprocal(ginv[:, :], gsum[:, :]).then_inc(ginv_ready.sem, 1)
                    dve.wait_ge(ginv_ready.sem, ginv_ready.at(b))
                    dve.wait_ge(gsel_ready.sem, gsel_ready.at(b))
                    vec.tensor_tensor(gate[:, :, :], gsel[:, :, :],
                                      ginv[:, :].unsqueeze(2).to_broadcast([P, NT, E]),
                                      ALU.mult).then_inc(gate_ready.sem, 1)
                    dve.wait_ge(gate_ready.sem, gate_ready.at(b))
                    for t in range(NT):
                        for n in range(2):
                            combine(s, t, n, ((MA, MB), SA)[t][n])
                    dve.wait_ge(acc_ready.sem, acc_ready.at(b))
                    if s.began(-2):
                        dve.wait_ge(ve2_ready.sem, ve2_ready.at(s.batch(-2)))
                    stats(lambda t: acc[:, t, 1, :], st2, mv2, st2_ready, mv2_ready, b, NT)
                if s.has_pair(3):
                    j, slot = s.pair(3), s.pair_slot(3)
                    dve.wait_ge(p5_ready.sem, p5_ready.at(j))
                    dve.wait_ge(den_done.sem, den_done.at(j))
                    for n in range(2):
                        for t in range(NT):
                            last = vec.scalar_tensor_tensor(
                                u_lin[:, NT * n + t, :], MC[:, (2 * t + n) * D:(2 * t + n + 1) * D],
                                den_inv[:, 2 * t + n:2 * t + n + 1], x_in[slot][:, NT * n + t, :],
                                ALU.mult, ALU.add)
                    last.then_inc(u_ready.sem, 1)
                    dve.wait_ge(u_ready.sem, u_ready.at(j))
                    stats(lambda t: u_lin[:, t, :], st_p, mv_p, stp_ready, mvp_ready, j, 2 * NT)
                if s.has(-1):
                    dve.wait_ge(rs2_ready.sem, rs2_ready.at(b))
                    if s.began(-2):
                        dve.wait_ge(n2w_ready.sem, n2w_ready.at(s.batch(-2)))
                    normed(lambda t: n2[:, t, :], lambda t: acc[:, t, 1, :], mv2, rs2, NT).then_inc(n2_ready.sem, 1)
                if s.has(1):
                    dve.wait_ge(a_used.sem, a_used.at(s.batch(1)))
                    vec.tensor_tensor(m_tok[:, :], mx[:, 1, :], mx[:, 2, :], ALU.max).then_inc(m_ready.sem, 1)
                if s.has_pair(3):
                    dve.wait_ge(rsp_ready.sem, rsp_ready.at(j))
                    if s.began(0):
                        dve.wait_ge(xb_ready.sem, xb_ready.at(s.batch(0)))
                        dve.wait_ge(q1_ready.sem, q1_ready.at(s.batch(0)))
                        dve.wait_ge(rot_ready.sem, rot_ready.at(s.batch(0)))
                    first = s.slot(3, 4)
                    normed(lambda t: xh[:, first + t // NT, t % NT, :],
                           lambda t: u_lin[:, t, :], mv_p, rs_p, 2 * NT).then_inc(xh_ready.sem, 1)

            steps(dve, step)

        @block.gpsimd
        def _(pool):
            gp = nc.gpsimd
            gp.memset(half_neg[:, :], -0.5)
            gp.memset(eps_t[:, :], EPS)
            gp.memset(k_st[1][:, :].bitcast(F32), 0.0)
            for i in range(2):
                gp.memset(v_aug[i][:, :, :, :], 0.0).then_inc(setup_q.sem, 1)
            pool.wait_ge(setup_q.sem, setup_q.at(0))
            for i in range(2):
                last = gp.memset(v_aug[i][:, :, :, HD:HD + 1], 1.0)
            last.then_inc(setup_p.sem, 1)
            pool.wait_ge(setup_done.sem, setup_done.at(0))

            def inverse_root(mv, ve, rs, n, mv_ready, ve_ready, rs_ready, index):
                pool.wait_ge(mv_ready.sem, mv_ready.at(index))
                gp.tensor_tensor(ve[:, 0:n].unsqueeze(2), mv[:, 0:n, 1:2],
                                 eps_t[:, 0:n].unsqueeze(2), ALU.add).then_inc(ve_ready.sem, 1)
                pool.wait_ge(ve_ready.sem, ve_ready.at(index))
                gp.tensor_tensor(rs[:, 0:n], ve[:, 0:n], half_neg[:, 0:n], ALU.pow).then_inc(rs_ready.sem, 1)

            def causal(s, c):
                if not s.has(0):
                    return
                if s.began(0):
                    count = pool.to_reg(b_used.at(s.batch(0), 3 * c + 3))
                    pool.wait_ge(b_used.sem, 1)
                    pool.wait_ge(b_used.sem, count)
                blocks = probs[c % 2][:, 0:2, :, :].rearrange("p k g x -> p (k g) x")
                gp.affine_select(out=blocks, in_=blocks, compare_op=ALU.is_ge, fill=0.0, base=0,
                                 pattern=[[0, 2 * G], [1, P]], channel_multiplier=-1).then_inc(masked.sem, 1)

            def over_tiles(name):
                return cut[name].unsqueeze(1).to_broadcast([P, NT, D])

            def step(s):
                if s.has(2):
                    b, i = s.batch(2), s.slot(2, 2)
                    pool.wait_ge(xh_ready.sem, xh_ready.at(s.pair(2) if s.has_pair(2) else s.pair(1)))
                    if s.began(1):
                        pool.wait_ge(rot_ready.sem, rot_ready.at(s.batch(1)))
                    if s.began(0):
                        pool.wait_ge(q1_ready.sem, q1_ready.at(s.batch(0)))
                    x = xh[:, s.slot(2, 4), :, :]
                    pairs = x.rearrange("p t (m two) -> p (t m) two", two=2)
                    sin = cut["rope_sin"].rearrange("p (m two) -> p m two", two=2)
                    turned = rot_t[:, :, :].rearrange("p t (m two) -> p (t m) two", two=2)
                    gp.tensor_tensor(rot_c[:, :, :], x, cut["rope_cos"].rearrange("p (t d) -> p t d", t=NT),
                                     ALU.mult)
                    gp.tensor_tensor(turned[:, :, 0:1], pairs[:, :, 1:2], sin[:, :, 0:1], ALU.mult)
                    gp.tensor_tensor(turned[:, :, 1:2], pairs[:, :, 0:1], sin[:, :, 1:2],
                                     ALU.mult).then_inc(rot_ready.sem, 1)
                    pool.wait_ge(rot_ready.sem, rot_ready.at(b, 1))
                    gp.tensor_tensor(q_in[i][:, :, :], rot_c[:, :, :], rot_t[:, :, :], ALU.add).then_inc(rot_ready.sem, 1)
                if s.has_pair(3):
                    j = s.pair(3)
                    pool.wait_ge(z_ready.sem, z_ready.at(j))
                    if s.began(1):
                        pool.wait_ge(den_ready.sem, den_ready.at(s.pair(1)))
                    gp.tensor_tensor(qzT[:, :], q_f[:, :], zT[:, :], ALU.mult).then_inc(qz_ready.sem, 1)
                if s.has(-2):
                    inverse_root(mv3, ve3, rs3, NT, mv3_ready, ve3_ready, rs3_ready, s.batch(-2))
                if s.has(-1):
                    inverse_root(mv1, ve1, rs1, NT, mv1_ready, ve1_ready, rs1_ready, s.batch(-1))
                causal(s, 0)
                if s.has(-1):
                    b = s.batch(-1)
                    pool.wait_ge(n1_ready.sem, n1_ready.at(b))
                    gp.tensor_tensor(n1w[:, :, :], n1[:, :, :], over_tiles("ln1_w"), ALU.mult).then_inc(n1w_ready.sem, 1)
                    pool.wait_ge(n1w_ready.sem, n1w_ready.at(b))
                    if s.began(-2):
                        pool.wait_ge(acc_ready.sem, acc_ready.at(s.batch(-2)))
                    gp.tensor_tensor(x1[:, :, :], n1w[:, :, :], over_tiles("ln1_b"), ALU.add).then_inc(x1_ready.sem, 1)
                causal(s, 1)
                if s.has(0):
                    i = s.slot(0, 2)
                    pool.wait_ge(xh_ready.sem, xh_ready.at(s.pair(0) if s.has_pair(0) else s.pair(-1)))
                    if s.began(-2):
                        pool.wait_ge(u2_ready.sem, u2_ready.at(s.batch(-2)))
                    x = xh[:, s.slot(0, 4), :, :]
                    gp.tensor_tensor(xb_out[i][:, :, :], x, over_tiles("b_out"), ALU.add)
                    gp.tensor_tensor(xb_ln2[i][:, :, :], x, over_tiles("ln2_b"), ALU.add).then_inc(xb_ready.sem, 1)
                causal(s, 2)
                if s.has(-1):
                    pool.wait_ge(hit_ready.sem, hit_ready.at(b, 2))
                    if s.began(-2):
                        pool.wait_ge(gsel_ready.sem, gsel_ready.at(s.batch(-2)))
                    gp.tensor_tensor(sel[:, :, :], hit[:, 0, :, :], hit[:, 1, :, :], ALU.add).then_inc(sel_ready.sem, 1)
                    pool.wait_ge(sel_ready.sem, sel_ready.at(b))
                    pool.wait_ge(ge_ready.sem, ge_ready.at(b))
                    if s.began(-2):
                        pool.wait_ge(gate_ready.sem, gate_ready.at(s.batch(-2)))
                    gp.tensor_tensor(gsel[:, :, :], ge[:, :, :], sel[:, :, :], ALU.mult).then_inc(gsel_ready.sem, 1)
                causal(s, 3)
                if s.has(-1):
                    inverse_root(mv2, ve2, rs2, NT, mv2_ready, ve2_ready, rs2_ready, b)
                if s.has_pair(3):
                    inverse_root(mv_p, ve_p, rs_p, 2 * NT, mvp_ready, vep_ready, rsp_ready, s.pair(3))
                if s.has(-1):
                    pool.wait_ge(n2_ready.sem, n2_ready.at(b))
                    gp.tensor_tensor(n2w[:, :, :], n2[:, :, :], over_tiles("ln2_w"), ALU.mult).then_inc(n2w_ready.sem, 1)
                    pool.wait_ge(n2w_ready.sem, n2w_ready.at(b))
                    if s.began(-2):
                        pool.wait_ge(y_ready.sem, y_ready.at(s.batch(-2)))
                    gp.tensor_tensor(z3[:, :, :], n2w[:, :, :], xb_ln2[s.slot(-1, 2)][:, :, :],
                                     ALU.add).then_inc(z3_ready.sem, 1)
            steps(pool, step)


def kernel(L0_attn_x, L0_attn_W_q, L0_attn_W_k, L0_attn_W_v, L0_attn_W_o, L0_ffn_in_proj_w, L0_ffn_in_proj_b,
           L0_ffn_out_proj_w, L0_ffn_out_proj_b, L0_ffn_gate_w, L0_ffn_gate_b, L0_ffn_expert_w,
           L0_ffn_expert_b, L0_ffn_ln1_w, L0_ffn_ln1_b, L0_ffn_ln2_w, L0_ffn_ln2_b):
    import numpy as np
    import concourse.bacc as bacc
    from concourse.bass_utils import run_bass_kernel_spmd

    f = np.float32
    arr = np.asarray
    tri = np.triu(np.ones((P, P), f))
    inv_freq = (f(1.0) / np.power(f(10000.0), np.arange(0, HD, 2, dtype=f) / f(HD))).astype(f)
    angle = np.arange(T, dtype=f)[:, None] * inv_freq[None, :]
    cos = np.repeat(np.cos(angle), 2, axis=1)
    sin = np.stack([-np.sin(angle), np.sin(angle)], axis=-1).reshape(T, HD)

    def by_tile(a):
        return np.tile(a, (1, H)).reshape(NT, P, D).transpose(1, 0, 2).reshape(P, NT * D)

    halves = np.zeros((P, 2), f)
    halves[:HID, 0] = 1
    halves[HID:, 1] = 1

    def rows(v):
        return np.broadcast_to(arr(v)[None, :], (P, arr(v).shape[0]))

    def head_last(a):
        return a.reshape((H, HD) + a.shape[1:]).swapaxes(0, 1).reshape(a.shape)

    wi, bi = arr(L0_ffn_in_proj_w), arr(L0_ffn_in_proj_b)
    wo = arr(L0_attn_W_o)
    none = np.zeros_like(wo)
    parts = {
        "ident": np.eye(P, dtype=f),
        "w_lin": np.concatenate([arr(L0_attn_W_q), arr(L0_attn_W_k), arr(L0_attn_W_v)], axis=1),
        "w_lin_out": np.block([[wo, none], [none, wo]]),
        "w_qk": np.concatenate([head_last(wi[0:D]).T, head_last(wi[D:2 * D]).T], axis=1),
        "w_v": wi[2 * D:].T,
        "w_out": arr(L0_ffn_out_proj_w).T,
        "w_gate": arr(L0_ffn_gate_w).T,
        "w_expert": arr(L0_ffn_expert_w).transpose(2, 0, 1).reshape(D, E * D),
        "b_v": rows(bi[2 * D:]),
        "b_out": rows(L0_ffn_out_proj_b),
        "b_gate": rows(L0_ffn_gate_b),
        "b_qk": np.stack([head_last(bi[0:D]), head_last(bi[D:2 * D])], axis=1),
        "ln1_w": rows(L0_ffn_ln1_w), "ln1_b": rows(L0_ffn_ln1_b),
        "ln2_w": rows(L0_ffn_ln2_w), "ln2_b": rows(L0_ffn_ln2_b),
        "rope_cos": by_tile(cos), "rope_sin": by_tile(sin),
        "causal": np.concatenate([tri, np.ones((P, P), f), tri], axis=1),
        "above": np.tile(np.triu(np.full((P, P), -1e30, f), 1), (1, G)),
        "halves": halves,
        "iota": rows(np.arange(E, dtype=f)),
    }
    packed = np.ascontiguousarray(np.concatenate([parts[n] for n in PACK], axis=1))
    arrays = {"x": np.ascontiguousarray(arr(L0_attn_x)), "params": packed,
              "expert_b": np.ascontiguousarray(arr(L0_ffn_expert_b).reshape(1, E * D))}

    nc = bacc.Bacc("TRN2", target_bir_lowering=False, num_devices=1)
    args = [nc.dram_tensor(n, a.shape, F32, kind="ExternalInput").ap() for n, a in arrays.items()]
    out = nc.dram_tensor("out", (NB, T, D), F32, kind="ExternalOutput").ap()
    build(nc, *args, out)
    result = run_bass_kernel_spmd(nc, [arrays], core_ids=[0])
    return result.results[0]["out"]
```

```python
from contextlib import ExitStack

import concourse.bass as bass
from concourse import mybir

ALU = mybir.AluOpType
ACT = mybir.ActivationFunctionType
F32 = mybir.dt.float32
F32R = mybir.dt.float32r
BF16 = mybir.dt.bfloat16
U32 = mybir.dt.uint32
AX = mybir.AxisListType

P = 128
NB, T, D = 32, 256, 128
HID = 64
NPAIR = NB // 2
NT = T // P
H, HD = 16, 8
G = 4
NG = H // G
VW = 32
E = 8
EPS = 1e-5
SCALE = HD ** -0.5
UNITS = 3 * NG
TRI = T + P
ROWS_HI, ROWS_MID, ROWS_LO = 0, 8, 64
ROW_MAX = 126
NSTACK = 6

FIRST, LOOP_FROM, LOOP_TO, LAST = -6, 3, 23, NB + 1
UNROLL = 4

PACK = {}
_at = 0
for _name, _width in (
    ("ident", P), ("w_lin", 3 * HID), ("w_lin_out", 2 * D), ("w_qk", 2 * D), ("w_v", D), ("w_out", D),
    ("w_gate", E), ("w_expert", E * D), ("b_v", D), ("b_out", D), ("b_gate", E), ("b_qk", 2),
    ("ln1_w", D), ("ln1_b", D), ("ln2_w", D), ("ln2_b", D), ("rope_cos", NT * D), ("rope_sin", NT * D),
    ("causal", TRI), ("above", G * P), ("halves", 2), ("iota", E),
):
    PACK[_name] = (_at, _width)
    _at += _width
PACK_W = _at


class Step:

    def __init__(self, first, loop=None):
        self.first, self.loop = first, loop

    def batch(self, k):
        return self.first + k if self.loop is None else self.loop * UNROLL + (self.first + k)

    def pair(self, k):
        n = (self.first + k) // 2
        return n if self.loop is None else self.loop * (UNROLL // 2) + n

    def has(self, k):
        return self.loop is not None or 0 <= self.first + k < NB

    def has_pair(self, k):
        even = (self.first + k) % 2 == 0
        return even and (self.loop is not None or 0 <= self.first + k < NB)

    def began(self, k):
        return self.loop is not None or self.first + k >= 0

    def slot(self, k, ring):
        return (self.first + k) % ring

    def pair_slot(self, k):
        return (self.first + k) // 2 % 2

    def pair_round(self, k):
        n = (self.first + k) // 2 // 2
        return n if self.loop is None else self.loop * (UNROLL // 4) + n


def steps(eng, step):
    for s in range(FIRST, LOOP_FROM):
        step(Step(s))
    with eng.Fori(0, (LOOP_TO - LOOP_FROM) // UNROLL) as loop:
        for s in range(LOOP_FROM, LOOP_FROM + UNROLL):
            step(Step(s, loop))
    for s in range(LOOP_TO, LAST + 1):
        step(Step(s))


class Signal:

    def __init__(self, sem, per, count, by):
        self.sem, self.per, self.count, self.by = sem, per, count, by

    def at(self, index, nth=None):
        nth = self.per if nth is None else nth
        if isinstance(index, int) and index >= self.count:
            index, nth = self.count - 1, self.per
        return (index * self.per + nth) * self.by


def build(nc, x_d, pack_d, eb_d, out_d):
    x_v = x_d.rearrange("(j b) (t p) d -> j p (b t) d", b=2, p=P)
    out_v = out_d.rearrange("b (t p) d -> b p t d", p=P)

    with ExitStack() as ctx:
        def sb(name, shape, dt=F32):
            return ctx.enter_context(nc.sbuf_tensor(name, shape, dt))

        def signal(name, per=1, count=NB, by=1):
            return Signal(ctx.enter_context(nc.semaphore(name)), per, count, by)

        pack = sb("pack", [P, PACK_W])
        cut = {n: pack[:, a:a + w] for n, (a, w) in PACK.items()}
        ident = cut["ident"]
        w_lin = cut["w_lin"]
        w_expert = cut["w_expert"]
        ident_b = sb("ident_b", [P, P], BF16)
        neg_ident = sb("neg_ident", [P, P])
        above_b = sb("above_b", [P, G * P], BF16)
        eb_row = sb("eb_row", [1, E * D])
        eb_st = sb("eb_st", [P, E * D], F32R)
        ones_r = sb("ones_r", [P, P], F32R)
        ones_f = sb("ones_f", [P, T])
        ones_row = sb("ones_row", [2, H * T])
        half_neg = sb("half_neg", [P, 2 * NT])
        eps_t = sb("eps_t", [P, 2 * NT])

        x_in = [sb(f"x_in{i}", [P, 2 * NT, D]) for i in range(2)]
        xT = sb("xT", [P, 2 * T])
        ex_qk = sb("ex_qk", [P, 2, T])
        re_qk = sb("re_qk", [P, 2, T])
        q_f = sb("q_f", [P, T])
        q_z = sb("q_z", [P, 2, T])
        kT = sb("kT", [P, T])
        vT = sb("vT", [P, T])
        zT = sb("zT", [P, T])
        qzT = sb("qzT", [P, T])
        lin_sc = [sb(f"lin_sc{i}", [P, TRI]) for i in range(2)]
        k_tok = sb("k_tok", [P, NT, P])
        oT = sb("oT", [P, T])
        den = sb("den", [P, 4])
        den_inv = sb("den_inv", [P, 4])
        u_lin = sb("u_lin", [P, 2 * NT, D])
        st_p = sb("st_p", [P, 2 * NT, 6])
        mv_p = sb("mv_p", [P, 2 * NT, 2])
        ve_p = sb("ve_p", [P, 2 * NT])
        rs_p = sb("rs_p", [P, 2 * NT])
        xh = sb("xh", [P, 4, NT, D])

        q_in = [sb(f"q_in{i}", [P, NT, D]) for i in range(2)]
        xqT = sb("xqT", [P, 2, T])
        rot_c = sb("rot_c", [P, NT, D])
        rot_t = sb("rot_t", [P, NT, D])
        hl = sb("hl", [P, 4, T], F32R)
        q_st = [sb(f"q_st{i}", [P, H * T], F32R) for i in range(2)]
        k_st = [sb(f"k_st{i}", [P, H * T], F32R) for i in range(2)]
        v_aug = [sb(f"v_aug{i}", [P, NT, H, VW]) for i in range(2)]
        xb_out = [sb(f"xb_out{i}", [P, NT, D]) for i in range(2)]
        xb_ln2 = [sb(f"xb_ln2{i}", [P, NT, D]) for i in range(2)]

        mx = sb("mx", [P, 3, H])
        m_tok = sb("m_tok", [P, H])
        m_hl = sb("m_hl", [H, 2, T], F32R)
        probs = [sb(f"probs{i}", [P, 3, G, P]) for i in range(2)]
        ctx_a = sb("ctx_a", [P, NG, T])

        rd = sb("rd", [P, NT, H])
        ctx_t = sb("ctx_t", [P, NT, D])
        ctxT = sb("ctxT", [P, T])
        u2 = sb("u2", [P, NT, D])
        st1 = sb("st1", [P, NT, 6])
        mv1 = sb("mv1", [P, NT, 2])
        ve1 = sb("ve1", [P, NT])
        rs1 = sb("rs1", [P, NT])
        n1 = sb("n1", [P, NT, D])
        n1w = sb("n1w", [P, NT, D])
        x1 = sb("x1", [P, NT, D])
        x1T = sb("x1T", [P, T])
        lg = sb("lg", [P, NT, E])
        top = sb("top", [P, NT, 8])
        topi = sb("topi", [P, NT, 8], U32)
        topf = sb("topf", [P, NT, 8])
        lgd = sb("lgd", [P, NT, E])
        ge = sb("ge", [P, NT, E])
        gsum = sb("gsum", [P, NT])
        ginv = sb("ginv", [P, NT])
        hit = sb("hit", [P, 2, NT, E])
        sel = sb("sel", [P, NT, E])
        gsel = sb("gsel", [P, NT, E])
        gate = sb("gate", [P, NT, E])
        acc = sb("acc", [P, NT, 2, D])
        st2 = sb("st2", [P, NT, 6])
        mv2 = sb("mv2", [P, NT, 2])
        ve2 = sb("ve2", [P, NT])
        rs2 = sb("rs2", [P, NT])
        n2 = sb("n2", [P, NT, D])
        n2w = sb("n2w", [P, NT, D])
        z3 = sb("z3", [P, NT, D])
        st3 = sb("st3", [P, NT, 6])
        mv3 = sb("mv3", [P, NT, 2])
        ve3 = sb("ve3", [P, NT])
        rs3 = sb("rs3", [P, NT])
        y = sb("y", [P, NT, D])

        bank = [ctx.enter_context(nc.psum_tensor(f"bank{i}", [P, 512], F32)) for i in range(8)]
        SA, SB, PV, MA, MB, MC = bank[0:2], bank[2:4], bank[4], bank[5], bank[6], bank[7]

        loaded = signal("loaded", 2, 1, 16)
        setup_v = signal("setup_v", 1, 1)
        setup_q = signal("setup_q", 2, 1)
        setup_p = signal("setup_p", 1, 1)
        setup_done = signal("setup_done", 1, 1)
        ones_landed = signal("ones_landed", 2, 1, 16)
        x_landed = [signal(f"x_landed{i}", 1, NPAIR // 2, 16) for i in range(2)]
        p1_ready = signal("p1_ready", 1, NPAIR)
        xT_ready = signal("xT_ready", 1, NPAIR)
        p2v_ready = signal("p2v_ready", 1, NPAIR)
        p2qk_ready = signal("p2qk_ready", 1, NPAIR)
        vT_ready = signal("vT_ready", 1, NPAIR)
        phi_parts = signal("phi_parts", 1, NPAIR)
        phi_ready = signal("phi_ready", 1, NPAIR)
        q_split = signal("q_split", 1, NPAIR)
        z_ready = signal("z_ready", 1, NPAIR)
        qz_ready = signal("qz_ready", 1, NPAIR)
        lin_ready = signal("lin_ready", 2, NPAIR)
        lin_masked = signal("lin_masked", 2, NPAIR)
        ktok_ready = signal("ktok_ready", 1, NPAIR)
        ktok_copied = signal("ktok_copied", 1, NPAIR)
        oT_ready = signal("oT_ready", 1, NPAIR)
        oT_copied = signal("oT_copied", 1, NPAIR)
        den_ready = signal("den_ready", 1, NPAIR)
        den_max = signal("den_max", 1, NPAIR)
        den_done = signal("den_done", 1, NPAIR)
        p5_ready = signal("p5_ready", 1, NPAIR)
        u_ready = signal("u_ready", 1, NPAIR)
        stp_ready = signal("stp_ready", 1, NPAIR)
        mvp_ready = signal("mvp_ready", 1, NPAIR)
        vep_ready = signal("vep_ready", 1, NPAIR)
        rsp_ready = signal("rsp_ready", 1, NPAIR)
        xh_ready = signal("xh_ready", 1, NPAIR)

        rot_ready = signal("rot_ready", 2)
        xb_ready = signal("xb_ready")
        q1_ready = signal("q1_ready")
        xqT_ready = signal("xqT_ready")
        v_ready = signal("v_ready")
        v_stored = signal("v_stored")
        qk_ready = signal("qk_ready")
        hi_ready = signal("hi_ready")
        lo_ready = signal("lo_ready")
        stack_landed = signal("stack_landed", NSTACK, NB, 16)
        a_ready = signal("a_ready", UNITS)
        a_used = signal("a_used", UNITS)
        m_ready = signal("m_ready")
        mT_ready = signal("mT_ready")
        mhi_ready = signal("mhi_ready")
        mlo_ready = signal("mlo_ready")
        m_landed = signal("m_landed", 2, NB, 16)
        b_ready = signal("b_ready", UNITS)
        b_used = signal("b_used", UNITS)
        masked = signal("masked", NG)
        pv_ready = signal("pv_ready", NG)
        pv_copied = signal("pv_copied", 2)

        c1_ready = signal("c1_ready", NT)
        c1_inv = signal("c1_inv", NT)
        ctx_ready = signal("ctx_ready", NT)
        c2_ready = signal("c2_ready")
        ctxT_ready = signal("ctxT_ready")
        c3_ready = signal("c3_ready")
        u2_ready = signal("u2_ready")
        st1_ready = signal("st1_ready")
        mv1_ready = signal("mv1_ready")
        ve1_ready = signal("ve1_ready")
        rs1_ready = signal("rs1_ready")
        n1_ready = signal("n1_ready")
        n1w_ready = signal("n1w_ready")
        x1_ready = signal("x1_ready")
        c4_ready = signal("c4_ready")
        x1T_ready = signal("x1T_ready")
        gl_ready = signal("gl_ready")
        lg_ready = signal("lg_ready")
        top_ready = signal("top_ready")
        topi_ready = signal("topi_ready", 2)
        ge_ready = signal("ge_ready")
        hit_ready = signal("hit_ready", 2)
        sel_ready = signal("sel_ready")
        gsel_ready = signal("gsel_ready")
        gsum_ready = signal("gsum_ready")
        ginv_ready = signal("ginv_ready")
        gate_ready = signal("gate_ready")
        ex_ready = signal("ex_ready", 2 * NT)
        acc_ready = signal("acc_ready", NT * E)
        st2_ready = signal("st2_ready")
        mv2_ready = signal("mv2_ready")
        ve2_ready = signal("ve2_ready")
        rs2_ready = signal("rs2_ready")
        n2_ready = signal("n2_ready")
        n2w_ready = signal("n2w_ready")
        z3_ready = signal("z3_ready")
        st3_ready = signal("st3_ready")
        mv3_ready = signal("mv3_ready")
        ve3_ready = signal("ve3_ready")
        rs3_ready = signal("rs3_ready")
        y_ready = signal("y_ready")
        stored = signal("stored", 1, NB, 16)

        block = ctx.enter_context(nc.Block())

        @block.sync
        def _(sp):
            sp.dma_start(pack[:, :], pack_d).then_inc(loaded.sem, 16)
            sp.dma_start(eb_row[:, :], eb_d).then_inc(loaded.sem, 16)
            sp.wait_ge(setup_done.sem, setup_done.at(0))
            for i in range(2):
                sp.dma_start(k_st[i][ROW_MAX:ROW_MAX + 2, :].bitcast(F32), ones_row[:, :]).then_inc(ones_landed.sem, 16)

            def step(s):
                if s.has_pair(6):
                    slot = s.pair_slot(6)
                    if s.began(2):
                        sp.wait_ge(u_ready.sem, u_ready.at(s.pair(2)))
                    sp.dma_start(x_in[slot][:, :, :], x_v[s.pair(6), :, :, :]).then_inc(x_landed[slot].sem, 16)
                if s.has(-2):
                    sp.wait_ge(y_ready.sem, y_ready.at(s.batch(-2)))
                    sp.dma_start(out_v[s.batch(-2), :, :, :], y[:, :, :]).then_inc(stored.sem, 16)
                if s.has(2):
                    i = s.slot(2, 2)
                    if s.began(0):
                        count = sp.to_reg(b_ready.at(s.batch(0)))
                        sp.wait_ge(b_ready.sem, 1)
                        sp.wait_ge(b_ready.sem, count)
                    sp.wait_ge(lo_ready.sem, lo_ready.at(s.batch(2)))
                    for stack, part, row in ((q_st, 0, ROWS_HI), (k_st, 2, ROWS_HI), (q_st, 0, ROWS_MID),
                                             (k_st, 3, ROWS_MID), (q_st, 1, ROWS_LO), (k_st, 2, ROWS_LO)):
                        sp.dma_start(stack[i][row:row + HD, :].bitcast(F32),
                                     hl[:, part, :].bitcast(F32)).then_inc(stack_landed.sem, 16)
                if s.has(1):
                    sp.wait_ge(mlo_ready.sem, mlo_ready.at(s.batch(1)))
                    for r in range(2):
                        sp.dma_start(q_st[s.slot(1, 2)][ROW_MAX + r:ROW_MAX + r + 1, :].bitcast(F32),
                                     m_hl[:, r, :].bitcast(F32)).then_inc(m_landed.sem, 16)

            steps(sp, step)
            sp.wait_ge(stored.sem, stored.at(NB - 1))

        @block.tensor
        def _(pe):
            pe.wait_ge(setup_done.sem, setup_done.at(0))
            pe.wait_ge(ones_landed.sem, ones_landed.at(0))
            mm = nc.tensor.matmul

            def a_unit(s, c, n):
                i, bank_ = s.slot(1, 2), SA[(3 * c + n) % 2]
                if n == 0 and c == 0:
                    pe.wait_ge(stack_landed.sem, stack_landed.at(s.batch(1)))
                if 3 * c + n < 2:
                    if s.began(-2):
                        pe.wait_ge(acc_ready.sem, acc_ready.at(s.batch(-2), NT * E // 2))
                    if s.began(0):
                        pe.wait_ge(a_used.sem, a_used.at(s.batch(0), UNITS - 1 + n))
                else:
                    pe.wait_ge(a_used.sem, a_used.at(s.batch(1), 3 * c + n - 1))
                qt, kt, diagonal = min(n, 1), n // 2, n != 1
                if diagonal:
                    mm(bank_[:, :], ident_b[:, :], above_b[:, :], start=True, stop=False)
                for g in range(G):
                    h = G * c + g
                    last = mm(bank_[:, g * P:(g + 1) * P],
                              q_st[i][0:ROW_MAX, h * T + qt * P:h * T + (qt + 1) * P],
                              k_st[i][0:ROW_MAX, h * T + kt * P:h * T + (kt + 1) * P],
                              start=not diagonal, stop=g == G - 1 or not diagonal)
                last.then_inc(a_ready.sem, 1)

            def b_unit(s, c, n):
                i, bank_ = s.slot(0, 2), SB[(3 * c + n) % 2]
                if n == 0 and c == 0:
                    pe.wait_ge(m_landed.sem, m_landed.at(s.batch(0)))
                if 3 * c + n < 2:
                    if s.began(-2):
                        pe.wait_ge(acc_ready.sem, acc_ready.at(s.batch(-2)))
                    if s.began(-1):
                        pe.wait_ge(b_used.sem, b_used.at(s.batch(-1), UNITS - 1 + n))
                else:
                    pe.wait_ge(b_used.sem, b_used.at(s.batch(0), 3 * c + n - 1))
                if n < 2:
                    for g in (2 * n, 2 * n + 1):
                        h = G * c + g
                        last = mm(bank_[:, (g % 2) * T:(g % 2 + 1) * T], k_st[i][:, h * T:h * T + P],
                                  q_st[i][:, h * T:(h + 1) * T], start=True, stop=True)
                else:
                    for g in range(G):
                        h = G * c + g
                        last = mm(bank_[:, g * P:(g + 1) * P], k_st[i][:, h * T + P:(h + 1) * T],
                                  q_st[i][:, h * T + P:(h + 1) * T], start=True, stop=True)
                last.then_inc(b_ready.sem, 1)

            def ab(s, c):
                for n in range(3):
                    if s.has(1):
                        a_unit(s, c, n)
                    if s.has(0):
                        b_unit(s, c, n)

            def pv(s, c):
                if not s.has(0):
                    return
                b, i, col = s.batch(0), s.slot(0, 2), (c % 2) * T
                pe.wait_ge(masked.sem, masked.at(b, c + 1))
                if c >= 2:
                    pe.wait_ge(pv_copied.sem, pv_copied.at(b, 1))
                elif s.began(-1):
                    pe.wait_ge(ctxT_ready.sem, ctxT_ready.at(s.batch(-1)))
                for g in range(G):
                    h, rows = G * c + g, slice(VW * g, VW * (g + 1))
                    mm(PV[rows, col:col + T], v_aug[i][:, 0, h, :], probs[c % 2][:, 0:3:2, g, :],
                       start=True, stop=False)
                    last = mm(PV[rows, col + P:col + T], v_aug[i][:, 1, h, :], probs[c % 2][:, 1, g, :],
                              start=False, stop=True)
                last.then_inc(pv_ready.sem, 1)

            def experts(s, n, banks):
                cols = slice(4 * n * D, 4 * (n + 1) * D)
                for t in range(NT):
                    mm(banks[t][:, :], ones_r[:, :], eb_st[:, cols], start=True, stop=False)
                    mm(banks[t][:, :], x1T[:, t * P:(t + 1) * P], w_expert[:, cols],
                       start=False, stop=True).then_inc(ex_ready.sem, 1)

            def step(s):
                ab(s, 0)
                if s.has_pair(4):
                    j, slot = s.pair(4), s.pair_slot(4)
                    pe.wait_ge(x_landed[slot].sem, x_landed[slot].at(s.pair_round(4)))
                    if s.began(2):
                        pe.wait_ge(den_max.sem, den_max.at(s.pair(2)))
                    if s.began(-1):
                        pe.wait_ge(u2_ready.sem, u2_ready.at(s.batch(-1)))
                    if s.began(0):
                        pe.wait_ge(mlo_ready.sem, mlo_ready.at(s.batch(0)))
                    for n in range(2 * NT):
                        last = nc.tensor.transpose(MC[:, n * P:(n + 1) * P], x_in[slot][:, n, :], ident)
                    last.then_inc(p1_ready.sem, 1)
                if s.has_pair(3):
                    j = s.pair(3)
                    pe.wait_ge(q_split.sem, q_split.at(j))
                    pe.wait_ge(vT_ready.sem, vT_ready.at(j))
                    pe.wait_ge(phi_parts.sem, phi_parts.at(j))
                    if s.began(-1):
                        pe.wait_ge(u2_ready.sem, u2_ready.at(s.batch(-1)))
                    if s.began(0):
                        pe.wait_ge(mlo_ready.sem, mlo_ready.at(s.batch(0)))
                    for n in range(2):
                        bank_ = (MB, MC)[n]
                        mm(bank_[:, 0:T], vT[:, 0:P], q_z[:, n, :], start=True, stop=True)
                        mm(bank_[:, T:TRI], vT[:, P:T], q_z[:, n, P:T],
                           start=True, stop=True).then_inc(lin_ready.sem, 1)

                ab(s, 1)
                pv(s, 0)
                if s.has(-1):
                    b = s.batch(-1)
                    pe.wait_ge(x1_ready.sem, x1_ready.at(b))
                    if s.has_pair(3):
                        pe.wait_ge(lin_masked.sem, lin_masked.at(s.pair(3), 1))
                    elif s.began(2):
                        pe.wait_ge(u_ready.sem, u_ready.at(s.pair(2)))
                    for t in range(NT):
                        last = nc.tensor.transpose(MB[:, t * P:(t + 1) * P], x1[:, t, :], ident)
                    last.then_inc(c4_ready.sem, 1)
                if s.has(2):
                    b = s.batch(2)
                    pe.wait_ge(rot_ready.sem, rot_ready.at(b))
                    if s.began(1):
                        pe.wait_ge(v_stored.sem, v_stored.at(s.batch(1)))
                    for t in range(NT):
                        nc.tensor.transpose(MA[:, t * P:(t + 1) * P], xh[:, s.slot(2, 4), t, :], ident)
                    for t in range(NT):
                        last = nc.tensor.transpose(MA[:, T + t * P:T + (t + 1) * P],
                                                   q_in[s.slot(2, 2)][:, t, :], ident)
                    last.then_inc(q1_ready.sem, 1)
                if s.has_pair(4):
                    j = s.pair(4)
                    pe.wait_ge(xT_ready.sem, xT_ready.at(j))
                    if s.began(2):
                        pe.wait_ge(u_ready.sem, u_ready.at(s.pair(2)))
                    if s.began(-1):
                        pe.wait_ge(x1T_ready.sem, x1T_ready.at(s.batch(-1)))
                    for n in range(2):
                        last = mm(MB[HID * n:HID * (n + 1), T:2 * T], w_lin[:, 2 * HID:3 * HID],
                                  xT[:, n * T:(n + 1) * T], start=True, stop=True)
                    last.then_inc(p2v_ready.sem, 1)
                if s.has_pair(3):
                    j = s.pair(3)
                    pe.wait_ge(lin_masked.sem, lin_masked.at(j, 1))
                    if s.began(-1):
                        pe.wait_ge(x1T_ready.sem, x1T_ready.at(s.batch(-1)))
                    for t in range(NT):
                        last = nc.tensor.transpose(MB[:, T + t * P:T + (t + 1) * P],
                                                   kT[:, t * P:(t + 1) * P], ident)
                    last.then_inc(ktok_ready.sem, 1)

                ab(s, 2)
                pv(s, 1)
                if s.has(-1):
                    pe.wait_ge(x1T_ready.sem, x1T_ready.at(s.batch(-1)))
                    if s.has_pair(4):
                        pe.wait_ge(vT_ready.sem, vT_ready.at(s.pair(4)))
                    if s.has_pair(3):
                        pe.wait_ge(ktok_copied.sem, ktok_copied.at(s.pair(3)))
                    for t in range(NT):
                        last = mm(MB[:, t * E:(t + 1) * E], x1T[:, t * P:(t + 1) * P], cut["w_gate"],
                                  start=True, stop=True)
                    last.then_inc(gl_ready.sem, 1)
                if s.has(2):
                    pe.wait_ge(xqT_ready.sem, xqT_ready.at(s.batch(2)))
                    for n in range(2):
                        last = mm(MA[:, n * T:(n + 1) * T], cut["w_qk"][:, n * D:(n + 1) * D],
                                  xqT[:, 1, :], start=True, stop=True)
                    last.then_inc(qk_ready.sem, 1)
                if s.has_pair(4):
                    for part in range(2):
                        for n in range(2):
                            last = mm(MC[HID * n:HID * (n + 1), part * T:(part + 1) * T],
                                      w_lin[:, part * HID:(part + 1) * HID], xT[:, n * T:(n + 1) * T],
                                      start=True, stop=True)
                    last.then_inc(p2qk_ready.sem, 1)
                if s.has_pair(3):
                    j = s.pair(3)
                    pe.wait_ge(ktok_copied.sem, ktok_copied.at(j))
                    if s.began(-1):
                        pe.wait_ge(lg_ready.sem, lg_ready.at(s.batch(-1)))
                    pe.wait_ge(lin_masked.sem, lin_masked.at(j))
                    for n in range(2):
                        rows = slice(HID * n, HID * (n + 1))
                        mm(MB[rows, T:2 * T], k_tok[:, 0, rows], lin_sc[n][:, 0:T], start=True, stop=False)
                        last = mm(MB[rows, T + P:2 * T], k_tok[:, 1, rows], lin_sc[n][:, T:TRI],
                                  start=False, stop=True)
                    last.then_inc(oT_ready.sem, 1)
                    pe.wait_ge(qz_ready.sem, qz_ready.at(j))
                    for t in range(NT):
                        last = mm(MC[:, 2 * t:2 * t + 2], qzT[:, t * P:(t + 1) * P], cut["halves"],
                                  start=True, stop=True)
                    last.then_inc(den_ready.sem, 1)

                ab(s, 3)
                pv(s, 2)
                if s.has(-1):
                    pe.wait_ge(a_used.sem, a_used.at(s.batch(1)))
                    experts(s, 0, SA)
                if s.has(1):
                    b = s.batch(1)
                    pe.wait_ge(m_ready.sem, m_ready.at(b))
                    if s.has_pair(4):
                        pe.wait_ge(phi_parts.sem, phi_parts.at(s.pair(4)))
                    if s.has_pair(3):
                        pe.wait_ge(den_max.sem, den_max.at(s.pair(3)))
                    if s.began(-1):
                        pe.wait_ge(u2_ready.sem, u2_ready.at(s.batch(-1)))
                    mm(MC[0:H, 0:P], mx[:, 0, :], neg_ident[:, :], start=True, stop=True)
                    mm(MC[0:H, P:T], m_tok[:, :], neg_ident[:, :], start=True, stop=True).then_inc(mT_ready.sem, 1)
                pv(s, 3)
                if s.has(-1):
                    pe.wait_ge(b_used.sem, b_used.at(s.batch(0)))
                    experts(s, 1, SB)
                if s.has(0):
                    b = s.batch(0)
                    pe.wait_ge(pv_copied.sem, pv_copied.at(b))
                    for t in range(NT):
                        if t == 1:
                            if s.has(1):
                                pe.wait_ge(mlo_ready.sem, mlo_ready.at(s.batch(1)))
                            else:
                                pe.wait_ge(u2_ready.sem, u2_ready.at(s.batch(-1)))
                        for c in range(NG):
                            last = nc.tensor.transpose((PV, MC)[t][:, c * P:(c + 1) * P],
                                                       ctx_a[:, c, t * P:(t + 1) * P], ident)
                        last.then_inc(c1_ready.sem, 1)
                if s.has_pair(3):
                    j = s.pair(3)
                    pe.wait_ge(oT_copied.sem, oT_copied.at(j))
                    for t in range(NT):
                        last = mm(MB[:, t * 2 * D:(t + 1) * 2 * D], oT[:, t * P:(t + 1) * P],
                                  cut["w_lin_out"], start=True, stop=True)
                    last.then_inc(p5_ready.sem, 1)
                if s.has(2):
                    b = s.batch(2)
                    pe.wait_ge(lo_ready.sem, lo_ready.at(b))
                    for t in range(NT):
                        last = mm(MA[:, t * D:(t + 1) * D], xqT[:, 0, t * P:(t + 1) * P], cut["w_v"],
                                  start=True, stop=True)
                    last.then_inc(v_ready.sem, 1)
                if s.has(0):
                    b = s.batch(0)
                    pe.wait_ge(ctx_ready.sem, ctx_ready.at(b))
                    for t in range(NT):
                        last = nc.tensor.transpose(PV[:, t * P:(t + 1) * P], ctx_t[:, t, :], ident)
                    last.then_inc(c2_ready.sem, 1)
                    pe.wait_ge(ctxT_ready.sem, ctxT_ready.at(b))
                    for t in range(NT):
                        last = mm(MC[:, t * D:(t + 1) * D], ctxT[:, t * P:(t + 1) * P], cut["w_out"],
                                  start=True, stop=True)
                    last.then_inc(c3_ready.sem, 1)

            steps(pe, step)

        @block.scalar
        def _(act):
            act.wait_ge(setup_done.sem, setup_done.at(0))
            run = nc.scalar.activation

            def exps(s, c):
                if not s.has(0):
                    return
                b = s.batch(0)
                if c >= 2:
                    act.wait_ge(pv_ready.sem, pv_ready.at(b, c - 1))
                elif s.began(-1):
                    act.wait_ge(pv_ready.sem, pv_ready.at(s.batch(-1), c + 3))
                for n in range(3):
                    act.wait_ge(b_ready.sem, b_ready.at(b, 3 * c + n + 1))
                    src = SB[(3 * c + n) % 2][:, :]
                    if n < 2:
                        src = src.rearrange("p (g t x) -> p t g x", t=NT, x=P)
                        dst = probs[c % 2][:, 0:3:2, 2 * n:2 * n + 2, :]
                    else:
                        src = src.rearrange("p (g x) -> p g x", x=P)
                        dst = probs[c % 2][:, 1, :, :]
                    run(dst, src, ACT.Exp, scale=SCALE).then_inc(b_used.sem, 1)

            def pv_copy(s, half_):
                act.wait_ge(pv_ready.sem, pv_ready.at(s.batch(0), 2 * half_ + 2))
                if half_ == 0 and s.began(-1):
                    act.wait_ge(c1_ready.sem, c1_ready.at(s.batch(-1)))
                run(ctx_a[:, 2 * half_:2 * half_ + 2, :],
                    PV[:, :].rearrange("p (c x) -> p c x", c=2), ACT.Copy).then_inc(pv_copied.sem, 1)

            def step(s):
                exps(s, 0)
                if s.has_pair(4):
                    act.wait_ge(p1_ready.sem, p1_ready.at(s.pair(4)))
                    if s.began(2):
                        act.wait_ge(p2qk_ready.sem, p2qk_ready.at(s.pair(2)))
                    run(xT[:, :], MC[:, :], ACT.Copy).then_inc(xT_ready.sem, 1)
                exps(s, 1)
                if s.has(-1):
                    act.wait_ge(c4_ready.sem, c4_ready.at(s.batch(-1)))
                    if s.began(-2):
                        act.wait_ge(ex_ready.sem, ex_ready.at(s.batch(-2)))
                    run(x1T[:, :], MB[:, 0:T], ACT.Copy).then_inc(x1T_ready.sem, 1)
                if s.has(2):
                    act.wait_ge(q1_ready.sem, q1_ready.at(s.batch(2)))
                    if s.began(1):
                        act.wait_ge(v_ready.sem, v_ready.at(s.batch(1)))
                    run(xqT[:, :, :], MA[:, :].rearrange("p (n x) -> p n x", n=2),
                        ACT.Copy).then_inc(xqT_ready.sem, 1)
                if s.has_pair(4):
                    act.wait_ge(p2v_ready.sem, p2v_ready.at(s.pair(4)))
                    if s.began(2):
                        act.wait_ge(lin_ready.sem, lin_ready.at(s.pair(2)))
                    run(vT[:, :], MB[:, T:2 * T], ACT.Copy).then_inc(vT_ready.sem, 1)
                if s.has_pair(3):
                    act.wait_ge(ktok_ready.sem, ktok_ready.at(s.pair(3)))
                    if s.began(1):
                        act.wait_ge(oT_ready.sem, oT_ready.at(s.pair(1)))
                    run(k_tok[:, :, :], MB[:, T:2 * T].rearrange("p (t x) -> p t x", t=NT),
                        ACT.Copy).then_inc(ktok_copied.sem, 1)
                exps(s, 2)
                if s.has(0):
                    pv_copy(s, 0)
                if s.has(2):
                    act.wait_ge(qk_ready.sem, qk_ready.at(s.batch(2)))
                    if s.began(1):
                        act.wait_ge(stack_landed.sem, stack_landed.at(s.batch(1)))
                    for n in range(2):
                        last = run(hl[:, 2 * n, :], MA[:, n * T:(n + 1) * T], ACT.Identity,
                                   bias=cut["b_qk"][:, n:n + 1])
                    last.then_inc(hi_ready.sem, 1)
                if s.has_pair(4):
                    j = s.pair(4)
                    act.wait_ge(p2qk_ready.sem, p2qk_ready.at(j))
                    if s.began(2):
                        act.wait_ge(phi_ready.sem, phi_ready.at(s.pair(2)))
                    both = MC[:, :].rearrange("p (n x) -> p n x", n=2)
                    run(ex_qk[:, :, :], both, ACT.Exp)
                    run(re_qk[:, :, :], both, ACT.Relu).then_inc(phi_parts.sem, 1)
                if s.has_pair(3):
                    act.wait_ge(oT_ready.sem, oT_ready.at(s.pair(3)))
                    if s.began(1):
                        act.wait_ge(p5_ready.sem, p5_ready.at(s.pair(1)))
                    run(oT[:, :], MB[:, T:2 * T], ACT.Copy).then_inc(oT_copied.sem, 1)
                if s.has(-1):
                    act.wait_ge(topi_ready.sem, topi_ready.at(s.batch(-1)))
                    if s.began(-2):
                        act.wait_ge(gsel_ready.sem, gsel_ready.at(s.batch(-2)))
                        act.wait_ge(gsum_ready.sem, gsum_ready.at(s.batch(-2)))
                    run(ge[:, :, :], lgd[:, :, :], ACT.Exp).then_inc(ge_ready.sem, 1)
                exps(s, 3)
                if s.has(1):
                    act.wait_ge(mT_ready.sem, mT_ready.at(s.batch(1)))
                    if s.began(0):
                        act.wait_ge(m_landed.sem, m_landed.at(s.batch(0)))
                    run(m_hl[:, 0, :], MC[0:H, 0:T], ACT.Copy).then_inc(mhi_ready.sem, 1)
                if s.has(0):
                    pv_copy(s, 1)
                if s.has_pair(4):
                    act.wait_ge(phi_ready.sem, phi_ready.at(s.pair(4)))
                    if s.began(2):
                        act.wait_ge(lin_ready.sem, lin_ready.at(s.pair(2)))
                    for n in range(2):
                        rows = slice(HID * n, HID * (n + 1))
                        last = run(q_z[rows, n, :], q_f[rows, :], ACT.Copy)
                    last.then_inc(q_split.sem, 1)
                if s.has(0):
                    act.wait_ge(c2_ready.sem, c2_ready.at(s.batch(0)))
                    if s.began(-1):
                        act.wait_ge(c3_ready.sem, c3_ready.at(s.batch(-1)))
                    run(ctxT[:, :], PV[:, 0:T], ACT.Copy).then_inc(ctxT_ready.sem, 1)

            steps(act, step)

        @block.vector
        def _(dve):
            vec = nc.vector
            dve.wait_ge(loaded.sem, loaded.at(0))
            vec.tensor_copy(ident_b[:, :], ident)
            vec.tensor_scalar(neg_ident[:, :], ident, -1.0, None, ALU.mult)
            vec.tensor_copy(above_b[:, :], cut["above"])
            vec.memset(ones_r[:, :].bitcast(F32), 1.0)
            vec.memset(ones_f[:, :], 1.0)
            vec.memset(ones_row[:, :], 1.0)
            vec.memset(q_z[:, :, :], 0.0)
            vec.memset(eb_st[:, :].bitcast(F32), 0.0)
            for i in range(2):
                vec.memset(q_st[i][:, :].bitcast(F32), 0.0)
            vec.memset(k_st[0][:, :].bitcast(F32), 0.0).then_inc(setup_v.sem, 1)
            dve.wait_ge(setup_v.sem, setup_v.at(0, 1))
            vec.tensor_copy(eb_st[0:1, :], eb_row[:, :]).then_inc(setup_v.sem, 1)
            dve.wait_ge(setup_v.sem, setup_v.at(0, 2))
            vec.tensor_tensor(eb_st[32:33, :], eb_row[:, :], eb_st[0:1, :].bitcast(F32),
                              ALU.subtract).then_inc(setup_v.sem, 1)
            dve.wait_ge(setup_v.sem, setup_v.at(0, 3))
            dve.wait_ge(setup_p.sem, setup_p.at(0))
            vec.memset(ones_f[:, :], 1.0).then_inc(setup_done.sem, 1)

            def maxima(s, c):
                if not s.has(1):
                    return
                b = s.batch(1)
                if c == 0 and s.began(0):
                    dve.wait_ge(mT_ready.sem, mT_ready.at(s.batch(0)))
                for n in range(3):
                    dve.wait_ge(a_ready.sem, a_ready.at(b, 3 * c + n + 1))
                    vec.tensor_reduce(mx[:, n, G * c:G * (c + 1)],
                                      SA[(3 * c + n) % 2][:, :].rearrange("p (g x) -> p g x", g=G),
                                      AX.X, ALU.max).then_inc(a_used.sem, 1)

            def stats(src, st, mv, st_ready, mv_ready, index, n):
                for t in range(n):
                    last = vec.bn_stats(st[:, t, :], src(t))
                last.then_inc(st_ready.sem, 1)
                count = dve.to_reg(st_ready.at(index))
                dve.wait_ge(st_ready.sem, 1)
                dve.wait_ge(st_ready.sem, count)
                for t in range(n):
                    last = vec.bn_aggr(mv[:, t, :], st[:, t, :])
                last.then_inc(mv_ready.sem, 1)

            def normed(dst, src, mv, rs, n):
                for t in range(n):
                    last = vec.tensor_scalar(dst(t), src(t), mv[:, t, 0:1], rs[:, t:t + 1],
                                             ALU.subtract, ALU.mult)
                return last

            def combine(s, n, banks):
                b = s.batch(-1)
                for e in range(4 * n, 4 * n + 4):
                    for t in range(NT):
                        if e % 4 == 0:
                            dve.wait_ge(ex_ready.sem, ex_ready.at(b, NT * n + t + 1))
                        if e > 0:
                            dve.wait_ge(acc_ready.sem, acc_ready.at(b, NT * (e - 1) + t + 1))
                        before = x1[:, t, :] if e == 0 else acc[:, t, (e - 1) % 2, :]
                        vec.scalar_tensor_tensor(acc[:, t, e % 2, :], banks[t][:, (e % 4) * D:(e % 4 + 1) * D],
                                                 gate[:, t, e:e + 1], before,
                                                 ALU.mult, ALU.add).then_inc(acc_ready.sem, 1)

            def step(s):
                if s.has(-1):
                    b = s.batch(-1)
                    dve.wait_ge(c3_ready.sem, c3_ready.at(b))
                    dve.wait_ge(xb_ready.sem, xb_ready.at(b))
                    vec.tensor_tensor(u2[:, :, :], MC[:, 0:T].rearrange("p (t d) -> p t d", t=NT),
                                      xb_out[s.slot(-1, 2)][:, :, :], ALU.add).then_inc(u2_ready.sem, 1)
                    dve.wait_ge(u2_ready.sem, u2_ready.at(b))
                    if s.began(-2):
                        dve.wait_ge(ve1_ready.sem, ve1_ready.at(s.batch(-2)))
                    stats(lambda t: u2[:, t, :], st1, mv1, st1_ready, mv1_ready, b, NT)
                maxima(s, 0)
                if s.has_pair(3):
                    j = s.pair(3)
                    if s.began(1):
                        dve.wait_ge(oT_ready.sem, oT_ready.at(s.pair(1)))
                    for n in range(2):
                        dve.wait_ge(lin_ready.sem, lin_ready.at(j, n + 1))
                        vec.tensor_tensor(lin_sc[n][:, :], (MB, MC)[n][:, 0:TRI],
                                          cut["causal"], ALU.mult).then_inc(lin_masked.sem, 1)
                if s.has(-1):
                    dve.wait_ge(rs1_ready.sem, rs1_ready.at(b))
                    if s.began(-2):
                        dve.wait_ge(n1w_ready.sem, n1w_ready.at(s.batch(-2)))
                    normed(lambda t: n1[:, t, :], lambda t: u2[:, t, :], mv1, rs1, NT).then_inc(n1_ready.sem, 1)
                if s.has(-2):
                    b = s.batch(-2)
                    dve.wait_ge(z3_ready.sem, z3_ready.at(b))
                    stats(lambda t: z3[:, t, :], st3, mv3, st3_ready, mv3_ready, b, NT)
                maxima(s, 1)
                if s.has(-2):
                    b = s.batch(-2)
                    dve.wait_ge(rs3_ready.sem, rs3_ready.at(b))
                    if s.began(-3):
                        dve.wait_ge(stored.sem, stored.at(s.batch(-3)))
                    normed(lambda t: y[:, t, :], lambda t: z3[:, t, :], mv3, rs3, NT).then_inc(y_ready.sem, 1)
                maxima(s, 2)
                if s.has(-1):
                    b = s.batch(-1)
                    dve.wait_ge(gl_ready.sem, gl_ready.at(b))
                    vec.tensor_tensor(lg[:, :, :], MB[:, 0:NT * E].rearrange("p (t e) -> p t e", t=NT),
                                      cut["b_gate"].unsqueeze(1).to_broadcast([P, NT, E]),
                                      ALU.add).then_inc(lg_ready.sem, 1)
                    count = dve.to_reg(lg_ready.at(b))
                    dve.wait_ge(lg_ready.sem, 1)
                    dve.wait_ge(lg_ready.sem, count)
                    for t in range(NT):
                        last = vec.max(top[:, t, :], lg[:, t, :])
                    last.then_inc(top_ready.sem, 1)
                    count = dve.to_reg(top_ready.at(b))
                    dve.wait_ge(top_ready.sem, 1)
                    dve.wait_ge(top_ready.sem, count)
                    if s.began(-2):
                        count = dve.to_reg(hit_ready.at(s.batch(-2), 1))
                        dve.wait_ge(hit_ready.sem, 1)
                        dve.wait_ge(hit_ready.sem, count)
                    for t in range(NT):
                        last = vec.max_index(topi[:, t, :], top[:, t, :], lg[:, t, :])
                    last.then_inc(topi_ready.sem, 1)
                    vec.tensor_tensor(lgd[:, :, :], lg[:, :, :], top[:, :, 0:1].to_broadcast([P, NT, E]),
                                      ALU.subtract).then_inc(topi_ready.sem, 1)
                    dve.wait_ge(topi_ready.sem, topi_ready.at(b, 1))
                    if s.began(-2):
                        dve.wait_ge(hit_ready.sem, hit_ready.at(s.batch(-2), 2))
                    vec.tensor_copy(topf[:, :, :], topi[:, :, :]).then_inc(hit_ready.sem, 1)
                    dve.wait_ge(hit_ready.sem, hit_ready.at(b, 1))
                    if s.began(-2):
                        dve.wait_ge(sel_ready.sem, sel_ready.at(s.batch(-2)))
                    for r in range(2):
                        last = vec.tensor_tensor(hit[:, r, :, :],
                                                 cut["iota"].unsqueeze(1).to_broadcast([P, NT, E]),
                                                 topf[:, :, r:r + 1].to_broadcast([P, NT, E]), ALU.is_equal)
                    last.then_inc(hit_ready.sem, 1)
                if s.has(2):
                    dve.wait_ge(hi_ready.sem, hi_ready.at(s.batch(2)))
                    for n in range(2):
                        last = vec.scalar_tensor_tensor(
                            hl[:, 2 * n + 1, :], MA[:, n * T:(n + 1) * T], cut["b_qk"][:, n:n + 1],
                            hl[:, 2 * n, :].bitcast(F32), ALU.add, ALU.subtract)
                    last.then_inc(lo_ready.sem, 1)
                if s.has_pair(3):
                    j = s.pair(3)
                    dve.wait_ge(den_ready.sem, den_ready.at(j))
                    vec.tensor_scalar(den[:, :], MC[:, 0:4], 1e-6, None, ALU.max).then_inc(den_max.sem, 1)
                    dve.wait_ge(den_max.sem, den_max.at(j))
                    vec.reciprocal(den_inv[:, :], den[:, :]).then_inc(den_done.sem, 1)
                maxima(s, 3)
                if s.has(1):
                    dve.wait_ge(a_used.sem, a_used.at(s.batch(1)))
                    vec.tensor_tensor(m_tok[:, :], mx[:, 1, :], mx[:, 2, :], ALU.max).then_inc(m_ready.sem, 1)
                if s.has(-1):
                    dve.wait_ge(ge_ready.sem, ge_ready.at(b))
                    vec.tensor_reduce(gsum[:, :], ge[:, :, :], AX.X, ALU.add).then_inc(gsum_ready.sem, 1)
                    dve.wait_ge(gsum_ready.sem, gsum_ready.at(b))
                    vec.reciprocal(ginv[:, :], gsum[:, :]).then_inc(ginv_ready.sem, 1)
                    dve.wait_ge(ginv_ready.sem, ginv_ready.at(b))
                    dve.wait_ge(gsel_ready.sem, gsel_ready.at(b))
                    vec.tensor_tensor(gate[:, :, :], gsel[:, :, :], ginv[:, :].unsqueeze(2).to_broadcast([P, NT, E]),
                                      ALU.mult).then_inc(gate_ready.sem, 1)
                    dve.wait_ge(gate_ready.sem, gate_ready.at(b))
                    combine(s, 0, SA)
                if s.has(1):
                    dve.wait_ge(mhi_ready.sem, mhi_ready.at(s.batch(1)))
                    vec.tensor_tensor(m_hl[:, 1, :], MC[0:H, 0:T], m_hl[:, 0, :].bitcast(F32),
                                      ALU.subtract).then_inc(mlo_ready.sem, 1)
                if s.has_pair(4):
                    j = s.pair(4)
                    dve.wait_ge(phi_parts.sem, phi_parts.at(j))
                    if s.began(2):
                        dve.wait_ge(ktok_ready.sem, ktok_ready.at(s.pair(2)))
                        dve.wait_ge(z_ready.sem, z_ready.at(s.pair(2)))
                        dve.wait_ge(q_split.sem, q_split.at(s.pair(2)))
                        dve.wait_ge(qz_ready.sem, qz_ready.at(s.pair(2)))
                    vec.scalar_tensor_tensor(q_f[:, :], ex_qk[:, 0, :], 1.0, re_qk[:, 0, :], ALU.min, ALU.add)
                    vec.scalar_tensor_tensor(kT[:, :], ex_qk[:, 1, :], 1.0, re_qk[:, 1, :],
                                             ALU.min, ALU.add).then_inc(phi_ready.sem, 1)
                if s.has(-1):
                    combine(s, 1, SB)
                if s.has(0):
                    b = s.batch(0)
                    for t in range(NT):
                        by_head = (PV, MC)[t][:, :].rearrange("p (h w) -> p h w", w=VW)
                        dve.wait_ge(c1_ready.sem, c1_ready.at(b, t + 1))
                        vec.reciprocal(rd[:, t, :].unsqueeze(2), by_head[:, :, HD:HD + 1]).then_inc(c1_inv.sem, 1)
                        dve.wait_ge(c1_inv.sem, c1_inv.at(b, t + 1))
                        if t == 0 and s.began(-1):
                            dve.wait_ge(c2_ready.sem, c2_ready.at(s.batch(-1)))
                        vec.tensor_tensor(ctx_t[:, t, :].rearrange("p (h d) -> p h d", d=HD), by_head[:, :, 0:HD],
                                          rd[:, t, :].unsqueeze(2).to_broadcast([P, H, HD]),
                                          ALU.mult).then_inc(ctx_ready.sem, 1)
                if s.has(2):
                    b = s.batch(2)
                    dve.wait_ge(v_ready.sem, v_ready.at(b))
                    if s.began(0):
                        dve.wait_ge(pv_ready.sem, pv_ready.at(s.batch(0)))
                    vec.tensor_tensor(v_aug[s.slot(2, 2)][:, :, :, 0:HD],
                                      MA[:, 0:T].rearrange("p (t h d) -> p t h d", t=NT, d=HD),
                                      cut["b_v"].rearrange("p (h d) -> p h d", d=HD).unsqueeze(1)
                                      .to_broadcast([P, NT, H, HD]), ALU.add).then_inc(v_stored.sem, 1)
                if s.has(-1):
                    b = s.batch(-1)
                    dve.wait_ge(acc_ready.sem, acc_ready.at(b))
                    if s.began(-2):
                        dve.wait_ge(ve2_ready.sem, ve2_ready.at(s.batch(-2)))
                    stats(lambda t: acc[:, t, 1, :], st2, mv2, st2_ready, mv2_ready, b, NT)
                if s.has_pair(4):
                    j = s.pair(4)
                    dve.wait_ge(phi_ready.sem, phi_ready.at(j))
                    vec.tensor_tensor_scan(zT[:, :], ones_f[:, :], kT[:, :], 0.0,
                                           ALU.mult, ALU.add).then_inc(z_ready.sem, 1)
                if s.has_pair(3):
                    j, slot = s.pair(3), s.pair_slot(3)
                    dve.wait_ge(p5_ready.sem, p5_ready.at(j))
                    dve.wait_ge(den_done.sem, den_done.at(j))
                    for n in range(2):
                        for t in range(NT):
                            last = vec.scalar_tensor_tensor(
                                u_lin[:, NT * n + t, :], MB[:, (2 * t + n) * D:(2 * t + n + 1) * D],
                                den_inv[:, 2 * t + n:2 * t + n + 1], x_in[slot][:, NT * n + t, :],
                                ALU.mult, ALU.add)
                    last.then_inc(u_ready.sem, 1)
                    dve.wait_ge(u_ready.sem, u_ready.at(j))
                    stats(lambda t: u_lin[:, t, :], st_p, mv_p, stp_ready, mvp_ready, j, 2 * NT)
                if s.has(-1):
                    dve.wait_ge(rs2_ready.sem, rs2_ready.at(b))
                    if s.began(-2):
                        dve.wait_ge(n2w_ready.sem, n2w_ready.at(s.batch(-2)))
                    normed(lambda t: n2[:, t, :], lambda t: acc[:, t, 1, :], mv2, rs2, NT).then_inc(n2_ready.sem, 1)
                if s.has_pair(3):
                    dve.wait_ge(rsp_ready.sem, rsp_ready.at(j))
                    if s.began(0):
                        dve.wait_ge(xb_ready.sem, xb_ready.at(s.batch(0)))
                        dve.wait_ge(q1_ready.sem, q1_ready.at(s.batch(0)))
                        dve.wait_ge(rot_ready.sem, rot_ready.at(s.batch(0)))
                    first = s.slot(3, 4)
                    normed(lambda t: xh[:, first + t // NT, t % NT, :], lambda t: u_lin[:, t, :],
                           mv_p, rs_p, 2 * NT).then_inc(xh_ready.sem, 1)

            steps(dve, step)

        @block.gpsimd
        def _(pool):
            gp = nc.gpsimd
            gp.memset(half_neg[:, :], -0.5)
            gp.memset(eps_t[:, :], EPS)
            gp.memset(k_st[1][:, :].bitcast(F32), 0.0)
            for i in range(2):
                gp.memset(v_aug[i][:, :, :, :], 0.0).then_inc(setup_q.sem, 1)
            pool.wait_ge(setup_q.sem, setup_q.at(0))
            for i in range(2):
                last = gp.memset(v_aug[i][:, :, :, HD:HD + 1], 1.0)
            last.then_inc(setup_p.sem, 1)
            pool.wait_ge(setup_done.sem, setup_done.at(0))

            def inverse_root(mv, ve, rs, n, mv_ready, ve_ready, rs_ready, index):
                pool.wait_ge(mv_ready.sem, mv_ready.at(index))
                gp.tensor_tensor(ve[:, 0:n].unsqueeze(2), mv[:, 0:n, 1:2],
                                 eps_t[:, 0:n].unsqueeze(2), ALU.add).then_inc(ve_ready.sem, 1)
                pool.wait_ge(ve_ready.sem, ve_ready.at(index))
                gp.tensor_tensor(rs[:, 0:n], ve[:, 0:n], half_neg[:, 0:n], ALU.pow).then_inc(rs_ready.sem, 1)

            def causal(s, c):
                if not s.has(0):
                    return
                count = pool.to_reg(b_used.at(s.batch(0), 3 * c + 3))
                pool.wait_ge(b_used.sem, 1)
                pool.wait_ge(b_used.sem, count)
                blocks = probs[c % 2][:, 0:2, :, :].rearrange("p k g x -> p (k g) x")
                gp.affine_select(out=blocks, in_=blocks, compare_op=ALU.is_ge, fill=0.0, base=0,
                                 pattern=[[0, 2 * G], [1, P]], channel_multiplier=-1).then_inc(masked.sem, 1)

            def over_tiles(name):
                return cut[name].unsqueeze(1).to_broadcast([P, NT, D])

            def step(s):
                if s.has(-1):
                    inverse_root(mv1, ve1, rs1, NT, mv1_ready, ve1_ready, rs1_ready, s.batch(-1))
                if s.has(2):
                    b, i = s.batch(2), s.slot(2, 2)
                    pool.wait_ge(xh_ready.sem, xh_ready.at(s.pair(2) if s.has_pair(2) else s.pair(1)))
                    if s.began(1):
                        pool.wait_ge(rot_ready.sem, rot_ready.at(s.batch(1)))
                    if s.began(0):
                        pool.wait_ge(q1_ready.sem, q1_ready.at(s.batch(0)))
                    x = xh[:, s.slot(2, 4), :, :]
                    pairs = x.rearrange("p t (m two) -> p (t m) two", two=2)
                    sin = cut["rope_sin"].rearrange("p (m two) -> p m two", two=2)
                    turned = rot_t[:, :, :].rearrange("p t (m two) -> p (t m) two", two=2)
                    gp.tensor_tensor(rot_c[:, :, :], x, cut["rope_cos"].rearrange("p (t d) -> p t d", t=NT),
                                     ALU.mult)
                    gp.tensor_tensor(turned[:, :, 0:1], pairs[:, :, 1:2], sin[:, :, 0:1], ALU.mult)
                    gp.tensor_tensor(turned[:, :, 1:2], pairs[:, :, 0:1], sin[:, :, 1:2],
                                     ALU.mult).then_inc(rot_ready.sem, 1)
                    pool.wait_ge(rot_ready.sem, rot_ready.at(b, 1))
                    gp.tensor_tensor(q_in[i][:, :, :], rot_c[:, :, :], rot_t[:, :, :],
                                     ALU.add).then_inc(rot_ready.sem, 1)
                causal(s, 0)
                if s.has(-1):
                    b = s.batch(-1)
                    pool.wait_ge(n1_ready.sem, n1_ready.at(b))
                    gp.tensor_tensor(n1w[:, :, :], n1[:, :, :], over_tiles("ln1_w"),
                                     ALU.mult).then_inc(n1w_ready.sem, 1)
                    pool.wait_ge(n1w_ready.sem, n1w_ready.at(b))
                    if s.began(-2):
                        pool.wait_ge(acc_ready.sem, acc_ready.at(s.batch(-2)))
                    gp.tensor_tensor(x1[:, :, :], n1w[:, :, :], over_tiles("ln1_b"),
                                     ALU.add).then_inc(x1_ready.sem, 1)
                if s.has(-2):
                    inverse_root(mv3, ve3, rs3, NT, mv3_ready, ve3_ready, rs3_ready, s.batch(-2))
                causal(s, 1)
                if s.has_pair(3):
                    j = s.pair(3)
                    pool.wait_ge(z_ready.sem, z_ready.at(j))
                    if s.began(1):
                        pool.wait_ge(den_ready.sem, den_ready.at(s.pair(1)))
                    gp.tensor_tensor(qzT[:, :], q_f[:, :], zT[:, :], ALU.mult).then_inc(qz_ready.sem, 1)
                if s.has(0):
                    i = s.slot(0, 2)
                    pool.wait_ge(xh_ready.sem, xh_ready.at(s.pair(0) if s.has_pair(0) else s.pair(-1)))
                    if s.began(-2):
                        pool.wait_ge(u2_ready.sem, u2_ready.at(s.batch(-2)))
                    x = xh[:, s.slot(0, 4), :, :]
                    gp.tensor_tensor(xb_out[i][:, :, :], x, over_tiles("b_out"), ALU.add)
                    gp.tensor_tensor(xb_ln2[i][:, :, :], x, over_tiles("ln2_b"), ALU.add).then_inc(xb_ready.sem, 1)
                causal(s, 2)
                if s.has(-1):
                    b = s.batch(-1)
                    pool.wait_ge(hit_ready.sem, hit_ready.at(b, 2))
                    if s.began(-2):
                        pool.wait_ge(gsel_ready.sem, gsel_ready.at(s.batch(-2)))
                    gp.tensor_tensor(sel[:, :, :], hit[:, 0, :, :], hit[:, 1, :, :],
                                     ALU.add).then_inc(sel_ready.sem, 1)
                    pool.wait_ge(sel_ready.sem, sel_ready.at(b))
                    pool.wait_ge(ge_ready.sem, ge_ready.at(b))
                    if s.began(-2):
                        pool.wait_ge(gate_ready.sem, gate_ready.at(s.batch(-2)))
                    gp.tensor_tensor(gsel[:, :, :], ge[:, :, :], sel[:, :, :], ALU.mult).then_inc(gsel_ready.sem, 1)
                causal(s, 3)
                if s.has(-1):
                    inverse_root(mv2, ve2, rs2, NT, mv2_ready, ve2_ready, rs2_ready, b)
                if s.has_pair(3):
                    inverse_root(mv_p, ve_p, rs_p, 2 * NT, mvp_ready, vep_ready, rsp_ready, s.pair(3))
                if s.has(-1):
                    pool.wait_ge(n2_ready.sem, n2_ready.at(b))
                    gp.tensor_tensor(n2w[:, :, :], n2[:, :, :], over_tiles("ln2_w"),
                                     ALU.mult).then_inc(n2w_ready.sem, 1)
                    pool.wait_ge(n2w_ready.sem, n2w_ready.at(b))
                    if s.began(-2):
                        pool.wait_ge(y_ready.sem, y_ready.at(s.batch(-2)))
                    gp.tensor_tensor(z3[:, :, :], n2w[:, :, :], xb_ln2[s.slot(-1, 2)][:, :, :],
                                     ALU.add).then_inc(z3_ready.sem, 1)

            steps(pool, step)


def kernel(L0_attn_x, L0_attn_W_q, L0_attn_W_k, L0_attn_W_v, L0_attn_W_o, L0_ffn_in_proj_w, L0_ffn_in_proj_b,
           L0_ffn_out_proj_w, L0_ffn_out_proj_b, L0_ffn_gate_w, L0_ffn_gate_b, L0_ffn_expert_w,
           L0_ffn_expert_b, L0_ffn_ln1_w, L0_ffn_ln1_b, L0_ffn_ln2_w, L0_ffn_ln2_b):
    import numpy as np
    import concourse.bacc as bacc
    from concourse.bass_utils import run_bass_kernel_spmd

    f = np.float32
    arr = np.asarray
    tri = np.triu(np.ones((P, P), f))
    inv_freq = (f(1.0) / np.power(f(10000.0), np.arange(0, HD, 2, dtype=f) / f(HD))).astype(f)
    angle = np.arange(T, dtype=f)[:, None] * inv_freq[None, :]
    cos = np.repeat(np.cos(angle), 2, axis=1)
    sin = np.stack([-np.sin(angle), np.sin(angle)], axis=-1).reshape(T, HD)

    def by_tile(a):
        return np.tile(a, (1, H)).reshape(NT, P, D).transpose(1, 0, 2).reshape(P, NT * D)

    halves = np.zeros((P, 2), f)
    halves[:HID, 0] = 1
    halves[HID:, 1] = 1

    def rows(v):
        return np.broadcast_to(arr(v)[None, :], (P, arr(v).shape[0]))

    def head_last(a):
        return a.reshape((H, HD) + a.shape[1:]).swapaxes(0, 1).reshape(a.shape)

    wi, bi = arr(L0_ffn_in_proj_w), arr(L0_ffn_in_proj_b)
    wo = arr(L0_attn_W_o)
    none = np.zeros_like(wo)
    parts = {
        "ident": np.eye(P, dtype=f),
        "w_lin": np.concatenate([arr(L0_attn_W_q), arr(L0_attn_W_k), arr(L0_attn_W_v)], axis=1),
        "w_lin_out": np.block([[wo, none], [none, wo]]),
        "w_qk": np.concatenate([head_last(wi[0:D]).T, head_last(wi[D:2 * D]).T], axis=1),
        "w_v": wi[2 * D:].T,
        "w_out": arr(L0_ffn_out_proj_w).T,
        "w_gate": arr(L0_ffn_gate_w).T,
        "w_expert": arr(L0_ffn_expert_w).transpose(2, 0, 1).reshape(D, E * D),
        "b_v": rows(bi[2 * D:]),
        "b_out": rows(L0_ffn_out_proj_b),
        "b_gate": rows(L0_ffn_gate_b),
        "b_qk": np.stack([head_last(bi[0:D]), head_last(bi[D:2 * D])], axis=1),
        "ln1_w": rows(L0_ffn_ln1_w), "ln1_b": rows(L0_ffn_ln1_b),
        "ln2_w": rows(L0_ffn_ln2_w), "ln2_b": rows(L0_ffn_ln2_b),
        "rope_cos": by_tile(cos), "rope_sin": by_tile(sin),
        "causal": np.concatenate([tri, np.ones((P, P), f), tri], axis=1),
        "above": np.tile(np.triu(np.full((P, P), -1e30, f), 1), (1, G)),
        "halves": halves,
        "iota": rows(np.arange(E, dtype=f)),
    }
    packed = np.ascontiguousarray(np.concatenate([parts[n] for n in PACK], axis=1))
    arrays = {"x": np.ascontiguousarray(arr(L0_attn_x)), "params": packed,
              "expert_b": np.ascontiguousarray(arr(L0_ffn_expert_b).reshape(1, E * D))}

    nc = bacc.Bacc("TRN2", target_bir_lowering=False, num_devices=1)
    args = [nc.dram_tensor(n, a.shape, F32, kind="ExternalInput").ap() for n, a in arrays.items()]
    out = nc.dram_tensor("out", (NB, T, D), F32, kind="ExternalOutput").ap()
    build(nc, *args, out)
    result = run_bass_kernel_spmd(nc, [arrays], core_ids=[0])
    return result.results[0]["out"]
```

```python
from contextlib import ExitStack

import concourse.bass as bass
from concourse import mybir

ALU = mybir.AluOpType
ACT = mybir.ActivationFunctionType
F32 = mybir.dt.float32
F32R = mybir.dt.float32r
BF16 = mybir.dt.bfloat16
U32 = mybir.dt.uint32
AX = mybir.AxisListType

P = 128
NB, T, D = 32, 256, 128
HID = 64
NPAIR = NB // 2
NT = T // P
H, HD = 16, 8
G = 4
NG = H // G
VW = 32
E = 8
EPS = 1e-5
SCALE = HD ** -0.5
UNITS = 3 * NG
TRI = T + P
ROWS_HI, ROWS_MID, ROWS_LO = 0, 8, 64
ROW_MAX = 126
NSTACK = 6

FIRST, LOOP_FROM, LOOP_TO, LAST = -6, 3, 23, NB + 1
UNROLL = 4

PACK = {}
_at = 0
for _name, _width in (
    ("ident", P), ("w_lin", 3 * HID), ("b_v", D), ("w_out", D), ("b_out", D),
    ("w_lin_out", 2 * D), ("w_qk", 2 * D), ("w_v", D),
    ("w_gate", E), ("w_expert", E * D), ("b_gate", E), ("b_qk", 2),
    ("ln1_w", D), ("ln1_b", D), ("ln2_w", D), ("ln2_b", D), ("rope_cos", NT * D), ("rope_sin", NT * D),
    ("causal", TRI), ("above", G * P), ("halves", 2), ("iota", E),
):
    PACK[_name] = (_at, _width)
    _at += _width
PACK_W = _at
PACK_FIRST = PACK["w_lin_out"][0]


class Step:

    def __init__(self, first, loop=None):
        self.first, self.loop = first, loop

    def batch(self, k):
        return self.first + k if self.loop is None else self.loop * UNROLL + (self.first + k)

    def pair(self, k):
        n = (self.first + k) // 2
        return n if self.loop is None else self.loop * (UNROLL // 2) + n

    def has(self, k):
        return self.loop is not None or 0 <= self.first + k < NB

    def has_pair(self, k):
        even = (self.first + k) % 2 == 0
        return even and (self.loop is not None or 0 <= self.first + k < NB)

    def began(self, k):
        return self.loop is not None or self.first + k >= 0

    def slot(self, k, ring):
        return (self.first + k) % ring

    def pair_slot(self, k):
        return (self.first + k) // 2 % 2

    def pair_round(self, k):
        n = (self.first + k) // 2 // 2
        return n if self.loop is None else self.loop * (UNROLL // 4) + n


def steps(eng, step):
    for s in range(FIRST, LOOP_FROM):
        step(Step(s))
    with eng.Fori(0, (LOOP_TO - LOOP_FROM) // UNROLL) as loop:
        for s in range(LOOP_FROM, LOOP_FROM + UNROLL):
            step(Step(s, loop))
    for s in range(LOOP_TO, LAST + 1):
        step(Step(s))


class Signal:

    def __init__(self, sem, per, count, by):
        self.sem, self.per, self.count, self.by = sem, per, count, by

    def at(self, index, nth=None):
        nth = self.per if nth is None else nth
        if isinstance(index, int) and index >= self.count:
            index, nth = self.count - 1, self.per
        return (index * self.per + nth) * self.by


def build(nc, x_d, pack_d, eb_d, out_d):
    x_v = x_d.rearrange("(j b) (t p) d -> j p (b t) d", b=2, p=P)
    out_v = out_d.rearrange("b (t p) d -> b p t d", p=P)

    with ExitStack() as ctx:
        def sb(name, shape, dt=F32):
            return ctx.enter_context(nc.sbuf_tensor(name, shape, dt))

        def signal(name, per=1, count=NB, by=1):
            return Signal(ctx.enter_context(nc.semaphore(name)), per, count, by)

        pack = sb("pack", [P, PACK_W])
        cut = {n: pack[:, a:a + w] for n, (a, w) in PACK.items()}
        ident = cut["ident"]
        w_lin = cut["w_lin"]
        w_expert = cut["w_expert"]
        ident_b = sb("ident_b", [P, P], BF16)
        neg_ident = sb("neg_ident", [P, P])
        above_b = sb("above_b", [P, G * P], BF16)
        eb_row = sb("eb_row", [1, E * D])
        eb_st = sb("eb_st", [P, E * D], F32R)
        ones_r = sb("ones_r", [P, P], F32R)
        ones_f = sb("ones_f", [P, T])
        ones_row = sb("ones_row", [2, H * T])
        half_neg = sb("half_neg", [P, 2 * NT])
        minus_one = sb("minus_one", [P, 2 * NT])
        eps_t = sb("eps_t", [P, 2 * NT])
        bvT = sb("bvT", [P, P])
        b_out_v = sb("b_out_v", [P, D])

        x_in = [sb(f"x_in{i}", [P, 2 * NT, D]) for i in range(2)]
        xT = sb("xT", [P, 2 * T])
        ex_qk = sb("ex_qk", [P, 2, T])
        re_qk = sb("re_qk", [P, 2, T])
        q_f = sb("q_f", [P, T])
        q_z = sb("q_z", [P, 2, T])
        kT = sb("kT", [P, T])
        vT = sb("vT", [P, T])
        zT = sb("zT", [P, T])
        qzT = sb("qzT", [P, T])
        lin_sc = [sb(f"lin_sc{i}", [P, TRI]) for i in range(2)]
        k_tok = sb("k_tok", [P, NT, P])
        oT = sb("oT", [P, T])
        den = sb("den", [P, 4])
        den_inv = sb("den_inv", [P, 4])
        u_lin = sb("u_lin", [P, 2 * NT, D])
        st_p = sb("st_p", [P, 2 * NT, 6])
        mv_p = sb("mv_p", [P, 2 * NT, 2])
        ve_p = sb("ve_p", [P, 2 * NT])
        rs_p = sb("rs_p", [P, 2 * NT])
        sh_p = sb("sh_p", [P, 2 * NT])
        xh = sb("xh", [P, 4, NT, D])

        q_in = [sb(f"q_in{i}", [P, NT, D]) for i in range(2)]
        xqT = sb("xqT", [P, 2, T])
        rot_c = sb("rot_c", [P, NT, D])
        rot_t = sb("rot_t", [P, NT, D])
        hl = sb("hl", [P, 4, T], F32R)
        q_st = [sb(f"q_st{i}", [P, H * T], F32R) for i in range(2)]
        k_st = [sb(f"k_st{i}", [P, H * T], F32R) for i in range(2)]
        v_aug = [sb(f"v_aug{i}", [P, NT, H, VW]) for i in range(2)]
        xb_out = [sb(f"xb_out{i}", [P, NT, D]) for i in range(2)]
        xb_ln2 = [sb(f"xb_ln2{i}", [P, NT, D]) for i in range(2)]

        mx = sb("mx", [P, NT, H])
        m_hl = sb("m_hl", [H, 2, T], F32R)
        probs = [sb(f"probs{i}", [P, 3, G, P]) for i in range(2)]
        ctx_a = sb("ctx_a", [P, NG, T])

        rd = sb("rd", [P, NT, H])
        ctx_t = sb("ctx_t", [P, NT, D])
        ctxT = sb("ctxT", [P, T])
        u2 = sb("u2", [P, NT, D])
        st1 = sb("st1", [P, NT, 6])
        mv1 = sb("mv1", [P, NT, 2])
        ve1 = sb("ve1", [P, NT])
        rs1 = sb("rs1", [P, NT])
        n1 = sb("n1", [P, NT, D])
        n1w = sb("n1w", [P, NT, D])
        x1 = sb("x1", [P, NT, D])
        x1_hl = sb("x1_hl", [P, 2, T], F32R)
        w_hl = sb("w_hl", [P, 2, E * D], F32R)
        lg = sb("lg", [P, NT, E])
        top = sb("top", [P, NT, 8])
        topi = sb("topi", [P, NT, 8], U32)
        topf = sb("topf", [P, NT, 8])
        lgd = sb("lgd", [P, NT, E])
        ge = sb("ge", [P, NT, E])
        gsum = sb("gsum", [P, NT])
        ginv = sb("ginv", [P, NT])
        hit = sb("hit", [P, 2, NT, E])
        sel = sb("sel", [P, NT, E])
        gsel = sb("gsel", [P, NT, E])
        gate = sb("gate", [P, NT, E])
        acc = sb("acc", [P, NT, 2, D])
        st2 = sb("st2", [P, NT, 6])
        mv2 = sb("mv2", [P, NT, 2])
        ve2 = sb("ve2", [P, NT])
        rs2 = sb("rs2", [P, NT])
        sh2 = sb("sh2", [P, NT])
        n2 = sb("n2", [P, NT, D])
        n2w = sb("n2w", [P, NT, D])
        z3 = sb("z3", [P, NT, D])
        st3 = sb("st3", [P, NT, 6])
        mv3 = sb("mv3", [P, NT, 2])
        ve3 = sb("ve3", [P, NT])
        rs3 = sb("rs3", [P, NT])
        sh3 = sb("sh3", [P, NT])
        y = sb("y", [P, NT, D])

        bank = [ctx.enter_context(nc.psum_tensor(f"bank{i}", [P, 512], F32)) for i in range(8)]
        SA, SB, PV, MA, MB, MC = bank[0:2], bank[2:4], bank[4], bank[5], bank[6], bank[7]

        loaded_first = signal("loaded_first", 1, 1, 16)
        loaded = signal("loaded", 2, 1, 16)
        setup_v = signal("setup_v", 5, 1)
        setup_done = signal("setup_done", 1, 1)
        setup_q = signal("setup_q", 1, 1)
        zeroed = signal("zeroed", 2, 1)
        bv_ready = signal("bv_ready", 1, 1)
        bvT_ready = signal("bvT_ready", 1, 1)
        bv_out_ready = signal("bv_out_ready", 1, 1)
        b_out_ready = signal("b_out_ready", 1, 1)
        ones_landed = signal("ones_landed", 2, 1, 16)
        x_landed = [signal(f"x_landed{i}", 1, NPAIR // 2, 16) for i in range(2)]
        p1_ready = signal("p1_ready", 1, NPAIR)
        xT_ready = signal("xT_ready", 1, NPAIR)
        p2v_ready = signal("p2v_ready", 1, NPAIR)
        p2qk_ready = signal("p2qk_ready", 1, NPAIR)
        vT_ready = signal("vT_ready", 1, NPAIR)
        phi_parts = signal("phi_parts", 1, NPAIR)
        phi_ready = signal("phi_ready", 1, NPAIR)
        q_split = signal("q_split", 1, NPAIR)
        z_ready = signal("z_ready", 1, NPAIR)
        qz_ready = signal("qz_ready", 1, NPAIR)
        lin_ready = signal("lin_ready", 2, NPAIR)
        lin_masked = signal("lin_masked", 2, NPAIR)
        ktok_ready = signal("ktok_ready", 1, NPAIR)
        ktok_copied = signal("ktok_copied", 1, NPAIR)
        oT_ready = signal("oT_ready", 1, NPAIR)
        oT_copied = signal("oT_copied", 1, NPAIR)
        den_ready = signal("den_ready", 1, NPAIR)
        den_max = signal("den_max", 1, NPAIR)
        den_done = signal("den_done", 1, NPAIR)
        p5_ready = signal("p5_ready", 1, NPAIR)
        u_ready = signal("u_ready", 1, NPAIR)
        stp_ready = signal("stp_ready", 1, NPAIR)
        mvp_ready = signal("mvp_ready", 1, NPAIR)
        vep_ready = signal("vep_ready", 1, NPAIR)
        rsp_ready = signal("rsp_ready", 2, NPAIR)
        xh_ready = signal("xh_ready", 2, NPAIR)

        rot_ready = signal("rot_ready", 2)
        xb_ready = signal("xb_ready")
        q1_ready = signal("q1_ready")
        xqT_ready = signal("xqT_ready")
        v_ready = signal("v_ready")
        v_stored = signal("v_stored")
        qk_ready = signal("qk_ready")
        hi_ready = signal("hi_ready")
        lo_ready = signal("lo_ready")
        stack_landed = signal("stack_landed", NSTACK, NB, 16)
        a_ready = signal("a_ready", UNITS)
        a_used = signal("a_used", UNITS)
        mT_ready = signal("mT_ready")
        mhi_ready = signal("mhi_ready")
        mlo_ready = signal("mlo_ready")
        m_landed = signal("m_landed", 2, NB, 16)
        b_ready = signal("b_ready", UNITS)
        b_used = signal("b_used", UNITS)
        masked = signal("masked", NG)
        pv_ready = signal("pv_ready", NG)
        pv_copied = signal("pv_copied", 2)

        c1_ready = signal("c1_ready", NT)
        c1_inv = signal("c1_inv", NT)
        ctx_ready = signal("ctx_ready", NT)
        c2_ready = signal("c2_ready")
        ctxT_ready = signal("ctxT_ready")
        c3_ready = signal("c3_ready")
        u2_ready = signal("u2_ready")
        st1_ready = signal("st1_ready")
        mv1_ready = signal("mv1_ready")
        ve1_ready = signal("ve1_ready")
        rs1_ready = signal("rs1_ready")
        n1_ready = signal("n1_ready")
        n1w_ready = signal("n1w_ready")
        x1_ready = signal("x1_ready")
        c4_ready = signal("c4_ready")
        x1_hi_ready = signal("x1_hi_ready")
        x1_lo_ready = signal("x1_lo_ready")
        gl_ready = signal("gl_ready")
        lg_ready = signal("lg_ready")
        top_ready = signal("top_ready")
        topi_ready = signal("topi_ready", 2)
        ge_ready = signal("ge_ready")
        hit_ready = signal("hit_ready", 2)
        sel_ready = signal("sel_ready")
        gsel_ready = signal("gsel_ready")
        gsum_ready = signal("gsum_ready")
        ginv_ready = signal("ginv_ready")
        gate_ready = signal("gate_ready")
        ex_ready = signal("ex_ready", 2 * NT)
        acc_ready = [signal(f"acc_ready{t}", E) for t in range(NT)]
        st2_ready = signal("st2_ready")
        mv2_ready = signal("mv2_ready")
        ve2_ready = signal("ve2_ready")
        rs2_ready = signal("rs2_ready", 2)
        n2_ready = signal("n2_ready")
        n2w_ready = signal("n2w_ready")
        z3_ready = signal("z3_ready")
        st3_ready = signal("st3_ready")
        mv3_ready = signal("mv3_ready")
        ve3_ready = signal("ve3_ready")
        rs3_ready = signal("rs3_ready", 2)
        y_ready = signal("y_ready")
        stored = signal("stored", 1, NB, 16)

        block = ctx.enter_context(nc.Block())

        @block.sync
        def _(sp):
            sp.dma_start(pack[:, 0:PACK_FIRST], pack_d[:, 0:PACK_FIRST]).then_inc(loaded_first.sem, 16)

            def step(s):
                if s.first == FIRST + 1:
                    sp.dma_start(pack[:, PACK_FIRST:], pack_d[:, PACK_FIRST:]).then_inc(loaded.sem, 16)
                    sp.dma_start(eb_row[:, :], eb_d).then_inc(loaded.sem, 16)
                if s.first == -2 and s.loop is None:
                    sp.wait_ge(zeroed.sem, zeroed.at(0))
                    sp.wait_ge(setup_done.sem, setup_done.at(0))
                    for i in range(2):
                        sp.dma_start(k_st[i][ROW_MAX:ROW_MAX + 2, :].bitcast(F32),
                                     ones_row[:, :]).then_inc(ones_landed.sem, 16)
                if s.has_pair(6):
                    slot = s.pair_slot(6)
                    if s.began(2):
                        sp.wait_ge(u_ready.sem, u_ready.at(s.pair(2)))
                    sp.dma_start(x_in[slot][:, :, :], x_v[s.pair(6), :, :, :]).then_inc(x_landed[slot].sem, 16)
                if s.has(2):
                    i = s.slot(2, 2)
                    if s.began(0):
                        count = sp.to_reg(b_ready.at(s.batch(0)))
                        sp.wait_ge(b_ready.sem, 1)
                        sp.wait_ge(b_ready.sem, count)
                    sp.wait_ge(hi_ready.sem, hi_ready.at(s.batch(2)))
                    for stack, part, row in ((q_st, 0, ROWS_HI), (k_st, 2, ROWS_HI), (q_st, 0, ROWS_MID),
                                             (k_st, 2, ROWS_LO)):
                        sp.dma_start(stack[i][row:row + HD, :].bitcast(F32),
                                     hl[:, part, :].bitcast(F32)).then_inc(stack_landed.sem, 16)
                    sp.wait_ge(lo_ready.sem, lo_ready.at(s.batch(2)))
                    for stack, part, row in ((k_st, 3, ROWS_MID), (q_st, 1, ROWS_LO)):
                        sp.dma_start(stack[i][row:row + HD, :].bitcast(F32),
                                     hl[:, part, :].bitcast(F32)).then_inc(stack_landed.sem, 16)
                if s.has(1):
                    sp.wait_ge(mlo_ready.sem, mlo_ready.at(s.batch(1)))
                    for r in range(2):
                        sp.dma_start(q_st[s.slot(1, 2)][ROW_MAX + r:ROW_MAX + r + 1, :].bitcast(F32),
                                     m_hl[:, r, :].bitcast(F32)).then_inc(m_landed.sem, 16)
                if s.has(-2):
                    sp.wait_ge(y_ready.sem, y_ready.at(s.batch(-2)))
                    sp.dma_start(out_v[s.batch(-2), :, :, :], y[:, :, :]).then_inc(stored.sem, 16)

            steps(sp, step)
            sp.wait_ge(stored.sem, stored.at(NB - 1))

        @block.tensor
        def _(pe):
            pe.wait_ge(loaded_first.sem, loaded_first.at(0))
            mm = nc.tensor.matmul
            nc.tensor.transpose(MA[:, 0:P], cut["b_v"], ident).then_inc(bv_ready.sem, 1)
            pe.wait_ge(bvT_ready.sem, bvT_ready.at(0))
            mm(MB[:, 0:D], bvT[:, :], cut["w_out"], start=True, stop=True).then_inc(bv_out_ready.sem, 1)
            pe.wait_ge(b_out_ready.sem, b_out_ready.at(0))

            def a_unit(s, c, n):
                i, bank_ = s.slot(1, 2), SA[(3 * c + n) % 2]
                if n == 0 and c == 0:
                    pe.wait_ge(stack_landed.sem, stack_landed.at(s.batch(1)))
                if 3 * c + n < 2:
                    if s.began(-2):
                        pe.wait_ge(acc_ready[n].sem, acc_ready[n].at(s.batch(-2), E // 2))
                    if s.began(0):
                        pe.wait_ge(a_used.sem, a_used.at(s.batch(0), UNITS - 1 + n))
                else:
                    pe.wait_ge(a_used.sem, a_used.at(s.batch(1), 3 * c + n - 1))
                if n == 0:
                    mm(bank_[:, :], ident_b[:, :], above_b[:, :], start=True, stop=False)
                    for g in range(G):
                        h = G * c + g
                        last = mm(bank_[:, g * P:(g + 1) * P], q_st[i][0:ROW_MAX, h * T:h * T + P],
                                  k_st[i][0:ROW_MAX, h * T:h * T + P], start=False, stop=g == G - 1)
                else:
                    for g in (2 * n - 2, 2 * n - 1):
                        h = G * c + g
                        mm(bank_[:, (g % 2) * T:(g % 2 + 1) * T], q_st[i][0:ROW_MAX, h * T + P:(h + 1) * T],
                           k_st[i][0:ROW_MAX, h * T:(h + 1) * T], start=g % 2 == 0, stop=False)
                    own = bank_[:, :].rearrange("p (g t x) -> p g t x", g=2, t=NT)[:, :, 1, :]
                    last = mm(own, ident_b[:, :], above_b[:, 0:2 * P].rearrange("p (g x) -> p g x", g=2),
                              start=False, stop=True)
                last.then_inc(a_ready.sem, 1)

            def b_unit(s, c, n):
                i, bank_ = s.slot(0, 2), SB[(3 * c + n) % 2]
                if n == 0 and c == 0:
                    if s.first == 0:
                        pe.wait_ge(ones_landed.sem, ones_landed.at(0))
                    pe.wait_ge(m_landed.sem, m_landed.at(s.batch(0)))
                if 3 * c + n < 2:
                    if s.began(-2):
                        pe.wait_ge(acc_ready[n].sem, acc_ready[n].at(s.batch(-2)))
                    if s.began(-1):
                        pe.wait_ge(b_used.sem, b_used.at(s.batch(-1), UNITS - 1 + n))
                else:
                    pe.wait_ge(b_used.sem, b_used.at(s.batch(0), 3 * c + n - 1))
                if n < 2:
                    for g in (2 * n, 2 * n + 1):
                        h = G * c + g
                        last = mm(bank_[:, (g % 2) * T:(g % 2 + 1) * T], k_st[i][:, h * T:h * T + P],
                                  q_st[i][:, h * T:(h + 1) * T], start=True, stop=True)
                else:
                    for g in range(G):
                        h = G * c + g
                        last = mm(bank_[:, g * P:(g + 1) * P], k_st[i][:, h * T + P:(h + 1) * T],
                                  q_st[i][:, h * T + P:(h + 1) * T], start=True, stop=True)
                last.then_inc(b_ready.sem, 1)

            def ab(s, c, n):
                if s.has(1):
                    a_unit(s, c, n)
                if s.has(0):
                    b_unit(s, c, n)

            def pv(s, c):
                if not s.has(0):
                    return
                b, i, col = s.batch(0), s.slot(0, 2), (c % 2) * T
                pe.wait_ge(masked.sem, masked.at(b, c + 1))
                if c >= 2:
                    pe.wait_ge(pv_copied.sem, pv_copied.at(b, 1))
                elif s.began(-1):
                    pe.wait_ge(ctxT_ready.sem, ctxT_ready.at(s.batch(-1)))
                for g in range(G):
                    h, rows = G * c + g, slice(VW * g, VW * (g + 1))
                    mm(PV[rows, col:col + T], v_aug[i][:, 0, h, :], probs[c % 2][:, 0:3:2, g, :],
                       start=True, stop=False)
                    last = mm(PV[rows, col + P:col + T], v_aug[i][:, 1, h, :], probs[c % 2][:, 1, g, :],
                              start=False, stop=True)
                last.then_inc(pv_ready.sem, 1)

            def inputs(s):
                if s.has(2):
                    b = s.batch(2)
                    pe.wait_ge(rot_ready.sem, rot_ready.at(b))
                    if s.began(1):
                        pe.wait_ge(v_stored.sem, v_stored.at(s.batch(1)))
                    if s.began(-1):
                        pe.wait_ge(x1_lo_ready.sem, x1_lo_ready.at(s.batch(-1)))
                    for t in range(NT):
                        nc.tensor.transpose(MA[:, t * P:(t + 1) * P], xh[:, s.slot(2, 4), t, :], ident)
                    for t in range(NT):
                        last = nc.tensor.transpose(MA[:, T + t * P:T + (t + 1) * P],
                                                   q_in[s.slot(2, 2)][:, t, :], ident)
                    last.then_inc(q1_ready.sem, 1)

            def queries_keys(s):
                if s.has(2):
                    pe.wait_ge(xqT_ready.sem, xqT_ready.at(s.batch(2)))
                    for n in range(2):
                        last = mm(MA[:, n * T:(n + 1) * T], cut["w_qk"][:, n * D:(n + 1) * D],
                                  xqT[:, 1, :], start=True, stop=True)
                    last.then_inc(qk_ready.sem, 1)

            def values(s):
                if s.has(2):
                    b = s.batch(2)
                    pe.wait_ge(lo_ready.sem, lo_ready.at(b))
                    for t in range(NT):
                        last = mm(MA[:, t * D:(t + 1) * D], xqT[:, 0, t * P:(t + 1) * P], cut["w_v"],
                                  start=True, stop=True)
                    last.then_inc(v_ready.sem, 1)

            def by_token(s, t, bank_):
                for c in range(NG):
                    last = nc.tensor.transpose(bank_[:, c * P:(c + 1) * P],
                                               ctx_a[:, c, t * P:(t + 1) * P], ident)
                last.then_inc(c1_ready.sem, 1)

            def experts(s, n, t, bank_):
                cols = slice(4 * n * D, 4 * (n + 1) * D)
                mm(bank_[:, :], ones_r[:, :], eb_st[:, cols], start=True, stop=False)
                for part, w_part in ((0, 0), (1, 0), (0, 1)):
                    last = mm(bank_[:, :], x1_hl[:, part, t * P:(t + 1) * P], w_hl[:, w_part, cols],
                              start=False, stop=(part, w_part) == (0, 1))
                last.then_inc(ex_ready.sem, 1)

            def step(s):
                if s.first == -3 and s.loop is None:
                    pe.wait_ge(setup_done.sem, setup_done.at(0))
                if s.has(-1):
                    pe.wait_ge(ctxT_ready.sem, ctxT_ready.at(s.batch(-1)))
                    pe.wait_ge(ctx_ready.sem, ctx_ready.at(s.batch(-1)))
                    for t in range(NT):
                        last = mm(MC[:, t * D:(t + 1) * D], ctxT[:, t * P:(t + 1) * P], cut["w_out"],
                                  start=True, stop=True)
                    last.then_inc(c3_ready.sem, 1)
                ab(s, 0, 0)
                ab(s, 0, 1)
                if s.has_pair(4):
                    j, slot = s.pair(4), s.pair_slot(4)
                    pe.wait_ge(x_landed[slot].sem, x_landed[slot].at(s.pair_round(4)))
                    if s.began(2):
                        pe.wait_ge(den_max.sem, den_max.at(s.pair(2)))
                    if s.began(-1):
                        pe.wait_ge(u2_ready.sem, u2_ready.at(s.batch(-1)))
                    if s.began(0):
                        pe.wait_ge(mlo_ready.sem, mlo_ready.at(s.batch(0)))
                    for n in range(2 * NT):
                        last = nc.tensor.transpose(MC[:, n * P:(n + 1) * P], x_in[slot][:, n, :], ident)
                    last.then_inc(p1_ready.sem, 1)
                ab(s, 0, 2)
                if s.has_pair(3):
                    j = s.pair(3)
                    pe.wait_ge(q_split.sem, q_split.at(j))
                    pe.wait_ge(vT_ready.sem, vT_ready.at(j))
                    pe.wait_ge(phi_parts.sem, phi_parts.at(j))
                    if s.began(-1):
                        pe.wait_ge(u2_ready.sem, u2_ready.at(s.batch(-1)))
                    if s.began(0):
                        pe.wait_ge(mlo_ready.sem, mlo_ready.at(s.batch(0)))
                    for n in range(2):
                        bank_ = (MB, MC)[n]
                        mm(bank_[:, 0:T], vT[:, 0:P], q_z[:, n, :], start=True, stop=True)
                        mm(bank_[:, T:TRI], vT[:, P:T], q_z[:, n, P:T],
                           start=True, stop=True).then_inc(lin_ready.sem, 1)
                ab(s, 1, 0)
                ab(s, 1, 1)
                ab(s, 1, 2)
                pv(s, 0)
                if s.has_pair(4):
                    j = s.pair(4)
                    pe.wait_ge(xT_ready.sem, xT_ready.at(j))
                    if s.began(2):
                        pe.wait_ge(u_ready.sem, u_ready.at(s.pair(2)))
                    for n in range(2):
                        last = mm(MB[HID * n:HID * (n + 1), T:2 * T], w_lin[:, 2 * HID:3 * HID],
                                  xT[:, n * T:(n + 1) * T], start=True, stop=True)
                    last.then_inc(p2v_ready.sem, 1)
                if s.has_pair(3):
                    j = s.pair(3)
                    pe.wait_ge(lin_masked.sem, lin_masked.at(j, 1))
                    for t in range(NT):
                        last = nc.tensor.transpose(MB[:, T + t * P:T + (t + 1) * P],
                                                   kT[:, t * P:(t + 1) * P], ident)
                    last.then_inc(ktok_ready.sem, 1)
                ab(s, 2, 0)
                if s.has(-1):
                    b = s.batch(-1)
                    pe.wait_ge(x1_ready.sem, x1_ready.at(b))
                    if s.began(1):
                        pe.wait_ge(v_stored.sem, v_stored.at(s.batch(1)))
                    for t in range(NT):
                        last = nc.tensor.transpose(MA[:, t * P:(t + 1) * P], x1[:, t, :], ident)
                    last.then_inc(c4_ready.sem, 1)
                ab(s, 2, 1)
                ab(s, 2, 2)
                if s.has(-1):
                    pe.wait_ge(x1_lo_ready.sem, x1_lo_ready.at(s.batch(-1)))
                    if s.has_pair(4):
                        pe.wait_ge(vT_ready.sem, vT_ready.at(s.pair(4)))
                    if s.has_pair(3):
                        pe.wait_ge(ktok_copied.sem, ktok_copied.at(s.pair(3)))
                    if s.began(2):
                        pe.wait_ge(u_ready.sem, u_ready.at(s.pair(2) if s.has_pair(2) else s.pair(1)))
                    for t in range(NT):
                        for part in range(2):
                            last = mm(MB[:, t * E:(t + 1) * E], x1_hl[:, part, t * P:(t + 1) * P].bitcast(F32),
                                      cut["w_gate"], start=part == 0, stop=part == 1)
                    last.then_inc(gl_ready.sem, 1)
                pv(s, 1)
                if s.first % 2 == 1:
                    inputs(s)
                if s.has_pair(4):
                    for part in range(2):
                        for n in range(2):
                            last = mm(MC[HID * n:HID * (n + 1), part * T:(part + 1) * T],
                                      w_lin[:, part * HID:(part + 1) * HID], xT[:, n * T:(n + 1) * T],
                                      start=True, stop=True)
                    last.then_inc(p2qk_ready.sem, 1)
                ab(s, 3, 0)
                if s.has_pair(3):
                    j = s.pair(3)
                    pe.wait_ge(ktok_copied.sem, ktok_copied.at(j))
                    if s.began(-1):
                        pe.wait_ge(lg_ready.sem, lg_ready.at(s.batch(-1)))
                    pe.wait_ge(lin_masked.sem, lin_masked.at(j))
                    for n in range(2):
                        rows = slice(HID * n, HID * (n + 1))
                        mm(MB[rows, T:2 * T], k_tok[:, 0, rows], lin_sc[n][:, 0:T], start=True, stop=False)
                        last = mm(MB[rows, T + P:2 * T], k_tok[:, 1, rows], lin_sc[n][:, T:TRI],
                                  start=False, stop=True)
                    last.then_inc(oT_ready.sem, 1)
                    pe.wait_ge(qz_ready.sem, qz_ready.at(j))
                    for t in range(NT):
                        last = mm(MC[:, 2 * t:2 * t + 2], qzT[:, t * P:(t + 1) * P], cut["halves"],
                                  start=True, stop=True)
                    last.then_inc(den_ready.sem, 1)
                ab(s, 3, 1)
                ab(s, 3, 2)
                if s.first % 2 == 0:
                    inputs(s)
                pv(s, 2)
                if s.first % 2 == 1:
                    queries_keys(s)
                if s.has(-1):
                    pe.wait_ge(a_used.sem, a_used.at(s.batch(1)))
                    experts(s, 0, 0, SA[0])
                if s.first % 2 == 0:
                    queries_keys(s)
                if s.has(-1):
                    experts(s, 0, 1, SA[1])
                if s.has(1):
                    b = s.batch(1)
                    pe.wait_ge(a_used.sem, a_used.at(b))
                    if s.has_pair(4):
                        pe.wait_ge(phi_parts.sem, phi_parts.at(s.pair(4)))
                    if s.has_pair(3):
                        pe.wait_ge(den_max.sem, den_max.at(s.pair(3)))
                    if s.began(-1):
                        pe.wait_ge(u2_ready.sem, u2_ready.at(s.batch(-1)))
                    mm(MC[0:H, 0:P], mx[:, 0, :], neg_ident[:, :], start=True, stop=True)
                    mm(MC[0:H, P:T], mx[:, 1, :], neg_ident[:, :],
                       start=True, stop=True).then_inc(mT_ready.sem, 1)
                pv(s, 3)
                if s.has(-1):
                    pe.wait_ge(b_used.sem, b_used.at(s.batch(0)))
                    experts(s, 1, 0, SB[0])
                if s.has(0):
                    pe.wait_ge(pv_copied.sem, pv_copied.at(s.batch(0)))
                    by_token(s, 0, PV)
                if s.has(-1):
                    experts(s, 1, 1, SB[1])
                if s.has(0):
                    if s.has(1):
                        pe.wait_ge(mlo_ready.sem, mlo_ready.at(s.batch(1)))
                    else:
                        pe.wait_ge(u2_ready.sem, u2_ready.at(s.batch(-1)))
                    by_token(s, 1, MC)
                if s.has_pair(3):
                    j = s.pair(3)
                    pe.wait_ge(oT_copied.sem, oT_copied.at(j))
                    for t in range(NT):
                        last = mm(MB[:, t * 2 * D:(t + 1) * 2 * D], oT[:, t * P:(t + 1) * P],
                                  cut["w_lin_out"], start=True, stop=True)
                    last.then_inc(p5_ready.sem, 1)
                if s.first % 2 == 0:
                    values(s)
                if s.has(0):
                    b = s.batch(0)
                    pe.wait_ge(ctx_ready.sem, ctx_ready.at(b))
                    for t in range(NT):
                        last = nc.tensor.transpose(PV[:, t * P:(t + 1) * P], ctx_t[:, t, :], ident)
                    last.then_inc(c2_ready.sem, 1)
                if s.first % 2 == 1:
                    values(s)

            steps(pe, step)

        @block.scalar
        def _(act):
            run = nc.scalar.activation
            act.wait_ge(bv_ready.sem, bv_ready.at(0))
            run(bvT[:, :], MA[:, 0:P], ACT.Copy).then_inc(bvT_ready.sem, 1)

            def exps(s, c, n):
                if not s.has(0):
                    return
                b = s.batch(0)
                if n == 0 and c >= 2:
                    act.wait_ge(pv_ready.sem, pv_ready.at(b, c - 1))
                elif n == 0 and s.began(-1):
                    act.wait_ge(pv_ready.sem, pv_ready.at(s.batch(-1), c + 3))
                act.wait_ge(b_ready.sem, b_ready.at(b, 3 * c + n + 1))
                src = SB[(3 * c + n) % 2][:, :]
                if n < 2:
                    src = src.rearrange("p (g t x) -> p t g x", t=NT, x=P)
                    dst = probs[c % 2][:, 0:3:2, 2 * n:2 * n + 2, :]
                else:
                    src = src.rearrange("p (g x) -> p g x", x=P)
                    dst = probs[c % 2][:, 1, :, :]
                run(dst, src, ACT.Exp, scale=SCALE).then_inc(b_used.sem, 1)

            def pv_copy(s, half_):
                act.wait_ge(pv_ready.sem, pv_ready.at(s.batch(0), 2 * half_ + 2))
                if half_ == 0 and s.began(-1):
                    act.wait_ge(c1_ready.sem, c1_ready.at(s.batch(-1)))
                run(ctx_a[:, 2 * half_:2 * half_ + 2, :],
                    PV[:, :].rearrange("p (c x) -> p c x", c=2), ACT.Copy).then_inc(pv_copied.sem, 1)

            def inputs(s):
                if s.has(2):
                    act.wait_ge(q1_ready.sem, q1_ready.at(s.batch(2)))
                    if s.began(1):
                        act.wait_ge(v_ready.sem, v_ready.at(s.batch(1)))
                    run(xqT[:, :, :], MA[:, :].rearrange("p (n x) -> p n x", n=2),
                        ACT.Copy).then_inc(xqT_ready.sem, 1)

            def values(s):
                if s.has(2):
                    act.wait_ge(v_ready.sem, v_ready.at(s.batch(2)))
                    if s.began(0):
                        act.wait_ge(pv_ready.sem, pv_ready.at(s.batch(0)))
                    run(v_aug[s.slot(2, 2)][:, :, :, 0:HD],
                        MA[:, 0:T].rearrange("p (t h d) -> p t h d", t=NT, d=HD),
                        ACT.Copy).then_inc(v_stored.sem, 1)

            def normed(dst, src, rs, shift, n):
                for t in range(n):
                    last = run(dst(t), src(t), ACT.Identity, scale=rs[:, t:t + 1], bias=shift[:, t:t + 1])
                return last

            def step(s):
                exps(s, 0, 0)
                exps(s, 0, 1)
                exps(s, 0, 2)
                if s.has_pair(4):
                    act.wait_ge(p1_ready.sem, p1_ready.at(s.pair(4)))
                    if s.began(2):
                        act.wait_ge(p2qk_ready.sem, p2qk_ready.at(s.pair(2)))
                    run(xT[:, :], MC[:, :], ACT.Copy).then_inc(xT_ready.sem, 1)
                exps(s, 1, 0)
                exps(s, 1, 1)
                exps(s, 1, 2)
                if s.has_pair(4):
                    act.wait_ge(p2v_ready.sem, p2v_ready.at(s.pair(4)))
                    if s.began(2):
                        act.wait_ge(lin_ready.sem, lin_ready.at(s.pair(2)))
                    run(vT[:, :], MB[:, T:2 * T], ACT.Copy).then_inc(vT_ready.sem, 1)
                if s.has_pair(3):
                    act.wait_ge(ktok_ready.sem, ktok_ready.at(s.pair(3)))
                    if s.began(1):
                        act.wait_ge(oT_ready.sem, oT_ready.at(s.pair(1)))
                    run(k_tok[:, :, :], MB[:, T:2 * T].rearrange("p (t x) -> p t x", t=NT),
                        ACT.Copy).then_inc(ktok_copied.sem, 1)
                if s.has(-1):
                    act.wait_ge(c4_ready.sem, c4_ready.at(s.batch(-1)))
                    if s.began(-2):
                        act.wait_ge(ex_ready.sem, ex_ready.at(s.batch(-2)))
                    run(x1_hl[:, 0, :], MA[:, 0:T], ACT.Copy).then_inc(x1_hi_ready.sem, 1)
                exps(s, 2, 0)
                exps(s, 2, 1)
                exps(s, 2, 2)
                if s.has(-2):
                    b = s.batch(-2)
                    act.wait_ge(rs2_ready.sem, rs2_ready.at(b))
                    if s.began(-3):
                        act.wait_ge(n2w_ready.sem, n2w_ready.at(s.batch(-3)))
                    normed(lambda t: n2[:, t, :], lambda t: acc[:, t, 1, :], rs2, sh2,
                           NT).then_inc(n2_ready.sem, 1)
                if s.has_pair(2):
                    j = s.pair(2)
                    act.wait_ge(rsp_ready.sem, rsp_ready.at(j))
                    if s.began(-1):
                        act.wait_ge(xb_ready.sem, xb_ready.at(s.batch(-1)))
                        act.wait_ge(q1_ready.sem, q1_ready.at(s.batch(-1)))
                        act.wait_ge(rot_ready.sem, rot_ready.at(s.batch(-1)))
                    first = s.slot(2, 4)
                    normed(lambda t: xh[:, first, t, :], lambda t: u_lin[:, t, :], rs_p, sh_p,
                           NT).then_inc(xh_ready.sem, 1)
                if s.has_pair(2):
                    first = s.slot(2, 4)
                    normed(lambda t: xh[:, first + 1, t, :], lambda t: u_lin[:, NT + t, :], rs_p[:, NT:],
                           sh_p[:, NT:], NT).then_inc(xh_ready.sem, 1)
                if s.has(0):
                    pv_copy(s, 0)
                if s.first % 2 == 1:
                    inputs(s)
                if s.has_pair(3):
                    act.wait_ge(oT_ready.sem, oT_ready.at(s.pair(3)))
                    if s.began(1):
                        act.wait_ge(p5_ready.sem, p5_ready.at(s.pair(1)))
                    run(oT[:, :], MB[:, T:2 * T], ACT.Copy).then_inc(oT_copied.sem, 1)
                if s.has_pair(4):
                    j = s.pair(4)
                    act.wait_ge(p2qk_ready.sem, p2qk_ready.at(j))
                    if s.began(2):
                        act.wait_ge(phi_ready.sem, phi_ready.at(s.pair(2)))
                    both = MC[:, :].rearrange("p (n x) -> p n x", n=2)
                    run(ex_qk[:, :, :], both, ACT.Exp)
                    run(re_qk[:, :, :], both, ACT.Relu).then_inc(phi_parts.sem, 1)
                if s.has(-1):
                    act.wait_ge(topi_ready.sem, topi_ready.at(s.batch(-1)))
                    if s.began(-2):
                        act.wait_ge(gsel_ready.sem, gsel_ready.at(s.batch(-2)))
                        act.wait_ge(gsum_ready.sem, gsum_ready.at(s.batch(-2)))
                    run(ge[:, :, :], lgd[:, :, :], ACT.Exp).then_inc(ge_ready.sem, 1)
                exps(s, 3, 0)
                exps(s, 3, 1)
                exps(s, 3, 2)
                if s.first % 2 == 0:
                    inputs(s)
                if s.has(2):
                    act.wait_ge(qk_ready.sem, qk_ready.at(s.batch(2)))
                    if s.began(1):
                        act.wait_ge(stack_landed.sem, stack_landed.at(s.batch(1)))
                    for n in range(2):
                        last = run(hl[:, 2 * n, :], MA[:, n * T:(n + 1) * T], ACT.Identity,
                                   bias=cut["b_qk"][:, n:n + 1])
                    last.then_inc(hi_ready.sem, 1)
                if s.has(1):
                    act.wait_ge(mT_ready.sem, mT_ready.at(s.batch(1)))
                    if s.began(0):
                        act.wait_ge(m_landed.sem, m_landed.at(s.batch(0)))
                    run(m_hl[:, 0, :], MC[0:H, 0:T], ACT.Copy).then_inc(mhi_ready.sem, 1)
                if s.has(0):
                    pv_copy(s, 1)
                if s.has_pair(4):
                    act.wait_ge(phi_ready.sem, phi_ready.at(s.pair(4)))
                    if s.began(2):
                        act.wait_ge(lin_ready.sem, lin_ready.at(s.pair(2)))
                    if s.first == -4 and s.loop is None:
                        act.wait_ge(setup_done.sem, setup_done.at(0))
                        act.wait_ge(setup_q.sem, setup_q.at(0))
                    for n in range(2):
                        rows = slice(HID * n, HID * (n + 1))
                        last = run(q_z[rows, n, :], q_f[rows, :], ACT.Copy)
                    last.then_inc(q_split.sem, 1)
                if s.first % 2 == 0:
                    values(s)
                if s.has(0):
                    act.wait_ge(c2_ready.sem, c2_ready.at(s.batch(0)))
                    if s.began(-1):
                        act.wait_ge(c3_ready.sem, c3_ready.at(s.batch(-1)))
                    run(ctxT[:, :], PV[:, 0:T], ACT.Copy).then_inc(ctxT_ready.sem, 1)
                if s.has(-2):
                    b = s.batch(-2)
                    act.wait_ge(rs3_ready.sem, rs3_ready.at(b))
                    if s.began(-3):
                        act.wait_ge(stored.sem, stored.at(s.batch(-3)))
                    normed(lambda t: y[:, t, :], lambda t: z3[:, t, :], rs3, sh3,
                           NT).then_inc(y_ready.sem, 1)
                if s.first % 2 == 1:
                    values(s)

            steps(act, step)

        @block.vector
        def _(dve):
            vec = nc.vector
            vec.memset(ones_r[:, :].bitcast(F32), 1.0)
            vec.memset(ones_row[:, :], 1.0)
            vec.memset(q_z[:, :, :], 0.0)
            vec.memset(ones_f[:, :], 1.0)
            vec.memset(eb_st[:, :].bitcast(F32), 0.0).then_inc(setup_v.sem, 1)
            dve.wait_ge(loaded_first.sem, loaded_first.at(0))
            vec.tensor_copy(ident_b[:, :], ident)
            vec.tensor_scalar(neg_ident[:, :], ident, -1.0, None, ALU.mult)
            dve.wait_ge(bv_out_ready.sem, bv_out_ready.at(0))
            vec.tensor_tensor(b_out_v[:, :], MB[:, 0:D], cut["b_out"], ALU.add).then_inc(b_out_ready.sem, 1)
            dve.wait_ge(loaded.sem, loaded.at(0))
            dve.wait_ge(setup_v.sem, setup_v.at(0, 1))
            vec.tensor_copy(above_b[:, :], cut["above"])
            vec.tensor_copy(eb_st[0:1, :], eb_row[:, :]).then_inc(setup_v.sem, 1)
            dve.wait_ge(setup_v.sem, setup_v.at(0, 2))
            vec.tensor_tensor(eb_st[32:33, :], eb_row[:, :], eb_st[0:1, :].bitcast(F32),
                              ALU.subtract).then_inc(setup_v.sem, 1)
            vec.tensor_copy(w_hl[:, 0, :], w_expert).then_inc(setup_v.sem, 1)
            dve.wait_ge(setup_v.sem, setup_v.at(0, 4))
            vec.tensor_tensor(w_hl[:, 1, :], w_expert, w_hl[:, 0, :].bitcast(F32),
                              ALU.subtract).then_inc(setup_v.sem, 1)
            dve.wait_ge(setup_v.sem, setup_v.at(0, 5))
            vec.memset(ones_f[:, :], 1.0).then_inc(setup_done.sem, 1)

            def maxima(s, c, n):
                if not s.has(1):
                    return
                b = s.batch(1)
                if c == 0 and n == 0 and s.began(0):
                    dve.wait_ge(mT_ready.sem, mT_ready.at(s.batch(0)))
                dve.wait_ge(a_ready.sem, a_ready.at(b, 3 * c + n + 1))
                if n == 0:
                    heads, dst = G, mx[:, 0, G * c:G * (c + 1)]
                else:
                    heads, dst = 2, mx[:, 1, G * c + 2 * n - 2:G * c + 2 * n]
                vec.tensor_reduce(dst, SA[(3 * c + n) % 2][:, :].rearrange("p (g x) -> p g x", g=heads),
                                  AX.X, ALU.max).then_inc(a_used.sem, 1)

            def stats(src, st, st_ready, n):
                for t in range(n):
                    last = vec.bn_stats(st[:, t, :], src(t))
                last.then_inc(st_ready.sem, 1)

            def aggregate(st, mv, st_ready, mv_ready, index, n):
                count = st_ready.at(index)
                if not isinstance(index, int):
                    count = dve.to_reg(count)
                    dve.wait_ge(st_ready.sem, 1)
                dve.wait_ge(st_ready.sem, count)
                for t in range(n):
                    last = vec.bn_aggr(mv[:, t, :], st[:, t, :])
                last.then_inc(mv_ready.sem, 1)

            def normed(dst, src, mv, rs, n):
                for t in range(n):
                    last = vec.tensor_scalar(dst(t), src(t), mv[:, t, 0:1], rs[:, t:t + 1],
                                             ALU.subtract, ALU.mult)
                return last

            def combine(s, n, banks, tiles, start=0, stop=4):
                b = s.batch(-1)
                for e in range(4 * n + start, 4 * n + stop):
                    for t in tiles:
                        if e % 4 == 0:
                            dve.wait_ge(ex_ready.sem, ex_ready.at(b, NT * n + t + 1))
                        if e > 0:
                            dve.wait_ge(acc_ready[t].sem, acc_ready[t].at(b, e))
                        before = x1[:, t, :] if e == 0 else acc[:, t, (e - 1) % 2, :]
                        vec.scalar_tensor_tensor(acc[:, t, e % 2, :], banks[t][:, (e % 4) * D:(e % 4 + 1) * D],
                                                 gate[:, t, e:e + 1], before,
                                                 ALU.mult, ALU.add).then_inc(acc_ready[t].sem, 1)

            def rests(s):
                if s.has(2):
                    dve.wait_ge(hi_ready.sem, hi_ready.at(s.batch(2)))
                    for n in range(2):
                        last = vec.scalar_tensor_tensor(
                            hl[:, 2 * n + 1, :], MA[:, n * T:(n + 1) * T], cut["b_qk"][:, n:n + 1],
                            hl[:, 2 * n, :].bitcast(F32), ALU.add, ALU.subtract)
                    last.then_inc(lo_ready.sem, 1)

            def maxima_rest(s):
                if s.has(1):
                    dve.wait_ge(mhi_ready.sem, mhi_ready.at(s.batch(1)))
                    vec.tensor_tensor(m_hl[:, 1, :], MC[0:H, 0:T], m_hl[:, 0, :].bitcast(F32),
                                      ALU.subtract).then_inc(mlo_ready.sem, 1)

            def contexts(s, t):
                if s.has(0):
                    b = s.batch(0)
                    by_head = (PV, MC)[t][:, :].rearrange("p (h w) -> p h w", w=VW)
                    dve.wait_ge(c1_ready.sem, c1_ready.at(b, t + 1))
                    vec.reciprocal(rd[:, t, :].unsqueeze(2), by_head[:, :, HD:HD + 1]).then_inc(c1_inv.sem, 1)
                    dve.wait_ge(c1_inv.sem, c1_inv.at(b, t + 1))
                    if t == 0 and s.began(-1):
                        dve.wait_ge(c2_ready.sem, c2_ready.at(s.batch(-1)))
                    vec.tensor_tensor(ctx_t[:, t, :].rearrange("p (h d) -> p h d", d=HD), by_head[:, :, 0:HD],
                                      rd[:, t, :].unsqueeze(2).to_broadcast([P, H, HD]),
                                      ALU.mult).then_inc(ctx_ready.sem, 1)

            def linear_residual(s, k, n):
                slot = s.pair_slot(k)
                for t in range(NT):
                    last = vec.scalar_tensor_tensor(
                        u_lin[:, NT * n + t, :], MB[:, (2 * t + n) * D:(2 * t + n + 1) * D],
                        den_inv[:, 2 * t + n:2 * t + n + 1], x_in[slot][:, NT * n + t, :],
                        ALU.mult, ALU.add)
                return last

            def step(s):
                if s.has(-1):
                    b = s.batch(-1)
                    dve.wait_ge(c3_ready.sem, c3_ready.at(b))
                    dve.wait_ge(xb_ready.sem, xb_ready.at(b))
                    vec.tensor_tensor(u2[:, :, :], MC[:, 0:T].rearrange("p (t d) -> p t d", t=NT),
                                      xb_out[s.slot(-1, 2)][:, :, :], ALU.add).then_inc(u2_ready.sem, 1)
                maxima(s, 0, 0)
                maxima(s, 0, 1)
                if s.has_pair(2):
                    linear_residual(s, 2, 1).then_inc(u_ready.sem, 1)
                if s.has(-1):
                    b = s.batch(-1)
                    dve.wait_ge(u2_ready.sem, u2_ready.at(b))
                    if s.began(-2):
                        dve.wait_ge(ve1_ready.sem, ve1_ready.at(s.batch(-2)))
                        dve.wait_ge(n1_ready.sem, n1_ready.at(s.batch(-2)))
                    stats(lambda t: u2[:, t, :], st1, st1_ready, NT)
                maxima(s, 0, 2)
                if s.has(-1):
                    b = s.batch(-1)
                    aggregate(st1, mv1, st1_ready, mv1_ready, b, NT)
                if s.has(-2):
                    b = s.batch(-2)
                    for t in range(NT):
                        dve.wait_ge(acc_ready[t].sem, acc_ready[t].at(b))
                    if s.began(-3):
                        dve.wait_ge(rs2_ready.sem, rs2_ready.at(s.batch(-3)))
                    stats(lambda t: acc[:, t, 1, :], st2, st2_ready, NT)
                if s.has_pair(3):
                    j = s.pair(3)
                    if s.began(1):
                        dve.wait_ge(oT_ready.sem, oT_ready.at(s.pair(1)))
                    for n in range(2):
                        dve.wait_ge(lin_ready.sem, lin_ready.at(j, n + 1))
                        vec.tensor_tensor(lin_sc[n][:, :], (MB, MC)[n][:, 0:TRI],
                                          cut["causal"], ALU.mult).then_inc(lin_masked.sem, 1)
                maxima(s, 1, 0)
                if s.has(-2):
                    aggregate(st2, mv2, st2_ready, mv2_ready, s.batch(-2), NT)
                if s.has(-1):
                    b = s.batch(-1)
                    dve.wait_ge(rs1_ready.sem, rs1_ready.at(b))
                    if s.began(-2):
                        dve.wait_ge(n1w_ready.sem, n1w_ready.at(s.batch(-2)))
                    normed(lambda t: n1[:, t, :], lambda t: u2[:, t, :], mv1, rs1, NT).then_inc(n1_ready.sem, 1)
                if s.has_pair(3):
                    j = s.pair(3)
                    dve.wait_ge(phi_ready.sem, phi_ready.at(j))
                    vec.tensor_tensor_scan(zT[:, :], ones_f[:, :], kT[:, :], 0.0,
                                           ALU.mult, ALU.add).then_inc(z_ready.sem, 1)
                maxima(s, 1, 1)
                if s.has_pair(2):
                    j = s.pair(2)
                    dve.wait_ge(u_ready.sem, u_ready.at(j))
                    if s.began(0):
                        dve.wait_ge(rsp_ready.sem, rsp_ready.at(s.pair(0)))
                    stats(lambda t: u_lin[:, t, :], st_p, stp_ready, 2 * NT)
                maxima(s, 1, 2)
                if s.has_pair(2):
                    aggregate(st_p, mv_p, stp_ready, mvp_ready, s.pair(2), 2 * NT)
                maxima(s, 2, 0)
                if s.has(-1):
                    b = s.batch(-1)
                    dve.wait_ge(x1_hi_ready.sem, x1_hi_ready.at(b))
                    vec.tensor_tensor(x1_hl[:, 1, :], MA[:, 0:T], x1_hl[:, 0, :].bitcast(F32),
                                      ALU.subtract).then_inc(x1_lo_ready.sem, 1)
                maxima(s, 2, 1)
                maxima(s, 2, 2)
                if s.has(-1):
                    b = s.batch(-1)
                    dve.wait_ge(gl_ready.sem, gl_ready.at(b))
                    vec.tensor_tensor(lg[:, :, :], MB[:, 0:NT * E].rearrange("p (t e) -> p t e", t=NT),
                                      cut["b_gate"].unsqueeze(1).to_broadcast([P, NT, E]),
                                      ALU.add).then_inc(lg_ready.sem, 1)
                    count = dve.to_reg(lg_ready.at(b))
                    dve.wait_ge(lg_ready.sem, 1)
                    dve.wait_ge(lg_ready.sem, count)
                    for t in range(NT):
                        last = vec.max(top[:, t, :], lg[:, t, :])
                    last.then_inc(top_ready.sem, 1)
                    count = dve.to_reg(top_ready.at(b))
                    dve.wait_ge(top_ready.sem, 1)
                    dve.wait_ge(top_ready.sem, count)
                    if s.began(-2):
                        count = dve.to_reg(hit_ready.at(s.batch(-2), 1))
                        dve.wait_ge(hit_ready.sem, 1)
                        dve.wait_ge(hit_ready.sem, count)
                    for t in range(NT):
                        last = vec.max_index(topi[:, t, :], top[:, t, :], lg[:, t, :])
                    last.then_inc(topi_ready.sem, 1)
                    vec.tensor_tensor(lgd[:, :, :], lg[:, :, :], top[:, :, 0:1].to_broadcast([P, NT, E]),
                                      ALU.subtract).then_inc(topi_ready.sem, 1)
                    dve.wait_ge(topi_ready.sem, topi_ready.at(b, 1))
                    if s.began(-2):
                        dve.wait_ge(hit_ready.sem, hit_ready.at(s.batch(-2), 2))
                    vec.tensor_copy(topf[:, :, :], topi[:, :, :]).then_inc(hit_ready.sem, 1)
                    dve.wait_ge(hit_ready.sem, hit_ready.at(b, 1))
                    if s.began(-2):
                        dve.wait_ge(sel_ready.sem, sel_ready.at(s.batch(-2)))
                    for r in range(2):
                        last = vec.tensor_tensor(hit[:, r, :, :],
                                                 cut["iota"].unsqueeze(1).to_broadcast([P, NT, E]),
                                                 topf[:, :, r:r + 1].to_broadcast([P, NT, E]), ALU.is_equal)
                    last.then_inc(hit_ready.sem, 1)
                maxima(s, 3, 0)
                if s.has_pair(3):
                    j = s.pair(3)
                    dve.wait_ge(den_ready.sem, den_ready.at(j))
                    vec.tensor_scalar(den[:, :], MC[:, 0:4], 1e-6, None, ALU.max).then_inc(den_max.sem, 1)
                    dve.wait_ge(den_max.sem, den_max.at(j))
                    vec.reciprocal(den_inv[:, :], den[:, :]).then_inc(den_done.sem, 1)
                maxima(s, 3, 1)
                if s.has_pair(4):
                    j = s.pair(4)
                    dve.wait_ge(phi_parts.sem, phi_parts.at(j))
                    if s.began(2):
                        dve.wait_ge(ktok_ready.sem, ktok_ready.at(s.pair(2)))
                        dve.wait_ge(z_ready.sem, z_ready.at(s.pair(2)))
                        dve.wait_ge(q_split.sem, q_split.at(s.pair(2)))
                        dve.wait_ge(qz_ready.sem, qz_ready.at(s.pair(2)))
                    vec.scalar_tensor_tensor(q_f[:, :], ex_qk[:, 0, :], 1.0, re_qk[:, 0, :], ALU.min, ALU.add)
                    vec.scalar_tensor_tensor(kT[:, :], ex_qk[:, 1, :], 1.0, re_qk[:, 1, :],
                                             ALU.min, ALU.add).then_inc(phi_ready.sem, 1)
                maxima(s, 3, 2)
                if s.has(-2):
                    dve.wait_ge(z3_ready.sem, z3_ready.at(s.batch(-2)))
                    if s.began(-3):
                        dve.wait_ge(rs3_ready.sem, rs3_ready.at(s.batch(-3)))
                    stats(lambda t: z3[:, t, :], st3, st3_ready, NT)
                if s.has(-1):
                    b = s.batch(-1)
                    dve.wait_ge(ge_ready.sem, ge_ready.at(b))
                    vec.tensor_reduce(gsum[:, :], ge[:, :, :], AX.X, ALU.add).then_inc(gsum_ready.sem, 1)
                    dve.wait_ge(gsum_ready.sem, gsum_ready.at(b))
                    vec.reciprocal(ginv[:, :], gsum[:, :]).then_inc(ginv_ready.sem, 1)
                    dve.wait_ge(ginv_ready.sem, ginv_ready.at(b))
                    dve.wait_ge(gsel_ready.sem, gsel_ready.at(b))
                    vec.tensor_tensor(gate[:, :, :], gsel[:, :, :],
                                      ginv[:, :].unsqueeze(2).to_broadcast([P, NT, E]),
                                      ALU.mult).then_inc(gate_ready.sem, 1)
                if s.has(-2):
                    aggregate(st3, mv3, st3_ready, mv3_ready, s.batch(-2), NT)
                if s.first % 2 == 1:
                    rests(s)
                if s.has(-1):
                    dve.wait_ge(gate_ready.sem, gate_ready.at(s.batch(-1)))
                    if s.began(-2):
                        dve.wait_ge(n2_ready.sem, n2_ready.at(s.batch(-2)))
                    combine(s, 0, SA, [0, 1] if s.first % 2 else [0], 0, 2)
                    if s.first % 2 == 0:
                        combine(s, 0, SA, [0], 2, 4)
                if s.first % 2 == 0:
                    rests(s)
                maxima_rest(s)
                if s.has(-1):
                    combine(s, 0, SA, [0, 1] if s.first % 2 else [1], 2 if s.first % 2 else 0, 4)
                contexts(s, 0)
                if s.has(-1):
                    combine(s, 1, SB, [0], 0, 2)
                contexts(s, 1)
                if s.has(-1):
                    for e in range(2):
                        combine(s, 1, SB, [0], e + 2, e + 3)
                        combine(s, 1, SB, [1], e, e + 1)
                if s.has(-1):
                    combine(s, 1, SB, [1], 2, 4)
                if s.has_pair(3):
                    j = s.pair(3)
                    dve.wait_ge(p5_ready.sem, p5_ready.at(j))
                    if s.began(1):
                        dve.wait_ge(xh_ready.sem, xh_ready.at(s.pair(1)))
                    dve.wait_ge(den_done.sem, den_done.at(j))
                    linear_residual(s, 3, 0)

            steps(dve, step)

        @block.gpsimd
        def _(pool):
            gp = nc.gpsimd
            gp.memset(half_neg[:, :], -0.5)
            gp.memset(minus_one[:, :], -1.0)
            gp.memset(eps_t[:, :], EPS)
            for i in range(2):
                last = gp.memset(v_aug[i][:, :, :, :], 0.0)
            last.then_inc(zeroed.sem, 1)
            pool.wait_ge(zeroed.sem, zeroed.at(0, 1))
            for i in range(2):
                last = gp.memset(v_aug[i][:, :, :, HD:HD + 1], 1.0)
            last.then_inc(setup_q.sem, 1)
            for i in range(2):
                gp.memset(k_st[i][:, :].bitcast(F32), 0.0)
                last = gp.memset(q_st[i][:, :].bitcast(F32), 0.0)
            last.then_inc(zeroed.sem, 1)
            pool.wait_ge(b_out_ready.sem, b_out_ready.at(0))
            pool.wait_ge(zeroed.sem, zeroed.at(0))

            def inverse_root(mv, ve, rs, n, mv_ready, ve_ready, rs_ready, index, shift=None):
                pool.wait_ge(mv_ready.sem, mv_ready.at(index))
                if shift is not None:
                    gp.tensor_tensor(shift[:, 0:n].unsqueeze(2), mv[:, 0:n, 0:1],
                                     minus_one[:, 0:n].unsqueeze(2), ALU.mult)
                gp.tensor_tensor(ve[:, 0:n].unsqueeze(2), mv[:, 0:n, 1:2], eps_t[:, 0:n].unsqueeze(2),
                                 ALU.add).then_inc(ve_ready.sem, 1)
                pool.wait_ge(ve_ready.sem, ve_ready.at(index))
                gp.tensor_tensor(rs[:, 0:n], ve[:, 0:n], half_neg[:, 0:n], ALU.pow).then_inc(rs_ready.sem, 1)
                if shift is not None:
                    pool.wait_ge(rs_ready.sem, rs_ready.at(index, 1))
                    gp.tensor_tensor(shift[:, 0:n], shift[:, 0:n], rs[:, 0:n],
                                     ALU.mult).then_inc(rs_ready.sem, 1)

            def causal(s, c):
                if not s.has(0):
                    return
                count = pool.to_reg(b_used.at(s.batch(0), 3 * c + 3))
                pool.wait_ge(b_used.sem, 1)
                pool.wait_ge(b_used.sem, count)
                blocks = probs[c % 2][:, 0:2, :, :].rearrange("p k g x -> p (k g) x")
                gp.affine_select(out=blocks, in_=blocks, compare_op=ALU.is_ge, fill=0.0, base=0,
                                 pattern=[[0, 2 * G], [1, P]], channel_multiplier=-1).then_inc(masked.sem, 1)

            def over_tiles(name):
                return cut[name].unsqueeze(1).to_broadcast([P, NT, D])

            def rotary(s):
                if s.has(2):
                    b, i = s.batch(2), s.slot(2, 2)
                    if s.has_pair(2):
                        pool.wait_ge(xh_ready.sem, xh_ready.at(s.pair(2), 1))
                    else:
                        pool.wait_ge(xh_ready.sem, xh_ready.at(s.pair(1)))
                    if s.began(1):
                        pool.wait_ge(rot_ready.sem, rot_ready.at(s.batch(1)))
                    if s.began(0):
                        pool.wait_ge(q1_ready.sem, q1_ready.at(s.batch(0)))
                    x = xh[:, s.slot(2, 4), :, :]
                    pairs = x.rearrange("p t (m two) -> p (t m) two", two=2)
                    sin = cut["rope_sin"].rearrange("p (m two) -> p m two", two=2)
                    turned = rot_t[:, :, :].rearrange("p t (m two) -> p (t m) two", two=2)
                    gp.tensor_tensor(rot_c[:, :, :], x, cut["rope_cos"].rearrange("p (t d) -> p t d", t=NT),
                                     ALU.mult)
                    gp.tensor_tensor(turned[:, :, 0:1], pairs[:, :, 1:2], sin[:, :, 0:1], ALU.mult)
                    gp.tensor_tensor(turned[:, :, 1:2], pairs[:, :, 0:1], sin[:, :, 1:2],
                                     ALU.mult).then_inc(rot_ready.sem, 1)
                    pool.wait_ge(rot_ready.sem, rot_ready.at(b, 1))
                    gp.tensor_tensor(q_in[i][:, :, :], rot_c[:, :, :], rot_t[:, :, :],
                                     ALU.add).then_inc(rot_ready.sem, 1)

            def step(s):
                if s.first % 2 == 1:
                    rotary(s)
                if s.has(-1):
                    inverse_root(mv1, ve1, rs1, NT, mv1_ready, ve1_ready, rs1_ready, s.batch(-1))
                causal(s, 0)
                if s.has(-1):
                    b = s.batch(-1)
                    pool.wait_ge(n1_ready.sem, n1_ready.at(b))
                    gp.tensor_tensor(n1w[:, :, :], n1[:, :, :], over_tiles("ln1_w"),
                                     ALU.mult).then_inc(n1w_ready.sem, 1)
                    pool.wait_ge(n1w_ready.sem, n1w_ready.at(b))
                    if s.began(-2):
                        for t in range(NT):
                            pool.wait_ge(acc_ready[t].sem, acc_ready[t].at(s.batch(-2)))
                    gp.tensor_tensor(x1[:, :, :], n1w[:, :, :], over_tiles("ln1_b"),
                                     ALU.add).then_inc(x1_ready.sem, 1)
                causal(s, 1)
                if s.has(-2):
                    if s.began(-3):
                        pool.wait_ge(n2_ready.sem, n2_ready.at(s.batch(-3)))
                    inverse_root(mv2, ve2, rs2, NT, mv2_ready, ve2_ready, rs2_ready, s.batch(-2), sh2)
                if s.has_pair(2):
                    if s.began(0):
                        pool.wait_ge(xh_ready.sem, xh_ready.at(s.pair(0)))
                    inverse_root(mv_p, ve_p, rs_p, 2 * NT, mvp_ready, vep_ready, rsp_ready, s.pair(2), sh_p)
                if s.has_pair(3):
                    j = s.pair(3)
                    pool.wait_ge(z_ready.sem, z_ready.at(j))
                    if s.began(1):
                        pool.wait_ge(den_ready.sem, den_ready.at(s.pair(1)))
                    gp.tensor_tensor(qzT[:, :], q_f[:, :], zT[:, :], ALU.mult).then_inc(qz_ready.sem, 1)
                causal(s, 2)
                if s.first % 2 == 0:
                    rotary(s)
                if s.has(-2):
                    b = s.batch(-2)
                    pool.wait_ge(n2_ready.sem, n2_ready.at(b))
                    gp.tensor_tensor(n2w[:, :, :], n2[:, :, :], over_tiles("ln2_w"),
                                     ALU.mult).then_inc(n2w_ready.sem, 1)
                if s.has(-2):
                    b = s.batch(-2)
                    pool.wait_ge(n2w_ready.sem, n2w_ready.at(b))
                    if s.began(-3):
                        pool.wait_ge(y_ready.sem, y_ready.at(s.batch(-3)))
                    gp.tensor_tensor(z3[:, :, :], n2w[:, :, :], xb_ln2[s.slot(-2, 2)][:, :, :],
                                     ALU.add).then_inc(z3_ready.sem, 1)
                if s.has(-1):
                    b = s.batch(-1)
                    pool.wait_ge(hit_ready.sem, hit_ready.at(b, 2))
                    if s.began(-2):
                        pool.wait_ge(gsel_ready.sem, gsel_ready.at(s.batch(-2)))
                    gp.tensor_tensor(sel[:, :, :], hit[:, 0, :, :], hit[:, 1, :, :],
                                     ALU.add).then_inc(sel_ready.sem, 1)
                    pool.wait_ge(sel_ready.sem, sel_ready.at(b))
                    pool.wait_ge(ge_ready.sem, ge_ready.at(b))
                    if s.began(-2):
                        pool.wait_ge(gate_ready.sem, gate_ready.at(s.batch(-2)))
                    gp.tensor_tensor(gsel[:, :, :], ge[:, :, :], sel[:, :, :],
                                     ALU.mult).then_inc(gsel_ready.sem, 1)
                causal(s, 3)
                if s.has(0):
                    i = s.slot(0, 2)
                    pool.wait_ge(xh_ready.sem, xh_ready.at(s.pair(0) if s.has_pair(0) else s.pair(-1)))
                    if s.began(-2):
                        pool.wait_ge(u2_ready.sem, u2_ready.at(s.batch(-2)))
                        pool.wait_ge(z3_ready.sem, z3_ready.at(s.batch(-2)))
                    x = xh[:, s.slot(0, 4), :, :]
                    gp.tensor_tensor(xb_out[i][:, :, :], x, b_out_v[:, :].unsqueeze(1).to_broadcast([P, NT, D]),
                                     ALU.add)
                    gp.tensor_tensor(xb_ln2[i][:, :, :], x, over_tiles("ln2_b"),
                                     ALU.add).then_inc(xb_ready.sem, 1)
                if s.has(-2):
                    if s.began(-3):
                        pool.wait_ge(y_ready.sem, y_ready.at(s.batch(-3)))
                    inverse_root(mv3, ve3, rs3, NT, mv3_ready, ve3_ready, rs3_ready, s.batch(-2), sh3)

            steps(pool, step)


def kernel(L0_attn_x, L0_attn_W_q, L0_attn_W_k, L0_attn_W_v, L0_attn_W_o, L0_ffn_in_proj_w, L0_ffn_in_proj_b,
           L0_ffn_out_proj_w, L0_ffn_out_proj_b, L0_ffn_gate_w, L0_ffn_gate_b, L0_ffn_expert_w,
           L0_ffn_expert_b, L0_ffn_ln1_w, L0_ffn_ln1_b, L0_ffn_ln2_w, L0_ffn_ln2_b):
    import numpy as np
    import concourse.bacc as bacc
    from concourse.bass_utils import run_bass_kernel_spmd

    f = np.float32
    arr = np.asarray
    tri = np.triu(np.ones((P, P), f))
    inv_freq = (f(1.0) / np.power(f(10000.0), np.arange(0, HD, 2, dtype=f) / f(HD))).astype(f)
    angle = np.arange(T, dtype=f)[:, None] * inv_freq[None, :]
    cos = np.repeat(np.cos(angle), 2, axis=1)
    sin = np.stack([-np.sin(angle), np.sin(angle)], axis=-1).reshape(T, HD)

    def by_tile(a):
        return np.tile(a, (1, H)).reshape(NT, P, D).transpose(1, 0, 2).reshape(P, NT * D)

    halves = np.zeros((P, 2), f)
    halves[:HID, 0] = 1
    halves[HID:, 1] = 1

    def rows(v):
        return np.broadcast_to(arr(v)[None, :], (P, arr(v).shape[0]))

    def head_last(a):
        return a.reshape((H, HD) + a.shape[1:]).swapaxes(0, 1).reshape(a.shape)

    wi, bi = arr(L0_ffn_in_proj_w), arr(L0_ffn_in_proj_b)
    wo = arr(L0_attn_W_o)
    none = np.zeros_like(wo)
    parts = {
        "ident": np.eye(P, dtype=f),
        "w_lin": np.concatenate([arr(L0_attn_W_q), arr(L0_attn_W_k), arr(L0_attn_W_v)], axis=1),
        "w_lin_out": np.block([[wo, none], [none, wo]]),
        "w_qk": np.concatenate([head_last(wi[0:D]).T, head_last(wi[D:2 * D]).T], axis=1),
        "w_v": wi[2 * D:].T,
        "w_out": arr(L0_ffn_out_proj_w).T,
        "w_gate": arr(L0_ffn_gate_w).T,
        "w_expert": arr(L0_ffn_expert_w).transpose(2, 0, 1).reshape(D, E * D),
        "b_v": rows(bi[2 * D:]),
        "b_out": rows(L0_ffn_out_proj_b),
        "b_gate": rows(L0_ffn_gate_b),
        "b_qk": np.stack([head_last(bi[0:D]), head_last(bi[D:2 * D])], axis=1),
        "ln1_w": rows(L0_ffn_ln1_w), "ln1_b": rows(L0_ffn_ln1_b),
        "ln2_w": rows(L0_ffn_ln2_w), "ln2_b": rows(L0_ffn_ln2_b),
        "rope_cos": by_tile(cos), "rope_sin": by_tile(sin),
        "causal": np.concatenate([tri, np.ones((P, P), f), tri], axis=1),
        "above": np.tile(np.triu(np.full((P, P), -1e30, f), 1), (1, G)),
        "halves": halves,
        "iota": rows(np.arange(E, dtype=f)),
    }
    packed = np.ascontiguousarray(np.concatenate([parts[n] for n in PACK], axis=1))
    arrays = {"x": np.ascontiguousarray(arr(L0_attn_x)), "params": packed,
              "expert_b": np.ascontiguousarray(arr(L0_ffn_expert_b).reshape(1, E * D))}

    nc = bacc.Bacc("TRN2", target_bir_lowering=False, num_devices=1)
    args = [nc.dram_tensor(n, a.shape, F32, kind="ExternalInput").ap() for n, a in arrays.items()]
    out = nc.dram_tensor("out", (NB, T, D), F32, kind="ExternalOutput").ap()
    build(nc, *args, out)
    result = run_bass_kernel_spmd(nc, [arrays], core_ids=[0])
    return result.results[0]["out"]
```
